# Optimizing a Trainium2 kernel written in Bass

```python
import numpy as np
import jax
import jax.numpy as jnp

def _softmax(x, axis=-1):
    return jax.nn.softmax(x, axis=axis)

def _gelu(x):
    return jax.nn.gelu(x, approximate=True)

def _silu(x):
    return jax.nn.silu(x)

def _sigmoid(x):
    return jax.nn.sigmoid(x)

def _layernorm(x, axis=-1, eps=1e-05):
    m = jnp.mean(x, axis=axis, keepdims=True)
    v = jnp.var(x, axis=axis, keepdims=True)
    return (x - m) / jnp.sqrt(v + eps)

def _scatter_add(tgt, idx, src, axis=0):
    return tgt.at[idx].add(src)

def _segment_sum(src, seg, n):
    return jax.ops.segment_sum(src, seg, n)
kernel_name = 'mk_decoder_preln_d1_seqx_r4_0ad0e3'

def setup_inputs(seed: int=0):
    np.random.seed(seed)
    _w = jnp.asarray

    def _rec_inputs():
        import jax
        import jax.numpy as jnp
        _rk = jax.random.key(seed)
        x = -0.0002928 + 1 * jax.random.normal(jax.random.fold_in(_rk, 1), (8, 512, 256), jnp.float32)
        _lenS = 512 - jax.random.randint(jax.random.fold_in(_rk, 7), (8,), 0, max(1, 512 // 4) + 1, jnp.int32)
        _lenS2 = 512 - jax.random.randint(jax.random.fold_in(_rk, 8), (8,), 0, max(1, 512 // 4) + 1, jnp.int32)
        _ctx_512P = jax.random.normal(jax.random.fold_in(_rk, 11), (8, 16, 128), jnp.float32)
        _ctx_512c = jax.random.dirichlet(jax.random.fold_in(_rk, 511), 0.3 * jnp.ones((16,), jnp.float32), (8, 512))
        _ctx_512t = jnp.einsum('bsk,bkd->bsd', _ctx_512c, _ctx_512P)
        _ctx_512t = _ctx_512t * jax.lax.rsqrt(jnp.mean(jnp.square(_ctx_512t)) + 1e-12) * 0.953939
        ctx_512 = 0.00222621 + 0.99962 * (_ctx_512t + 0.3 * jax.random.normal(jax.random.fold_in(_rk, 611), (8, 512, 128), jnp.float32))
        return (x, ctx_512)
    x, ctx_512 = _rec_inputs()

    def _L0_attn_setup():
        import jax, jax.numpy as jnp
        import numpy as np
        D_MODEL = 256
        N_HEADS = 16
        HEAD_DIM = D_MODEL // N_HEADS
        ROPE_BASE = 10000.0

        def _rope_cos_sin(seq_len, dtype):
            half = HEAD_DIM // 2
            theta = 1.0 / ROPE_BASE ** (jnp.arange(half, dtype=jnp.float32) / half)
            freqs = jnp.arange(seq_len, dtype=jnp.float32)[:, None] * theta[None, :]
            cos = jnp.repeat(jnp.cos(freqs), 2, axis=-1).astype(dtype)
            sin = jnp.repeat(jnp.sin(freqs), 2, axis=-1).astype(dtype)
            return (cos[None, None, :, :], sin[None, None, :, :])

        def _rotate_half(x):
            x_even = x[..., ::2]
            x_odd = x[..., 1::2]
            return jnp.stack((-x_odd, x_even), axis=-1).reshape(x.shape)
        key = jax.random.key(seed)
        k1, k2, k3, k4, k5 = jax.random.split(key, 5)
        bsz, seq_len = (4, 512)
        s = 1.0 / np.sqrt(D_MODEL)
        return {'x': jax.random.normal(k1, (bsz, seq_len, D_MODEL), dtype=jnp.float32), 'W_qkv': jax.random.uniform(k2, (3 * D_MODEL, D_MODEL), minval=-s, maxval=s, dtype=jnp.float32), 'b_qkv': jax.random.uniform(k3, (3 * D_MODEL,), minval=-s, maxval=s, dtype=jnp.float32), 'W_out': jax.random.uniform(k4, (D_MODEL, D_MODEL), minval=-s, maxval=s, dtype=jnp.float32), 'b_out': jax.random.uniform(k5, (D_MODEL,), minval=-s, maxval=s, dtype=jnp.float32)}
    _L0_attn_all = _L0_attn_setup()
    _L0_attn_in = {k: v for k, v in _L0_attn_all.items() if k in ('W_qkv', 'b_qkv', 'W_out', 'b_out')}
    del _L0_attn_all

    def _L0_xattn_setup():
        import jax, jax.numpy as jnp
        import numpy as np
        B, T, TC, C, CC, H = (2, 512, 128, 256, 128, 16)
        D = C // H

        def _heads(t):
            b, l, _ = t.shape
            return t.reshape(b, l, H, D).transpose(0, 2, 1, 3)
        key = jax.random.key(seed)
        ks = jax.random.split(key, 18)
        w = lambda k, i, o: jax.random.normal(k, (i, o), jnp.float32) / np.sqrt(i).astype(np.float32)
        return {'x': jax.random.normal(ks[0], (B, T, C), jnp.float32), 'cross_input': jax.random.normal(ks[1], (B, TC, CC), jnp.float32), 'Wk': w(ks[2], C, C), 'bk': jnp.zeros((C,), jnp.float32), 'Wq': w(ks[3], C, C), 'bq': jnp.zeros((C,), jnp.float32), 'Wv': w(ks[4], C, C), 'bv': jnp.zeros((C,), jnp.float32), 'Wck': w(ks[5], CC, C), 'bck': jnp.zeros((C,), jnp.float32), 'Wcq': w(ks[6], C, C), 'bcq': jnp.zeros((C,), jnp.float32), 'Wcv': w(ks[7], CC, C), 'bcv': jnp.zeros((C,), jnp.float32), 'Wp': w(ks[8], C, C), 'bp': jnp.zeros((C,), jnp.float32)}
    _L0_xattn_all = _L0_xattn_setup()
    _L0_xattn_in = {k: v for k, v in _L0_xattn_all.items() if k in ('Wk', 'bk', 'Wq', 'bq', 'Wv', 'bv', 'Wck', 'bck', 'Wcq', 'bcq', 'Wcv', 'bcv', 'Wp', 'bp')}
    del _L0_xattn_all

    def _L0_ffn_setup():
        import jax, jax.numpy as jnp
        import numpy as np
        key = jax.random.key(seed)
        k1, k2, k3, k4 = jax.random.split(key, 4)
        B, T, M = (4, 512, 256)
        E, F = (16, 1024)
        x = jax.random.normal(k1, (B, T, M), dtype=jnp.float32) * 0.02
        Wg = jax.random.normal(k2, (M, E), dtype=jnp.float32) * 0.02
        w1 = jax.random.normal(k3, (E, M, F), dtype=jnp.float32) * 0.02
        w2 = jax.random.normal(k4, (E, F, M), dtype=jnp.float32) * 0.02
        return {'x': x, 'Wg': Wg, 'w1': w1, 'w2': w2}
    _L0_ffn_all = _L0_ffn_setup()
    _L0_ffn_in = {k: v for k, v in _L0_ffn_all.items() if k in ('Wg', 'w1', 'w2')}
    del _L0_ffn_all
    return {'x': x, 'ctx_512': ctx_512, 'L0_attn_W_qkv': _L0_attn_in['W_qkv'], 'L0_attn_b_qkv': _L0_attn_in['b_qkv'], 'L0_attn_W_out': _L0_attn_in['W_out'], 'L0_attn_b_out': _L0_attn_in['b_out'], 'L0_xattn_Wk': _L0_xattn_in['Wk'], 'L0_xattn_bk': _L0_xattn_in['bk'], 'L0_xattn_Wq': _L0_xattn_in['Wq'], 'L0_xattn_bq': _L0_xattn_in['bq'], 'L0_xattn_Wv': _L0_xattn_in['Wv'], 'L0_xattn_bv': _L0_xattn_in['bv'], 'L0_xattn_Wck': _L0_xattn_in['Wck'], 'L0_xattn_bck': _L0_xattn_in['bck'], 'L0_xattn_Wcq': _L0_xattn_in['Wcq'], 'L0_xattn_bcq': _L0_xattn_in['bcq'], 'L0_xattn_Wcv': _L0_xattn_in['Wcv'], 'L0_xattn_bcv': _L0_xattn_in['bcv'], 'L0_xattn_Wp': _L0_xattn_in['Wp'], 'L0_xattn_bp': _L0_xattn_in['bp'], 'L0_ffn_Wg': _L0_ffn_in['Wg'], 'L0_ffn_w1': _L0_ffn_in['w1'], 'L0_ffn_w2': _L0_ffn_in['w2']}

def reference(x, ctx_512, L0_attn_W_qkv, L0_attn_b_qkv, L0_attn_W_out, L0_attn_b_out, L0_xattn_Wk, L0_xattn_bk, L0_xattn_Wq, L0_xattn_bq, L0_xattn_Wv, L0_xattn_bv, L0_xattn_Wck, L0_xattn_bck, L0_xattn_Wcq, L0_xattn_bcq, L0_xattn_Wcv, L0_xattn_bcv, L0_xattn_Wp, L0_xattn_bp, L0_ffn_Wg, L0_ffn_w1, L0_ffn_w2):
    import jax
    import jax.numpy as jnp

    def _L0_attn_ref(x, W_qkv, b_qkv, W_out, b_out):
        import jax, jax.numpy as jnp
        import numpy as np
        D_MODEL = 256
        N_HEADS = 16
        HEAD_DIM = D_MODEL // N_HEADS
        ROPE_BASE = 10000.0

        def _rope_cos_sin(seq_len, dtype):
            half = HEAD_DIM // 2
            theta = 1.0 / ROPE_BASE ** (jnp.arange(half, dtype=jnp.float32) / half)
            freqs = jnp.arange(seq_len, dtype=jnp.float32)[:, None] * theta[None, :]
            cos = jnp.repeat(jnp.cos(freqs), 2, axis=-1).astype(dtype)
            sin = jnp.repeat(jnp.sin(freqs), 2, axis=-1).astype(dtype)
            return (cos[None, None, :, :], sin[None, None, :, :])

        def _rotate_half(x):
            x_even = x[..., ::2]
            x_odd = x[..., 1::2]
            return jnp.stack((-x_odd, x_even), axis=-1).reshape(x.shape)
        bsz, seq_len, _ = x.shape
        qkv = x @ W_qkv.T + b_qkv
        qkv = qkv.reshape(bsz, seq_len, 3, N_HEADS, HEAD_DIM)
        q = jnp.transpose(qkv[:, :, 0], (0, 2, 1, 3))
        k = jnp.transpose(qkv[:, :, 1], (0, 2, 1, 3))
        v = jnp.transpose(qkv[:, :, 2], (0, 2, 1, 3))
        cos, sin = _rope_cos_sin(seq_len, x.dtype)
        q = q * cos + _rotate_half(q) * sin
        k = k * cos + _rotate_half(k) * sin
        attn = jnp.einsum('bhqd,bhkd->bhqk', q, k) / jnp.sqrt(jnp.asarray(HEAD_DIM, x.dtype))
        attn = jax.nn.softmax(attn, axis=-1)
        out = jnp.einsum('bhqk,bhkd->bhqd', attn, v)
        out = jnp.transpose(out, (0, 2, 1, 3)).reshape(bsz, seq_len, D_MODEL)
        return out @ W_out.T + b_out

    def _L0_xattn_ref(x, cross_input, Wk, bk, Wq, bq, Wv, bv, Wck, bck, Wcq, bcq, Wcv, bcv, Wp, bp):
        import jax, jax.numpy as jnp
        import numpy as np
        B, T, TC, C, CC, H = (2, 512, 128, 256, 128, 16)
        D = C // H

        def _heads(t):
            b, l, _ = t.shape
            return t.reshape(b, l, H, D).transpose(0, 2, 1, 3)
        scale = np.float32(1.0 / np.sqrt(D))
        q = _heads(x @ Wq + bq)
        k = _heads(x @ Wk + bk)
        v = _heads(x @ Wv + bv)
        att = jnp.einsum('bhqd,bhkd->bhqk', q, k) * scale
        causal = jnp.tril(jnp.ones((T, T), bool))
        att = jnp.where(causal[None, None], att, -jnp.inf)
        y = jnp.einsum('bhqk,bhkd->bhqd', jax.nn.softmax(att, axis=-1), v)
        qc = _heads(x @ Wcq + bcq)
        kc = _heads(cross_input @ Wck + bck)
        vc = _heads(cross_input @ Wcv + bcv)
        attc = jnp.einsum('bhqd,bhkd->bhqk', qc, kc) * scale
        y = y + jnp.einsum('bhqk,bhkd->bhqd', jax.nn.softmax(attc, axis=-1), vc)
        y = y.transpose(0, 2, 1, 3).reshape(x.shape[0], T, C)
        return y @ Wp + bp

    def _L0_ffn_ref(x, Wg, w1, w2):
        import jax, jax.numpy as jnp
        import numpy as np
        d = x.shape[-1]
        xr = x.reshape(-1, d)
        S = xr.shape[0]
        E = Wg.shape[1]
        C = (S + E - 1) // E
        gate = jax.nn.softmax(xr @ Wg, axis=-1)
        idx = jnp.argmax(gate, axis=1)
        gates_s = jnp.take_along_axis(gate, idx[:, None], axis=1)[:, 0]
        onehot = jax.nn.one_hot(idx, E, dtype=jnp.int32)
        loc = jnp.sum((jnp.cumsum(onehot, axis=0) - 1) * onehot, axis=1)
        valid = loc < C
        loc_pad = jnp.minimum(loc, C)
        dispatched = jnp.zeros((E, C + 1, d), dtype=x.dtype).at[idx, loc_pad].set(xr)
        dispatched = dispatched[:, :C]
        h = jax.nn.relu(jnp.einsum('ecm,emf->ecf', dispatched, w1))
        expert_out = jnp.einsum('ecf,efm->ecm', h, w2)
        gathered = expert_out[idx, jnp.minimum(loc, C - 1)]
        combined = gathered * (gates_s * valid.astype(x.dtype))[:, None]
        return combined.reshape(x.shape)
    x = x + _L0_attn_ref(_layernorm(x, axis=-1), L0_attn_W_qkv, L0_attn_b_qkv, L0_attn_W_out, L0_attn_b_out)
    x = x + _L0_xattn_ref(_layernorm(x, axis=-1), ctx_512, L0_xattn_Wk, L0_xattn_bk, L0_xattn_Wq, L0_xattn_bq, L0_xattn_Wv, L0_xattn_bv, L0_xattn_Wck, L0_xattn_bck, L0_xattn_Wcq, L0_xattn_bcq, L0_xattn_Wcv, L0_xattn_bcv, L0_xattn_Wp, L0_xattn_bp)
    x = x + _L0_ffn_ref(_layernorm(x, axis=-1), L0_ffn_Wg, L0_ffn_w1, L0_ffn_w2)
    return x

_drawn_inputs = setup_inputs


def setup_inputs(seed=0):
    import zlib

    import numpy as np

    out = dict(_drawn_inputs(seed))
    spreads = {'L0_xattn_bk': (0.0, 0.8),
     'L0_xattn_bq': (0.0, 0.62),
     'L0_xattn_bv': (0.0, 0.1),
     'L0_xattn_bck': (0.0, 0.8),
     'L0_xattn_bcq': (0.0, 0.405),
     'L0_xattn_bcv': (0.0, 0.1),
     'L0_xattn_bp': (0.0, 0.1)}
    factors = {'L0_ffn_Wg': 5.061, 'L0_ffn_w1': 5.865, 'L0_ffn_w2': 4.868}
    for name, (base, spread) in spreads.items():
        noise = np.random.default_rng([zlib.crc32(name.encode()), seed]).standard_normal(out[name].shape)
        drawn = base * np.exp(spread * noise) if base else spread * noise
        out[name] = jnp.asarray(drawn.astype(out[name].dtype))
    for name, factor in factors.items():
        out[name] = (out[name] * factor).astype(out[name].dtype)
    return out
```

```python
from contextlib import ExitStack

import numpy as np

import concourse.bass as bass
from concourse import mybir

F32 = mybir.dt.float32
F16 = mybir.dt.float16
BF16 = mybir.dt.bfloat16
U32 = mybir.dt.uint32
ALU = mybir.AluOpType
ACT = mybir.ActivationFunctionType
AX_X = mybir.AxisListType.X

P = 128
NB, T, D, DC = 8, 512, 256, 128
H, HD = 16, 16
TT = T // P
FT = D // P
GH = 4
NG = H // GH
SLOTS = NG * TT * 2
S_UNITS = H * TT
LEAD = 12
E, CAP, F = 16, NB * T // 16, 1024
FF = F // P
STACK = 96
MROWS = STACK + 2
MSCALE = 1024.0
SM_SCALE = HD ** -0.5
P_RING = 4
NEG = -1e30
LN_EPS = 1e-5


class Body:

    def __init__(self, kind, prev, nxt, parity, n, dn=0, route=False):
        self.kind, self.prev, self.nxt, self.parity, self.route = kind, prev, nxt, parity, route
        self.fin = prev if prev in ("A", "C") else None
        self.n, self.dn = n, dn
        self.base, self.stride, self.i = {}, {}, 0

    def at(self, sem, k=0):
        return self.base[sem] + self.i * self.stride.get(sem, 0) + k if self.stride.get(sem, 0) \
            else self.base[sem] + k

    def batch(self, ahead=0):
        n = self.n + ahead
        if n < NB:
            return n + self.dn * self.i if self.dn else n
        b = (n - NB) // 2
        return b + (self.dn // 2) * self.i if self.dn else b

    def counts(self):
        c, run, prep, had = {}, self.kind is not None, self.nxt, self.prev is not None
        c["scores_q"] = c["max_done"] = (2 * (SLOTS - LEAD) if run else 0) + (2 * LEAD if prep else 0)
        groups = (3 if run else 0) + (1 if prep else 0)
        c["negmax_hi"] = c["negmax_split"] = c["negmax_rows"] = groups
        c["negmax_in_0"] = 32 * ((1 if run else 0) + (1 if prep else 0))
        c["negmax_in_1"] = 64 if run else 0
        c["scores_k"] = c["exp_done"] = SLOTS if run else 0
        c["av_done"] = (15 if run else 0) + (1 if had else 0)
        c["av_out"] = (3 if run else 0) + (1 if had else 0)
        c["packed_0"] = 128 * 2 if run else 0
        c["packed_1"] = (128 if run else 0) + (128 if had else 0)
        for s in ("recip_done", "attn_out"):
            c[s] = int(had)
        c["recip_stored"] = 16 * int(had)
        c["recip_in"] = 16 * FT * int(had)
        c["attn_mul"] = int(self.prev == "C")
        c["jobs_done"] = len(self.jobs())
        ln = int(prep in ("A", "B"))
        rt = int(self.route)
        c["bn_done"] = c["ln_var"] = c["ln_rstd"] = c["ln_out"] = ln + rt
        c["ln_step"] = 3 * (ln + rt)
        c["x_bias"] = ln
        c["xT_out"] = 2 * ln
        c["ctx_in"] = 16 * int(prep == "C")
        c["ctxT_out"] = int(prep == "C")
        rope = 4 * int(prep == "A")
        for s in ("rope_in", "rope_cos", "rope_sin", "rope_out"):
            c[s] = rope
        c["hi_out"] = c["lo_out"] = 4 if prep else 0
        c["parts_stored"] = 64 if prep else 0
        c["stack_in"] = 128 if prep else 0
        c["v_out"] = 4 if prep else 0
        c["x_out"] = 2 if self.fin else 0
        c["zT_out"] = 2 * rt
        c["route_dve"] = ROUTE_STEPS * rt
        c["route_exp"] = c["onehot_out"] = c["index_out"] = rt
        c["scattered"] = 16 * TT * rt
        return c

    def jobs(self):
        out = []
        if self.nxt == "A":
            out += [(2, "xT", 0), (3, "xT", 1), (4, "proj", 0), (5, "proj", 1), (6, "rope", 0), (7, "rope", 1),
                    (8, "proj", 2), (9, "proj", 3), (10, "rope", 2), (11, "rope", 3), (14, "v", 0), (15, "v", 1)]
        if self.nxt == "B":
            out += [(2, "xT", 0), (3, "xT", 1)]
        if self.nxt == "C":
            out += [(2, "ctxT", 0)]
        if self.nxt in ("B", "C"):
            out += [(4, "proj", 0), (5, "proj", 1), (6, "proj", 2), (7, "proj", 3), (9, "v", 0), (10, "v", 1)]
        if self.kind:
            out += [(5, "negmax", 1), (13, "negmax", 2), (21, "negmax", 3)]
        if self.nxt:
            out += [(29, "negmax", 0)]
        if self.fin:
            out += [(16, "out", 0), (17, "out", 1)]
        if self.route:
            out += [(22, "zT", 0), (23, "zT", 1), (24, "logits", 0), (27, "count", 0)]
        return sorted(out, key=lambda j: j[0])

    def freed(self, idx):
        if idx < 0:
            return ("negmax_rows" if self.nxt or self.kind else "route_dve"), 0
        _, name, j = self.jobs()[idx]
        if name == "proj":
            return ("rope_in" if self.nxt == "A" else "lo_out"), j + 1
        if name == "negmax":
            return "negmax_rows", (j if j else 4) if self.kind else 1
        return {"xT": ("xT_out", j + 1), "ctxT": ("ctxT_out", 1), "zT": ("zT_out", j + 1), "v": ("v_out", 2 * j + 2),
                "rope": ("rope_sin", j + 1), "out": ("x_out", j + 1), "logits": ("route_dve", 2),
                "count": ("route_dve", 12)}[name]


ROUTE_STEPS = 20


def plan():
    blocks = [
        (1, [Body(None, None, "A", 1, -1)]),
        (1, [Body("A", None, "A", 0, 0)]),
        (3, [Body("A", "A", "A", 1, 1, 2), Body("A", "A", "A", 0, 2, 2)]),
        (1, [Body("A", "A", "B", 1, 7)]),
        (1, [Body("B", "A", "C", 0, 8)]),
        (1, [Body("C", "B", "B", 1, 9)]),
        (6, [Body("B", "C", "C", 0, 10, 2), Body("C", "B", "B", 1, 11, 2, route=True)]),
        (1, [Body("B", "C", "C", 0, 22)]),
        (1, [Body("C", "B", None, 1, 23, route=True)]),
        (1, [Body(None, "C", None, 0, 24, route=True)]),
    ]
    total = {}
    for times, bodies in blocks:
        cycle = {}
        for b in bodies:
            for s, k in b.counts().items():
                b.base[s] = total.get(s, 0) + cycle.get(s, 0)
                cycle[s] = cycle.get(s, 0) + k
        for b in bodies:
            b.stride = dict(cycle) if times > 1 else {}
        for s, k in cycle.items():
            total[s] = total.get(s, 0) + k * times
    return blocks, total


def stretches(eng, blocks):
    for times, bodies in blocks:
        if times == 1:
            for b in bodies:
                yield b
        else:
            with eng.Fori(0, times) as i:
                for b in bodies:
                    b.i = i
                    yield b
                    b.i = 0


def need(eng, sem, value):
    if not isinstance(value, int) or value > 0:
        eng.wait_ge(sem, value)


def build(nc, a):
    blocks, total = plan()
    ctx = ExitStack()
    with ctx:
        def sb(name, shape, dt):
            return ctx.enter_context(nc.sbuf_tensor(name, shape, dt))

        def sem(name):
            return ctx.enter_context(nc.semaphore(name))

        parts_dram = nc.dram_tensor("parts_scratch", [2, 2, 2, D, T], F16).ap()
        recip_dram = nc.dram_tensor("recip_scratch", [H, T], F32).ap()
        rows_dram = nc.dram_tensor("rows_scratch", [E * CAP, D], F32).ap()
        expert_dram = nc.dram_tensor("expert_scratch", [E * CAP, D], F32).ap()

        psS = ctx.enter_context(nc.psum_tensor("psS", [P, 2, T], F32))
        psK = ctx.enter_context(nc.psum_tensor("psK", [P, 2, 2, T], F32))
        psO = ctx.enter_context(nc.psum_tensor("psO", [P, T], F32))
        psM = ctx.enter_context(nc.psum_tensor("psM", [P, T], F32))

        X = sb("X", [P, NB, TT * D], F32)
        stack = sb("stack", [P, 2, 2, H * T], F16)
        probs = sb("probs", [P, P_RING, 2, T], F32)
        V = sb("V", [P, 2, TT, H * 2 * HD], F32)
        parts = sb("parts", [P, 2, FT, 2, T], F16)
        xn = sb("xn", [P, TT, D], F32)
        xT = sb("xT", [P, FT, T], F32)
        U = sb("U", [P, 2, T], F32)
        packed = sb("packed", [P, FT, T], F32)
        sums = sb("sums", [P, 64], F32)
        recip = sb("recip", [P, 64], F32)
        recipB = sb("recipB", [P, FT, T], F32)
        attn = sb("attn", [P, FT, T], F32)
        wo1 = sb("wo1", [P, FT, D], F32)
        wx = sb("wx", [P, 4, FT, D], F32)
        wc = sb("wc", [P, 2, D], F32)
        wp = sb("wp", [P, FT, D], F32)
        wg = sb("wg", [P, FT, E], F32)
        shared = sb("shared", [P, 3072 + 1536], F32)
        rope_cs = shared[:, 0:1024].rearrange("p (s t) -> p s t", s=2)
        rope_x = shared[:, 1024:2048].rearrange("p (s t) -> p s t", s=2)
        rope_c = shared[:, 2048:2560]
        rope_s = shared[:, 2560:3072]
        wqkv = shared[:, 3072:4608].rearrange("p (k n) -> p k n", k=FT)
        attn_b = shared[:, 0:1024].rearrange("p (f t) -> p f t", f=FT)
        ctx_sb = shared[:, 1024:1536].rearrange("p (t c) -> p t c", t=TT)
        ctxT = shared[:, 1536:2048]
        zT = shared[:, 2048:3072].rearrange("p (f t) -> p f t", f=FT)
        bias_v = sb("bias_v", [P, 3, D], F32)
        bias_o = sb("bias_o", [P, 2, D], F32)
        bias_qk = sb("bias_qk", [P, 6, FT], F32)
        consts = sb("consts", [P, 5 * P + TT * E], F32)
        ident = consts[:, 0:P]
        rot = consts[:, P:2 * P]
        expert_no = consts[:, 5 * P:5 * P + TT * E]
        halves = sb("halves", [P, 4, P], BF16)
        ident_bf, mask_q, mask_k, tri = (halves[:, j, :] for j in range(4))
        ones_bf = sb("ones_bf", [P, P], BF16)
        ident_h = sb("ident_h", [P, P], F16)
        negmax = sb("negmax", [P, 2, S_UNITS // NG], F32)
        mparts = sb("mparts", [P, TT, 2, GH], F16)
        mrows = sb("mrows", [2 * GH, T], F16)
        stats = sb("stats", [P, TT, 6], F32)
        lnt = sb("lnt", [P, 7, TT], F32)
        rstd = sb("rstd", [P, TT], F32)
        minus_half = sb("minus_half", [P, TT], F32)
        rt = sb("rt", [P, 6, TT * E], F32)
        rs = sb("rs", [P, 10, TT], F32)
        onehot = sb("onehot", [P, TT * E], BF16)
        filled = sb("filled", [P, E], F32)
        scatter_to = sb("scatter_to", [P, TT], U32)
        gather_from = sb("gather_from", [P, NB, TT], U32)
        gates = sb("gates", [P, NB, TT], F32)

        free0, free1 = (stack[:, q, :, :].rearrange("p a n -> p (a n)").bitcast(F32) for q in range(2))
        w1_sb = [free0[:, 2048 * c:2048 * (c + 1)].rearrange("p (k f) -> p k f", k=FT) for c in range(2)]
        w2_sb = [free0[:, 4096 + 2048 * c:4096 + 2048 * (c + 1)].rearrange("p (k m) -> p k m", k=FF) for c in range(2)]
        hT = [free1[:, 2048 * c:2048 * (c + 1)].rearrange("p (f s) -> p f s", f=FF) for c in range(2)]
        rows_sb = [free1[:, 4096 + 512 * c:4096 + 512 * (c + 1)].rearrange("p (s m) -> p s m", s=2) for c in range(2)]
        rowsT = [free1[:, 5120 + 512 * c:5120 + 512 * (c + 1)].rearrange("p (m s) -> p m s", m=FT) for c in range(2)]
        eo_sb = [free1[:, 6144 + 512 * c:6144 + 512 * (c + 1)].rearrange("p (s m) -> p s m", s=2) for c in range(2)]
        psH = [psS[:, 0, :], psS[:, 1, :], psK[:, 0, 0, :], psK[:, 0, 1, :]]
        psY = [psK[:, 1, 0, :], psK[:, 1, 1, :]]
        psR = [psO[:, :], psM[:, :]]
        got = probs[:, :, :, :].rearrange("p r h t -> p r (h t)")

        s = {name: sem(name) for name in total}
        x0_in, x_in, w_in, w1_in0, cst_in = (sem(n) for n in ("x0_in", "x_in", "w_in", "w1_in0", "cst_in"))
        zeroed, rows_zero, stack_set0, stack_set1, cst_set, v_ones, misc_set = (
            sem(n) for n in ("zeroed", "rows_zero", "stack_set0", "stack_set1", "cst_set", "v_ones", "misc_set"))
        w1_in, w2_in, rows_in, eo_stored = ([sem(f"{n}_{c}") for c in range(2)]
                                            for n in ("w1_in", "w2_in", "rows_in", "eo_stored"))
        rowsT_done, rowsT_out, hid_done, hid_out, y_done, y_out = (
            sem(n) for n in ("rowsT_done", "rowsT_out", "hid_done", "hid_out", "y_done", "y_out"))
        got_in = [sem(f"got_in_{c}") for c in range(P_RING)]
        got_used, out_stored = sem("got_used"), sem("out_stored")

        def s_unit(b, t, j):
            u = 2 * (t + LEAD) + j
            later = u >= S_UNITS
            return later, u % S_UNITS, 2 * t + j if b.kind else 2 * t + j - 2 * (SLOTS - LEAD)

        def has_s(b, later):
            return b.nxt if later else b.kind

        def stack_of(parity, q_or_k):
            return stack[:, parity, q_or_k, :].rearrange("p (h t) -> p h t", h=H)

        def v_of(parity):
            return V[:, parity, :, :].rearrange("p k (h c) -> p k h c", h=H)

        def q_from(kind, kt):
            return kt * P if kind == "B" else 0

        block = ctx.enter_context(nc.Block())

        @block.sync
        def _(sp):
            sp.dma_start(X[:, 0, :].rearrange("p (t d) -> p t d", t=TT),
                         a["x"][0].rearrange("(t p) d -> p t d", p=P)).then_inc(x0_in, 16)
            sp.dma_start(consts[:, :], a["consts"]).then_inc(cst_in, 16)
            sp.dma_start(wqkv, a["W_qkv_T"].rearrange("(k p) n -> p k n", p=P)).then_inc(w1_in0, 16)
            sp.dma_start(rope_cs, a["rope"].rearrange("s p t -> p s t")).then_inc(w1_in0, 16)
            for j, name in enumerate(("A_bq", "A_bk", "L0_xattn_bq", "L0_xattn_bk", "L0_xattn_bcq", "L0_xattn_bck")):
                src = a["L0_attn_b_qkv"][D * j:D * (j + 1)] if j < 2 else a[name]
                with nc.allow_non_contiguous_dma("a bias per feature, once"):
                    sp.dma_start(bias_qk[:, j, :], src.rearrange("(f p) -> p f", p=P)).then_inc(w1_in0, 16)
            for j, src in enumerate((a["L0_attn_b_qkv"][2 * D:3 * D], a["L0_xattn_bv"], a["L0_xattn_bcv"])):
                sp.dma_start(bias_v[:, j, :], src.rearrange("(o n) -> o n", o=1).to_broadcast([P, D])).then_inc(w1_in0, 16)
            for j, src in enumerate((a["L0_attn_b_out"], a["L0_xattn_bp"])):
                sp.dma_start(bias_o[:, j, :], src.rearrange("(o n) -> o n", o=1).to_broadcast([P, D])).then_inc(w1_in0, 16)
            for n in range(1, NB):
                sp.dma_start(X[:, n, :].rearrange("p (t d) -> p t d", t=TT),
                             a["x"][n].rearrange("(t p) d -> p t d", p=P)).then_inc(x_in, 16)
            sp.dma_start(wo1[:, :, :], a["W_out_T"].rearrange("(k p) n -> p k n", p=P)).then_inc(w_in, 16)
            for j, name in enumerate(("L0_xattn_Wq", "L0_xattn_Wk", "L0_xattn_Wv", "L0_xattn_Wcq")):
                sp.dma_start(wx[:, j, :, :], a[name].rearrange("(k p) n -> p k n", p=P)).then_inc(w_in, 16)
            sp.dma_start(wc[:, 0, :], a["L0_xattn_Wck"]).then_inc(w_in, 16)
            sp.dma_start(wc[:, 1, :], a["L0_xattn_Wcv"]).then_inc(w_in, 16)
            sp.dma_start(wp[:, :, :], a["L0_xattn_Wp"].rearrange("(k p) n -> p k n", p=P)).then_inc(w_in, 16)
            sp.dma_start(wg[:, :, :], a["L0_ffn_Wg"].rearrange("(k p) n -> p k n", p=P)).then_inc(w_in, 16)
            sp.wait_ge(zeroed, 1)
            for j in range(2):
                sp.dma_start(rows_dram.rearrange("(j p r) d -> j p (r d)", j=2, p=P)[j],
                             probs[:, :, :, :].rearrange("p r h t -> p (r h t)")).then_inc(rows_zero, 16)
            for b in stretches(sp, blocks):
                np_ = 1 - b.parity
                last = {}
                for t in range(SLOTS):
                    if t == 0 and b.nxt == "C":
                        need(sp, s["ctxT_out"], b.at("ctxT_out"))
                        if b.n == 8:
                            sp.wait_ge(s["lo_out"], b.at("lo_out"))
                        sp.dma_start(ctx_sb, a["ctx"][bass.ds(b.batch(1), 1)].rearrange("o (t p) c -> p (o t) c", p=P)
                                     ).then_inc(s["ctx_in"], 16)
                    for g in range(NG):
                        mine = g < NG - 1 and b.kind and t == 8 * g + 9
                        prev = g == NG - 1 and b.prev and t == 1
                        if not (mine or prev):
                            continue
                        k = (1 if b.prev else 0) + g + 1 if mine else 1
                        sp.wait_ge(s["av_out"], b.at("av_out", k))
                        if mine and g == 0:
                            need(sp, s["attn_out"], b.at("attn_out", int(b.prev is not None)))
                        for i in range(GH):
                            h = GH * g + i
                            sp.dma_start(packed[HD * (h % 8):HD * (h % 8 + 1), h // 8, :],
                                         U[32 * i:32 * i + HD, g % 2, :]).then_inc(s[f"packed_{g % 2}"], 16)
                            sp.dma_start(sums[8 * h:8 * h + 8, :],
                                         U[32 * i + HD:32 * i + HD + 1, g % 2, :]).then_inc(s[f"packed_{g % 2}"], 16)
                    if t == 3 and b.prev:
                        sp.wait_ge(s["recip_done"], b.at("recip_done", 1))
                        sp.dma_start(recip_dram.rearrange("h (c t) -> (h c) t", c=8), recip[:, :]).then_inc(s["recip_stored"], 16)
                        sp.wait_ge(s["recip_stored"], b.at("recip_stored", 16))
                        for ft in range(FT):
                            sp.dma_start(recipB[:, ft, :],
                                         recip_dram.rearrange("(f h o) t -> f h o t", f=FT, o=1)[ft].to_broadcast([8, HD, T])
                                         ).then_inc(s["recip_in"], 16)
                    if b.nxt:
                        for j, at in enumerate((9, 10, 13, 14) if b.nxt == "A" else (4, 5, 6, 7)):
                            if t == at:
                                ft, qk = j // 2, j % 2
                                sp.wait_ge(s["lo_out"], b.at("lo_out", j + 1))
                                sp.dma_start(parts_dram[np_, qk, :, ft * P:(ft + 1) * P, :].rearrange("s p t -> p s t"),
                                             parts[:, qk, ft, :, :]).then_inc(s["parts_stored"], 16)
                        if t == (14 if b.nxt == "A" else 8):
                            sp.wait_ge((stack_set0, stack_set1)[np_], 2)
                            need(sp, s["parts_stored"], b.at("parts_stored", 64))
                            for qk, slots in ((0, (0, 0, 1, 1)), (1, (0, 1, 0, 1))):
                                for j, part in enumerate(slots):
                                    sp.dma_start(stack_of(np_, qk)[HD * j:HD * (j + 1), :, :],
                                                 parts_dram[np_, qk, part].rearrange("(h d) t -> d h t", d=HD)
                                                 ).then_inc(s["stack_in"], 16)
                    if b.n == 23 and t == 16:
                        for c in range(2):
                            sp.dma_start(w1_sb[c], a["L0_ffn_w1"][c].rearrange("(k p) f -> p k f", p=P)).then_inc(w1_in[c], 16)
                            sp.dma_start(w2_sb[c], a["L0_ffn_w2"][c].rearrange("(k p) m -> p k m", p=P)).then_inc(w2_in[c], 16)
            sp.wait_ge(s["scattered"], total["scattered"])

            def load_rows(e, c):
                sp.dma_start(rows_sb[c], rows_dram[bass.ds(e * CAP, CAP), :].rearrange("(s p) m -> p s m", p=P)
                             ).then_inc(rows_in[c], 16)

            def store_out(e, c):
                need(sp, y_out, e + 1)
                sp.dma_start(expert_dram[bass.ds(e * CAP, CAP), :].rearrange("(s p) m -> p s m", p=P), eo_sb[c]
                             ).then_inc(eo_stored[c], 16)

            for c in range(2):
                load_rows(c, c)
            with sp.Fori(0, E // 2 - 1) as i:
                for c in range(2):
                    need(sp, hid_done, (i * 2 + c + 1) * 4)
                    sp.dma_start(w1_sb[c], a["L0_ffn_w1"][bass.ds(i * 2 + 2 + c, 1)].rearrange("o (k p) f -> p (o k) f", p=P)
                                 ).then_inc(w1_in[c], 16)
                    need(sp, rowsT_done, i * 2 + c + 1)
                    load_rows(i * 2 + 2 + c, c)
                    need(sp, y_done, i * 2 + c + 1)
                    sp.dma_start(w2_sb[c], a["L0_ffn_w2"][bass.ds(i * 2 + 2 + c, 1)].rearrange("o (k p) m -> p (o k) m", p=P)
                                 ).then_inc(w2_in[c], 16)
                    store_out(i * 2 + c, c)
            for c in range(2):
                store_out(E - 2 + c, c)
            for n in range(NB):
                sp.wait_ge(got_used, n * TT + TT)
                sp.dma_start(a["out"][n].rearrange("(t p) d -> p t d", p=P),
                             X[:, n, :].rearrange("p (t d) -> p t d", t=TT)).then_inc(out_stored, 16)
            sp.wait_ge(out_stored, 16 * NB)

        @block.tensor
        def _(pe):
            pe.wait_ge(cst_set, 7)
            pe.wait_ge(w1_in0, 16 * 13)
            for b in stretches(pe, blocks):
                np_ = 1 - b.parity
                jobs = b.jobs()
                for t in range(SLOTS):
                    for j in range(2):
                        later, u, k = s_unit(b, t, j)
                        kind = has_s(b, later)
                        if not kind:
                            continue
                        par = np_ if later else b.parity
                        h, qt = u // TT, u % TT
                        if later and u == 0:
                            pe.wait_ge(s["stack_in"], b.at("stack_in", 128))
                        need(pe, s["max_done"], b.at("max_done", k - 1))
                        n = (qt + 1) * P if kind == "B" else T
                        out = psS[:, u % 2, 0:n]
                        mm = nc.tensor.matmul(out, stack_of(par, 0)[0:STACK, h, qt * P:(qt + 1) * P],
                                              stack_of(par, 1)[0:STACK, h, 0:n], start=True, stop=kind != "B",
                                              skip_group_check=kind == "B")
                        if kind == "B":
                            mm = nc.tensor.matmul(psS[:, u % 2, n - P:n], ident_bf, mask_q, start=False, stop=True,
                                                  skip_group_check=True)
                        mm.then_inc(s["scores_q"], 1)
                    if b.kind:
                        g, kt, hp = t // 8, t % 8 // 2, t % 2
                        if t % 8 == 0:
                            pe.wait_ge(s[f"negmax_in_{g % 2}"], b.at(f"negmax_in_{g % 2}", (0, 32, 32, 64)[g]))
                        need(pe, s["exp_done"], b.at("exp_done", t - 1))
                        q0 = q_from(b.kind, kt)
                        for i in range(2):
                            h = GH * g + 2 * hp + i
                            mm = nc.tensor.matmul(psK[:, t % 2, i, q0:T],
                                                  stack_of(b.parity, 1)[0:MROWS, h, kt * P:(kt + 1) * P],
                                                  stack_of(b.parity, 0)[0:MROWS, h, q0:T],
                                                  start=True, stop=b.kind != "B", skip_group_check=b.kind == "B")
                            if b.kind == "B":
                                mm = nc.tensor.matmul(psK[:, t % 2, i, q0:q0 + P], ident_bf, mask_k, start=False,
                                                      stop=True, skip_group_check=True)
                        mm.then_inc(s["scores_k"], 1)
                    if t % 2 and (b.kind if t > 1 else b.prev):
                        mine = t > 1
                        unit = t - 3 if mine else SLOTS - 2
                        kind, par = (b.kind, b.parity) if mine else (b.prev, np_)
                        g, kt = unit // 8, unit % 8 // 2
                        need(pe, s["exp_done"], b.at("exp_done", t - 1 if mine else 0))
                        if mine and unit == 0:
                            pe.wait_ge(s["v_out"], b.at("v_out"))
                        if kt == 0:
                            need(pe, s["av_out"], b.at("av_out", int(b.prev is not None) + g))
                        q0 = q_from(kind, kt)
                        for i in range(GH):
                            mm = nc.tensor.matmul(psO[32 * i:32 * i + 32, q0:T], v_of(par)[:, kt, GH * g + i, :],
                                                  probs[:, (unit + i // 2) % P_RING, i % 2, q0:T],
                                                  start=kt == 0, stop=kt == TT - 1, skip_group_check=True)
                        mm.then_inc(s["av_done"], 1)
                    for idx, (slot, name, j) in enumerate(jobs):
                        if slot != t:
                            continue
                        freed = b.freed(idx - 1)
                        need(pe, s[freed[0]], b.at(*freed))
                        if name == "xT" or name == "zT":
                            route = name == "zT"
                            ln_no = int(b.nxt in ("A", "B")) + 1 if route else 1
                            pe.wait_ge(s["ln_out"], b.at("ln_out", ln_no))
                            for tt in range(TT):
                                mm = nc.tensor.transpose(psM[:, tt * P:(tt + 1) * P], xn[:, tt, j * P:(j + 1) * P], ident)
                        elif name == "ctxT":
                            pe.wait_ge(s["ctx_in"], b.at("ctx_in", 16))
                            for tt in range(TT):
                                mm = nc.tensor.transpose(psM[:, tt * P:(tt + 1) * P], ctx_sb[:, tt, :], ident)
                        elif name == "proj":
                            ft, qk = j // 2, j % 2
                            if j == 0:
                                pe.wait_ge(w_in, 16 * 9) if b.nxt != "A" else None
                                if b.nxt != "C":
                                    pe.wait_ge(s["xT_out"], b.at("xT_out", 2))
                            if b.nxt == "C" and qk == 1:
                                pe.wait_ge(s["ctxT_out"], b.at("ctxT_out", 1))
                                mm = nc.tensor.matmul(psM[:, :], wc[:, 0, ft * P:(ft + 1) * P], ctxT, start=True, stop=True)
                            else:
                                for k in range(FT):
                                    if b.nxt == "A":
                                        w = wqkv[:, k, qk * D + ft * P:qk * D + (ft + 1) * P]
                                    else:
                                        w = wx[:, 3 if b.nxt == "C" else qk, k, ft * P:(ft + 1) * P]
                                    mm = nc.tensor.matmul(psM[:, :], w, xT[:, k, :], start=k == 0, stop=k == FT - 1)
                        elif name == "rope":
                            pe.wait_ge(s["rope_in"], b.at("rope_in", j + 1))
                            mm = nc.tensor.matmul(psM[:, :], rot, rope_x[:, j % 2, :], start=True, stop=True)
                        elif name == "v":
                            for i in range(2):
                                tt = 2 * j + i
                                out = psM[:, i * D:(i + 1) * D]
                                if b.nxt == "C":
                                    mm = nc.tensor.matmul(out, ctxT[:, tt * P:(tt + 1) * P], wc[:, 1, :], start=True, stop=True)
                                    continue
                                for k in range(FT):
                                    w = wqkv[:, k, 2 * D:3 * D] if b.nxt == "A" else wx[:, 2, k, :]
                                    mm = nc.tensor.matmul(out, xT[:, k, tt * P:(tt + 1) * P], w, start=k == 0, stop=k == FT - 1)
                        elif name == "negmax":
                            k = j if b.kind and j else (4 if b.kind else 1)
                            pe.wait_ge(s["negmax_split"], b.at("negmax_split", k))
                            mrow_ps = psM[:, 0:T // 2].bitcast(F16)
                            for qt in range(TT):
                                mm = nc.tensor.transpose(mrow_ps[0:2 * GH, qt * P:(qt + 1) * P],
                                                         mparts[:, qt, :, :].rearrange("p s h -> p (s h)"), ident_h[:, :])
                        elif name == "out":
                            pe.wait_ge(s["attn_out"], b.at("attn_out", 1))
                            if b.fin == "A":
                                pe.wait_ge(w_in, 16 * 9)
                            w = wo1 if b.fin == "A" else wp
                            for i in range(2):
                                tt = 2 * j + i
                                for k in range(FT):
                                    mm = nc.tensor.matmul(psM[:, i * D:(i + 1) * D], attn[:, k, tt * P:(tt + 1) * P],
                                                          w[:, k, :], start=k == 0, stop=k == FT - 1)
                        elif name == "logits":
                            pe.wait_ge(s["zT_out"], b.at("zT_out", 2))
                            for tt in range(TT):
                                for k in range(FT):
                                    mm = nc.tensor.matmul(psM[:, tt * E:(tt + 1) * E], zT[:, k, tt * P:(tt + 1) * P],
                                                          wg[:, k, :], start=k == 0, stop=k == FT - 1)
                        elif name == "count":
                            pe.wait_ge(s["onehot_out"], b.at("onehot_out", 1))
                            for tt in range(TT + 1):
                                for o in range(min(tt + 1, TT)):
                                    w = tri if o == tt else ones_bf[:, :]
                                    mm = nc.tensor.matmul(psM[:, tt * E:(tt + 1) * E], w, onehot[:, o * E:(o + 1) * E],
                                                          start=o == 0, stop=o == min(tt, TT - 1))
                        mm.then_inc(s["jobs_done"], 1)
            pe.wait_ge(s["route_dve"], total["route_dve"])
            pe.wait_ge(s["av_out"], total["av_out"])

            def transpose_rows(c, loaded, free):
                pe.wait_ge(rows_in[c], loaded)
                need(pe, rowsT_out, free)
                for m in range(FT):
                    for st in range(2):
                        mm = nc.tensor.transpose(psR[c][:, m * CAP + st * P:m * CAP + (st + 1) * P],
                                                 rows_sb[c][:, st, m * P:(m + 1) * P], ident)
                mm.then_inc(rowsT_done, 1)

            def hidden(e, c, loaded):
                pe.wait_ge(w1_in[c], loaded)
                pe.wait_ge(rowsT_out, e + 1)
                for f2 in range(FF // 2):
                    need(pe, hid_out, e * 4 + f2 - 3)
                    for i in range(2):
                        f = 2 * f2 + i
                        for k in range(FT):
                            mm = nc.tensor.matmul(psH[f2][:, i * CAP:(i + 1) * CAP], w1_sb[c][:, k, f * P:(f + 1) * P],
                                                  rowsT[c][:, k, :], start=k == 0, stop=k == FT - 1)
                    mm.then_inc(hid_done, 1)

            def output(e, c, loaded, free):
                pe.wait_ge(w2_in[c], loaded)
                pe.wait_ge(hid_out, e * 4 + 4)
                need(pe, y_out, free)
                for st in range(2):
                    for f in range(FF):
                        mm = nc.tensor.matmul(psY[c][:, st * D:(st + 1) * D], hT[c][:, f, st * P:(st + 1) * P],
                                              w2_sb[c][:, f, :], start=f == 0, stop=f == FF - 1)
                mm.then_inc(y_done, 1)

            transpose_rows(0, 16, 0)
            transpose_rows(1, 16, 0)
            hidden(0, 0, 16)
            hidden(1, 1, 16)
            transpose_rows(0, 32, 1)
            output(0, 0, 16, 0)
            hidden(2, 0, 32)
            transpose_rows(1, 32, 2)
            output(1, 1, 16, 0)
            with pe.Fori(0, E // 2 - 2) as i:
                hidden(i * 2 + 3, 1, i * 16 + 32)
                transpose_rows(0, i * 16 + 48, i * 2 + 3)
                output(i * 2 + 2, 0, i * 16 + 32, i * 2 + 1)
                hidden(i * 2 + 4, 0, i * 16 + 48)
                transpose_rows(1, i * 16 + 48, i * 2 + 4)
                output(i * 2 + 3, 1, i * 16 + 32, i * 2 + 2)
            hidden(E - 1, 1, 16 * (E // 2))
            output(E - 2, 0, 16 * (E // 2), E - 3)
            output(E - 1, 1, 16 * (E // 2), E - 2)

        @block.scalar
        def _(act):
            act.wait_ge(rows_zero, 32)
            act.wait_ge(w1_in0, 16 * 13)
            for b in stretches(act, blocks):
                np_ = 1 - b.parity
                jobs = b.jobs()
                for t in range(SLOTS):
                    if b.kind:
                        q0 = q_from(b.kind, t % 8 // 2)
                        act.wait_ge(s["scores_k"], b.at("scores_k", t + 1))
                        k = int(b.prev is not None) + (t - 4) // 2 + 1 if t >= 2 else -99
                        if t >= 4:
                            need(act, s["av_done"], b.at("av_done", k))
                        elif b.prev:
                            need(act, s["av_done"], b.at("av_done", t // 2))
                        nc.scalar.activation(probs[:, t % P_RING, :, q0:T], psK[:, t % 2, :, q0:T], ACT.Exp,
                                             scale=SM_SCALE).then_inc(s["exp_done"], 1)
                    for idx, (slot, name, j) in enumerate(jobs):
                        if slot == t and name in ("xT", "zT", "ctxT", "proj", "negmax"):
                            act.wait_ge(s["jobs_done"], b.at("jobs_done", idx + 1))
                            if name == "xT":
                                need(act, s["v_out"], b.at("v_out"))
                                nc.scalar.copy(xT[:, j, :], psM[:, :]).then_inc(s["xT_out"], 1)
                            elif name == "zT":
                                nc.scalar.copy(zT[:, j, :], psM[:, :]).then_inc(s["zT_out"], 1)
                            elif name == "ctxT":
                                nc.scalar.copy(ctxT, psM[:, :]).then_inc(s["ctxT_out"], 1)
                            elif name == "proj":
                                ft, qk = j // 2, j % 2
                                bias = bias_qk[:, 2 * "ABC".index(b.nxt) + qk, ft:ft + 1]
                                if b.nxt == "A":
                                    need(act, s["rope_out"], b.at("rope_out", j - 1))
                                    nc.scalar.activation(rope_x[:, j % 2, :], psM[:, :], ACT.Identity, bias=bias
                                                         ).then_inc(s["rope_in"], 1)
                                else:
                                    if j == 0:
                                        need(act, s["parts_stored"], b.at("parts_stored"))
                                    nc.scalar.activation(parts[:, qk, ft, 0, :], psM[:, :], ACT.Identity, bias=bias
                                                         ).then_inc(s["hi_out"], 1)
                            else:
                                k = j if b.kind and j else (4 if b.kind else 1)
                                g = j
                                o = (g + 1) % 2
                                if b.kind:
                                    before = {1: (0, 0), 2: (1, 32), 3: (0, 32), 0: (1, 64)}[g]
                                    need(act, s[f"negmax_in_{before[0]}"], b.at(f"negmax_in_{before[0]}", before[1]))
                                nc.scalar.copy(mrows[:, :], psM[0:2 * GH, 0:T // 2].bitcast(F16)
                                               ).then_inc(s["negmax_rows"], 1)
                                act.wait_ge(s["negmax_rows"], b.at("negmax_rows", k))
                                par = b.parity if j else np_
                                for part in range(2):
                                    act.dma_start(stack_of(par, 0)[STACK + part:STACK + part + 1, GH * g:GH * (g + 1), :],
                                                  mrows[GH * part:GH * (part + 1), :]).then_inc(s[f"negmax_in_{g % 2}"], 16)
                        if name == "rope" and slot == t - 1:
                            act.wait_ge(s["rope_out"], b.at("rope_out", j + 1))
                            if j == 0:
                                need(act, s["parts_stored"], b.at("parts_stored"))
                            nc.scalar.copy(parts[:, j % 2, j // 2, 0, :], rope_s).then_inc(s["hi_out"], 1)
                        if name == "logits" and slot == t:
                            act.wait_ge(s["route_dve"], b.at("route_dve", 2))
                            nc.scalar.activation(rt[:, 1, :], rt[:, 0, :], ACT.Exp).then_inc(s["route_exp"], 1)
            def out_rows(e, c):
                act.wait_ge(rowsT_done, e + 1)
                need(act, hid_done, e * 4 - 4)
                nc.scalar.copy(rowsT[c].rearrange("p m s -> p (m s)"), psR[c]).then_inc(rowsT_out, 1)

            def out_y(e, c, stored):
                act.wait_ge(y_done, e + 1)
                need(act, eo_stored[c], stored)
                nc.scalar.copy(eo_sb[c].rearrange("p s m -> p (s m)"), psY[c]).then_inc(y_out, 1)

            out_rows(0, 0)
            out_rows(1, 1)
            out_rows(2, 0)
            out_y(0, 0, 0)
            out_rows(3, 1)
            out_y(1, 1, 0)
            with act.Fori(0, E // 2 - 2) as i:
                out_rows(i * 2 + 4, 0)
                out_y(i * 2 + 2, 0, i * 16 + 16)
                out_rows(i * 2 + 5, 1)
                out_y(i * 2 + 3, 1, i * 16 + 16)
            out_y(E - 2, 0, 16 * (E // 2 - 1))
            out_y(E - 1, 1, 16 * (E // 2 - 1))

        @block.vector
        def _(dve):
            nc.vector.memset(probs[:, :, :, :], 0.0).then_inc(zeroed, 1)
            nc.vector.memset(minus_half[:, :], -0.5).then_inc(misc_set, 1)
            nc.vector.memset(filled[:, :], 0.0).then_inc(misc_set, 1)
            dve.wait_ge(cst_in, 16)
            nc.vector.tensor_copy(ident_bf, ident).then_inc(cst_set, 1)
            nc.vector.tensor_copy(ident_h[:, :], ident).then_inc(cst_set, 1)
            for j, dst in ((2, mask_q), (3, mask_k), (4, tri)):
                nc.vector.tensor_copy(dst, consts[:, j * P:(j + 1) * P]).then_inc(cst_set, 1)
            nc.vector.memset(ones_bf[:, :], 1.0).then_inc(cst_set, 1)
            nc.vector.memset(V[:, :, :, :].rearrange("p a k (h c) -> p (a k) h c", h=H)[:, :, :, HD:2 * HD], 1.0
                             ).then_inc(cst_set, 1)
            dve.wait_ge(cst_set, 7)
            nc.vector.memset(stack[64:96, 0, :, :], 0.0).then_inc(stack_set0, 1)
            nc.vector.memset(stack[96:98, 0, 1, :], MSCALE).then_inc(stack_set0, 1)
            dve.wait_ge(w1_in0, 16 * 13)

            def layernorm(b, batch, t, first, k):
                if t == first:
                    for tt in range(TT):
                        o = nc.vector.bn_stats(stats[:, tt, :], X[:, bass.ds(batch, 1), tt * D:(tt + 1) * D].rearrange("p o d -> p (o d)"))
                    o.then_inc(s["bn_done"], 1)
                    need(dve, s["bn_done"], b.at("bn_done", k))
                    mean_e, ss_e, mean_o, ss_o = (stats[:, :, c] for c in (1, 2, 4, 5))
                    nc.vector.tensor_tensor(lnt[:, 0, :], mean_e, mean_o, ALU.add)
                    nc.vector.tensor_tensor(lnt[:, 1, :], mean_e, mean_o, ALU.subtract)
                    nc.vector.tensor_tensor(lnt[:, 2, :], ss_e, ss_o, ALU.add).then_inc(s["ln_step"], 1)
                    dve.wait_ge(s["ln_step"], b.at("ln_step", 3 * k - 2))
                    nc.vector.tensor_tensor(lnt[:, 3, :], lnt[:, 1, :], lnt[:, 1, :], ALU.mult).then_inc(s["ln_step"], 1)
                    nc.vector.tensor_scalar(lnt[:, 5, :], lnt[:, 0, :], 0.5, None, ALU.mult)
                    dve.wait_ge(s["ln_step"], b.at("ln_step", 3 * k - 1))
                    nc.vector.scalar_tensor_tensor(out=lnt[:, 4, :], in0=lnt[:, 3, :], scalar=D / 4.0, in1=lnt[:, 2, :],
                                                   op0=ALU.mult, op1=ALU.add).then_inc(s["ln_step"], 1)
                    dve.wait_ge(s["ln_step"], b.at("ln_step", 3 * k))
                    nc.vector.tensor_scalar(lnt[:, 6, :], lnt[:, 4, :], 1.0 / D, LN_EPS, ALU.mult, ALU.add
                                            ).then_inc(s["ln_var"], 1)
                if t == first + 1:
                    dve.wait_ge(s["ln_rstd"], b.at("ln_rstd", k))
                    need(dve, s["scattered"], b.at("scattered"))
                    for tt in range(TT):
                        o = nc.vector.tensor_scalar(xn[:, tt, :], X[:, bass.ds(batch, 1), tt * D:(tt + 1) * D].rearrange("p o d -> p (o d)"),
                                                    lnt[:, 5, tt:tt + 1], rstd[:, tt:tt + 1], ALU.subtract, ALU.mult)
                    o.then_inc(s["ln_out"], 1)

            for b in stretches(dve, blocks):
                np_ = 1 - b.parity
                jobs = b.jobs()
                ln = int(b.nxt in ("A", "B"))
                for t in range(SLOTS):
                    if b.nxt == "B" and t == 0:
                        need(dve, s["x_out"], b.at("x_out"))
                    if b.route and t == 20:
                        need(dve, s["x_out"], b.at("x_out", 2 if b.fin else 0))
                    for j in range(2):
                        later, u, k = s_unit(b, t, j)
                        kind = has_s(b, later)
                        if not kind:
                            continue
                        g = u // (S_UNITS // NG)
                        n = (u % TT + 1) * P if kind == "B" else T
                        if u % (S_UNITS // NG) == 0:
                            need(dve, s["negmax_split"], b.at("negmax_split", t // 8 if b.kind else 0))
                        dve.wait_ge(s["scores_q"], b.at("scores_q", k + 1))
                        nc.vector.tensor_reduce(negmax[:, g % 2, u % 16:u % 16 + 1], psS[:, u % 2, 0:n], AX_X, ALU.max,
                                                negate=True).then_inc(s["max_done"], 1)
                    if (b.kind and t in (4, 12, 20)) or (b.nxt and t == 28):
                        g = (t // 8 + 1) % NG
                        k = t // 8 + 1 if b.kind else 1
                        done = 2 * (t - 4) + 8 if b.kind else 16
                        view = negmax[:, g % 2, :].rearrange("p (h q) -> p q h", h=GH)
                        dve.wait_ge(s["max_done"], b.at("max_done", done))
                        need(dve, s["negmax_rows"], b.at("negmax_rows", k - 1))
                        nc.vector.tensor_scalar(mparts[:, :, 0, :], view, 1.0 / MSCALE, None, ALU.mult
                                                ).then_inc(s["negmax_hi"], 1)
                        dve.wait_ge(s["negmax_hi"], b.at("negmax_hi", k))
                        nc.vector.scalar_tensor_tensor(out=mparts[:, :, 1, :], in0=view, scalar=1.0 / MSCALE,
                                                       in1=mparts[:, :, 0, :], op0=ALU.mult, op1=ALU.subtract
                                                       ).then_inc(s["negmax_split"], 1)
                    for g in range(NG):
                        mine = g < NG - 1 and b.kind and t == 8 * g + 9
                        prev = g == NG - 1 and b.prev and t == 1
                        if mine or prev:
                            k = int(b.prev is not None) + 4 * (g + 1) if mine else 1
                            dve.wait_ge(s["av_done"], b.at("av_done", k))
                            if prev:
                                used = b.at("packed_1")
                            elif g % 2:
                                used = b.at("packed_1", 128 if b.prev else 0)
                            else:
                                used = b.at("packed_0", 64 * g)
                            need(dve, s[f"packed_{g % 2}"], used)
                            nc.vector.tensor_copy(U[:, g % 2, :], psO[:, :]).then_inc(s["av_out"], 1)
                    if t == 3 and b.prev:
                        dve.wait_ge(s["packed_0"], b.at("packed_0"))
                        dve.wait_ge(s["packed_1"], b.at("packed_1", 128))
                        need(dve, s["recip_stored"], b.at("recip_stored"))
                        nc.vector.reciprocal(recip[:, :], sums[:, :]).then_inc(s["recip_done"], 1)
                    if ln and t in (0, 1):
                        if b.nxt == "A" and t == 0:
                            dve.wait_ge(*((x0_in, 16) if b.n < 0 else (x_in, 16 * (NB - 1))))
                        layernorm(b, b.batch(1), t, 0, 1)
                    if b.n == -1 and t == 2:
                        nc.vector.memset(stack[64:96, 1, :, :], 0.0).then_inc(stack_set1, 1)
                        nc.vector.memset(stack[96:98, 1, 1, :], MSCALE).then_inc(stack_set1, 1)
                    for idx, (slot, name, j) in enumerate(jobs):
                        if slot != t:
                            continue
                        done = b.at("jobs_done", idx + 1)
                        if name == "proj" and b.nxt != "A":
                            ft, qk = j // 2, j % 2
                            dve.wait_ge(s["hi_out"], b.at("hi_out", j + 1))
                            nc.vector.scalar_tensor_tensor(
                                out=parts[:, qk, ft, 1, :], in0=psM[:, :],
                                scalar=bias_qk[:, 2 * "ABC".index(b.nxt) + qk, ft:ft + 1], in1=parts[:, qk, ft, 0, :],
                                op0=ALU.add, op1=ALU.subtract).then_inc(s["lo_out"], 1)
                        elif name == "rope":
                            dve.wait_ge(s["jobs_done"], done)
                            need(dve, s["lo_out"], b.at("lo_out", j))
                            nc.vector.tensor_tensor(rope_s, psM[:, :], rope_cs[:, 1, :], ALU.mult
                                                    ).then_inc(s["rope_sin"], 1)
                            dve.wait_ge(s["rope_sin"], b.at("rope_sin", j + 1))
                            dve.wait_ge(s["rope_cos"], b.at("rope_cos", j + 1))
                            nc.vector.tensor_tensor(rope_s, rope_s, rope_c, ALU.add).then_inc(s["rope_out"], 1)
                        elif name == "v":
                            dve.wait_ge(s["jobs_done"], done)
                            for i in range(2):
                                tt = 2 * j + i
                                nc.vector.tensor_tensor(
                                    v_of(np_)[:, tt, :, 0:HD],
                                    psM[:, i * D:(i + 1) * D].rearrange("p (h c) -> p h c", h=H),
                                    bias_v[:, "ABC".index(b.nxt), :].rearrange("p (h c) -> p h c", h=H), ALU.add
                                ).then_inc(s["v_out"], 1)
                        elif name == "out":
                            dve.wait_ge(s["jobs_done"], done)
                            need(dve, s["x_bias"], b.at("x_bias", 0))
                            xs = X[:, bass.ds(b.batch(-1), 1), 2 * j * D:2 * (j + 1) * D].rearrange("p o d -> p (o d)")
                            nc.vector.tensor_tensor(xs, psM[:, :], xs, ALU.add).then_inc(s["x_out"], 1)
                    if b.route:
                        layernorm(b, b.batch(-1) if b.kind is None else b.batch(-2), t, 20, ln + 1)
                        step = [2 * 0]

                        def chain(ins, k):
                            ins.then_inc(s["route_dve"], 1)
                            dve.wait_ge(s["route_dve"], b.at("route_dve", k))

                        def wide(j):
                            return rt[:, j, :].rearrange("p (t e) -> p t e", e=E)

                        def over(j):
                            return rs[:, j, :, None].to_broadcast([P, TT, E])

                        gb = b.batch(-1) if b.kind is None else b.batch(-2)
                        idx = [i for i, job in enumerate(jobs) if job[1] == "logits"][0]
                        if t == 24:
                            dve.wait_ge(s["jobs_done"], b.at("jobs_done", idx + 1))
                            logits = psM[:, 0:TT * E].rearrange("p (t e) -> p t e", e=E)
                            chain(nc.vector.tensor_reduce(rs[:, 0, :], logits, AX_X, ALU.max), 1)
                            chain(nc.vector.tensor_tensor(wide(0), logits, over(0), ALU.subtract), 2)
                        if t == 25:
                            dve.wait_ge(s["route_exp"], b.at("route_exp", 1))
                            chain(nc.vector.tensor_reduce(rs[:, 1, :], wide(1), AX_X, ALU.add), 3)
                            chain(nc.vector.reciprocal(rs[:, 2, :], rs[:, 1, :]), 4)
                            chain(nc.vector.tensor_tensor(wide(2), wide(1), over(2), ALU.mult), 5)
                            chain(nc.vector.tensor_reduce(rs[:, 3, :], wide(2), AX_X, ALU.max), 6)
                            chain(nc.vector.tensor_tensor(wide(3), wide(2), over(3), ALU.is_ge), 7)
                            chain(nc.vector.scalar_tensor_tensor(out=rt[:, 4, :], in0=rt[:, 3, :], scalar=-1000.0,
                                                                 in1=expert_no, op0=ALU.mult, op1=ALU.add), 8)
                            chain(nc.vector.tensor_reduce(rs[:, 4, :], wide(4), AX_X, ALU.min), 9)
                            chain(nc.vector.tensor_tensor(wide(5), wide(4), over(4), ALU.is_equal), 10)
                            nc.vector.tensor_copy(onehot[:, :], rt[:, 5, :]).then_inc(s["onehot_out"], 1)
                        if t == 27:
                            dve.wait_ge(s["jobs_done"], b.at("jobs_done", idx + 2))
                            before = psM[:, 0:TT * E].rearrange("p (t e) -> p t e", e=E)
                            chain(nc.vector.tensor_tensor(wide(0), before, filled[:, None, :].to_broadcast([P, TT, E]), ALU.add), 11)
                            chain(nc.vector.tensor_tensor(filled[:, :], psM[:, TT * E:(TT + 1) * E], filled[:, :], ALU.add), 12)
                            chain(nc.vector.tensor_tensor(wide(1), wide(0), wide(5), ALU.mult), 13)
                            chain(nc.vector.tensor_reduce(rs[:, 5, :], wide(1), AX_X, ALU.add), 14)
                            chain(nc.vector.tensor_scalar(rs[:, 6, :], rs[:, 5, :], float(CAP), None, ALU.is_lt), 15)
                            chain(nc.vector.tensor_tensor(gates[:, bass.ds(gb, 1), :].rearrange("p o t -> p (o t)"),
                                                          rs[:, 3, :], rs[:, 6, :], ALU.mult), 16)
                            chain(nc.vector.tensor_scalar(rs[:, 7, :], rs[:, 5, :], float(CAP - 1), 1000.0 * CAP,
                                                          ALU.min, ALU.add), 17)
                            chain(nc.vector.scalar_tensor_tensor(out=rs[:, 8, :], in0=rs[:, 4, :], scalar=float(CAP),
                                                                 in1=rs[:, 7, :], op0=ALU.mult, op1=ALU.add), 18)
                            chain(nc.vector.tensor_copy(gather_from[:, bass.ds(gb, 1), :].rearrange("p o t -> p (o t)"),
                                                        rs[:, 8, :]), 19)
                            chain(nc.vector.tensor_scalar(rs[:, 9, :], rs[:, 6, :], -65536.0, 65536.0, ALU.mult, ALU.add), 20)
                            nc.vector.tensor_tensor(scatter_to[:, :], rs[:, 8, :], rs[:, 9, :], ALU.add
                                                    ).then_inc(s["index_out"], 1)

            def relu(e, c):
                for f2 in range(FF // 2):
                    dve.wait_ge(hid_done, e * 4 + f2 + 1)
                    if f2 == 0:
                        need(dve, y_done, e - 1)
                    nc.vector.tensor_scalar(hT[c][:, 2 * f2:2 * f2 + 2, :].rearrange("p f s -> p (f s)"), psH[f2],
                                            0.0, None, ALU.max).then_inc(hid_out, 1)

            relu(0, 0)
            relu(1, 1)
            with dve.Fori(0, E // 2 - 1) as i:
                for c in range(2):
                    relu(i * 2 + 2 + c, c)
            for n in range(NB):
                dve.wait_ge(got_in[n % P_RING], 16 * TT * (n // P_RING + 1))
                for tt in range(TT):
                    xs = X[:, n, tt * D:(tt + 1) * D]
                    nc.vector.scalar_tensor_tensor(out=xs, in0=got[:, n % P_RING, tt * D:(tt + 1) * D],
                                                   scalar=gates[:, n, tt:tt + 1], in1=xs, op0=ALU.mult, op1=ALU.add
                                                   ).then_inc(got_used, 1)

        @block.gpsimd
        def _(pool):
            pool.wait_ge(misc_set, 2)
            pool.wait_ge(w1_in0, 16 * 13)

            def rstd_of(b, k):
                need(pool, s["ln_var"], b.at("ln_var", k))
                nc.gpsimd.tensor_tensor(rstd[:, :], lnt[:, 6, :], minus_half[:, :], ALU.pow).then_inc(s["ln_rstd"], 1)

            for b in stretches(pool, blocks):
                jobs = b.jobs()
                ln = int(b.nxt in ("A", "B"))
                for t in range(SLOTS):
                    if ln and t == 0:
                        rstd_of(b, 1)
                    if ln and t == 3:
                        need(pool, s["ln_out"], b.at("ln_out", 1))
                        xs = X[:, bass.ds(b.batch(1), 1), :].rearrange("p o (t d) -> p (o t) d", t=TT)
                        bo = bias_o[:, 0 if b.nxt == "A" else 1, None, :].to_broadcast([P, TT, D])
                        nc.gpsimd.tensor_tensor(xs, xs, bo, ALU.add).then_inc(s["x_bias"], 1)
                    if t == 4 and b.prev:
                        pool.wait_ge(s["recip_in"], b.at("recip_in", 16 * FT))
                        need(pool, s["x_out"], b.at("x_out"))
                        pool.wait_ge(s["packed_0"], b.at("packed_0"))
                        pool.wait_ge(s["packed_1"], b.at("packed_1", 128))
                        if b.prev == "C":
                            nc.gpsimd.tensor_tensor(packed[:, :, :], packed[:, :, :], recipB[:, :, :], ALU.mult
                                                    ).then_inc(s["attn_mul"], 1)
                            pool.wait_ge(s["attn_mul"], b.at("attn_mul", 1))
                            nc.gpsimd.tensor_tensor(attn[:, :, :], attn_b, packed[:, :, :], ALU.add
                                                    ).then_inc(s["attn_out"], 1)
                        else:
                            dst = attn[:, :, :] if b.prev == "A" else attn_b
                            nc.gpsimd.tensor_tensor(dst, packed[:, :, :], recipB[:, :, :], ALU.mult
                                                    ).then_inc(s["attn_out"], 1)
                    for slot, name, j in jobs:
                        if name == "rope":
                            if slot == t + 1:
                                pool.wait_ge(s["rope_in"], b.at("rope_in", j + 1))
                                need(pool, s["rope_out"], b.at("rope_out", j))
                                nc.gpsimd.tensor_tensor(rope_c, rope_x[:, j % 2, :], rope_cs[:, 0, :], ALU.mult
                                                        ).then_inc(s["rope_cos"], 1)
                            if slot == t:
                                pool.wait_ge(s["hi_out"], b.at("hi_out", j + 1))
                                nc.gpsimd.tensor_tensor(parts[:, j % 2, j // 2, 1, :], rope_s, parts[:, j % 2, j // 2, 0, :],
                                                        ALU.subtract).then_inc(s["lo_out"], 1)
                    if b.route and t == 20:
                        rstd_of(b, ln + 1)
                    if b.route and t == 28:
                        pool.wait_ge(rows_zero, 32)
                        pool.wait_ge(s["index_out"], b.at("index_out", 1))
                        for tt in range(TT):
                            nc.gpsimd.indirect_dma_start(
                                out=rows_dram[:, :], out_offset=bass.IndirectOffsetOnAxis(ap=scatter_to[:, tt:tt + 1], axis=0),
                                in_=xn[:, tt, :], in_offset=None, bounds_check=E * CAP - 1, oob_is_err=False
                            ).then_inc(s["scattered"], 16)
            for c in range(2):
                pool.wait_ge(eo_stored[c], 16 * (E // 2))
            for n in range(NB):
                if n >= P_RING:
                    pool.wait_ge(got_used, TT * (n - P_RING + 1))
                for tt in range(TT):
                    nc.gpsimd.indirect_dma_start(
                        out=got[:, n % P_RING, tt * D:(tt + 1) * D], out_offset=None, in_=expert_dram[:, :],
                        in_offset=bass.IndirectOffsetOnAxis(ap=gather_from[:, n, tt:tt + 1], axis=0)
                    ).then_inc(got_in[n % P_RING], 16)


def _constants():
    i = np.arange(P)
    ident = np.eye(P, dtype=np.float32)
    rot = np.zeros((P, P), np.float32)
    rot[i[1::2], i[0::2]] = -1.0
    rot[i[0::2], i[1::2]] = 1.0
    mask_q = np.where(i[None, :] > i[:, None], np.float32(NEG), np.float32(0))
    mask_k = np.ascontiguousarray(mask_q.T)
    before = (i[:, None] < i[None, :]).astype(np.float32)
    number = np.tile(np.arange(E, dtype=np.float32), (P, TT))
    consts = np.concatenate([ident, rot, mask_q, mask_k, before, number], axis=1)
    half = HD // 2
    theta = (np.float32(1.0) / np.float32(10000.0) ** (np.arange(half, dtype=np.float32) / np.float32(half)))
    freqs = np.arange(T, dtype=np.float32)[:, None] * theta[None, :].astype(np.float32)
    col = (i % HD) // 2
    rope = np.stack([np.cos(freqs)[:, col].T, np.sin(freqs)[:, col].T]).astype(np.float32)
    return consts, np.ascontiguousarray(rope)


def kernel(**inputs):
    import numpy as _np
    import concourse.bacc as _bacc
    from concourse import mybir as _mybir
    from concourse.bass_utils import run_bass_kernel_spmd as _run

    nc = _bacc.Bacc("TRN2", target_bir_lowering=False, num_devices=1)
    consts, rope = _constants()
    arrays = {"consts": consts, "rope": rope}
    for name, v in inputs.items():
        if name == "L0_attn_W_qkv":
            arrays["W_qkv_T"] = _np.ascontiguousarray(_np.asarray(v).T)
        elif name == "L0_attn_W_out":
            arrays["W_out_T"] = _np.ascontiguousarray(_np.asarray(v).T)
        else:
            arrays["ctx" if name == "ctx_512" else name] = _np.ascontiguousarray(v)
    aps, feed = {}, {}
    for name, v in arrays.items():
        feed[f"in_{name}_dram"] = v
        aps[name] = nc.dram_tensor(f"in_{name}_dram", v.shape, _mybir.dt.from_np(v.dtype), kind="ExternalInput").ap()
    aps["out"] = nc.dram_tensor("out_0_dram", (NB, T, D), _mybir.dt.from_np(_np.dtype("float32")), kind="ExternalOutput").ap()
    build(nc, aps)
    r = _run(nc, [feed], core_ids=[0])
    return r.results[0]["out_0_dram"]
```

```python
from contextlib import ExitStack

import numpy as np

import concourse.bass as bass
from concourse import mybir

F32 = mybir.dt.float32
F16 = mybir.dt.float16
BF16 = mybir.dt.bfloat16
U32 = mybir.dt.uint32
ALU = mybir.AluOpType
ACT = mybir.ActivationFunctionType
AX_X = mybir.AxisListType.X

P = 128
NB, T, D, DC = 8, 512, 256, 128
H, HD = 16, 16
TT = T // P
FT = D // P
GH = 4
NG = H // GH
SLOTS = NG * TT * 2
S_UNITS = H * TT
RING_S = RING_K = 3
LEAD = 12
E, CAP, F = 16, NB * T // 16, 1024
FF = F // P
STACK = 96
MROWS = STACK + 2
MSCALE = 1024.0
SM_SCALE = HD ** -0.5
P_RING = 4
NEG = -1e30
LN_EPS = 1e-5


def q_from(kind, kt):
    return kt * P if kind == "B" else 0


class Body:

    def __init__(self, kind, prev, nxt, nx2, n, dn=0, route=False):
        self.kind, self.prev, self.nxt, self.nx2, self.route = kind, prev, nxt, nx2, route
        self.parity = n % 2
        self.fin = prev if prev in ("A", "C") else None
        self.n, self.dn = n, dn
        self.base, self.stride, self.i = {}, {}, 0

    def at(self, sem, k=0):
        return self.base[sem] + self.i * self.stride.get(sem, 0) + k if self.stride.get(sem, 0) \
            else self.base[sem] + k

    def batch(self, ahead=0):
        n = self.n + ahead
        if n < NB:
            return n + self.dn * self.i if self.dn else n
        b = (n - NB) // 2
        return b + (self.dn // 2) * self.i if self.dn else b

    def counts(self):
        c, run, prep, had = {}, self.kind is not None, self.nxt, self.prev is not None
        c["scores_q"] = c["max_done"] = (2 * (SLOTS - LEAD) if run else 0) + (2 * LEAD if prep else 0)
        groups = (3 if run else 0) + (1 if prep else 0)
        c["negmax_hi"] = c["negmax_split"] = c["negmax_rows"] = groups
        c["negmax_in_0"] = 32 * ((1 if run else 0) + (1 if prep else 0))
        c["negmax_in_1"] = 64 if run else 0
        c["scores_k"] = c["exp_done"] = 2 * SLOTS if run else 0
        c["av_done"] = self.av_count(SLOTS - 1)
        c["av_out"] = (3 if run else 0) + (1 if had else 0)
        c["packed_0"] = 128 * 2 if run else 0
        c["packed_1"] = (128 if run else 0) + (128 if had else 0)
        for s in ("recip_done", "attn_out"):
            c[s] = int(had)
        c["recip_stored"] = 16 * int(had)
        c["recip_in"] = 16 * FT * int(had)
        c["attn_mul"] = int(self.prev == "C")
        c["jobs_done"] = len(self.jobs())
        ln = int(self.nx2 in ("A", "B"))
        rt = int(self.route)
        c["bn_done"] = c["ln_var"] = c["ln_rstd"] = c["ln_out"] = ln + rt
        c["ln_step"] = 3 * (ln + rt)
        c["x_bias"] = ln
        c["xT_out"] = 2 * ln
        c["ctx_in"] = 16 * int(self.nx2 == "C")
        c["ctxT_out"] = int(self.nx2 == "C")
        rope = 4 * int(self.nx2 == "A")
        for s in ("rope_in", "rope_cos", "rope_sin", "rope_out"):
            c[s] = rope
        c["swap_in"] = 32 * rope
        c["hi_out"] = c["lo_out"] = 4 if self.nx2 else 0
        c["parts_stored"] = 64 if self.nx2 else 0
        c["stack_in"] = 128 if prep else 0
        c["v_out"] = 4 if prep else 0
        c["x_out"] = 2 if self.fin else 0
        c["zT_out"] = 2 * rt
        c["route_dve"] = ROUTE_STEPS * rt
        c["route_exp"] = c["onehot_out"] = c["index_out"] = rt
        c["scattered"] = 16 * TT * rt
        return c

    def av(self, t):
        kind = self.kind if t >= 3 else self.prev
        if not kind:
            return None
        half = (t + 1) % 2
        unit = (t - 3 - half) % SLOTS
        first = q_from(kind, unit % 8 // 2)
        q0, q1 = max(first, half * T // 2), (half + 1) * T // 2
        return (t < 3, unit, q0, q1, q0 == first) if q0 < q1 else None

    def av_count(self, t):
        return sum(self.av(i) is not None for i in range(t + 1))

    def jobs(self):
        out = []
        if self.nxt:
            out += [(2, "v", 0), (4, "v", 1), (29, "negmax", 0)]
        if self.kind:
            out += [(5, "negmax", 1), (13, "negmax", 2), (21, "negmax", 3)]
        if self.nx2 in ("A", "B"):
            out += [(7, "xT", 0), (9, "xT", 1), (11, "proj", 0), (14, "proj", 1), (17, "proj", 2), (20, "proj", 3)]
        if self.nx2 == "C":
            out += [(7, "ctxT", 0), (9, "proj", 0), (11, "proj", 1), (14, "proj", 2), (17, "proj", 3)]
        if self.fin:
            out += [(23, "out", 0), (25, "out", 1)] if self.kind else [(6, "out", 0), (7, "out", 1)]
        if self.route:
            out += [(19, "zT", 0), (20, "zT", 1), (22, "logits", 0), (25, "count", 0)]
        return sorted(out, key=lambda j: j[0])

    def freed(self, idx):
        if idx < 0:
            return ("rope_in" if self.n < 0 else "negmax_rows" if self.kind else "route_dve"), 0
        _, name, j = self.jobs()[idx]
        if name == "proj":
            return ("rope_in" if self.nx2 == "A" else "lo_out"), j + 1
        if name == "negmax":
            return "negmax_rows", (j if j else 4) if self.kind else 1
        return {"xT": ("xT_out", j + 1), "ctxT": ("ctxT_out", 1), "zT": ("zT_out", j + 1), "v": ("v_out", 2 * j + 2),
                "out": ("x_out", j + 1), "logits": ("route_dve", 2),
                "count": ("route_dve", 12)}[name]


ROUTE_STEPS = 20


def plan():
    blocks = [
        (1, [Body(None, None, None, "A", -2)]),
        (1, [Body(None, None, "A", "A", -1)]),
        (1, [Body("A", None, "A", "A", 0)]),
        (2, [Body("A", "A", "A", "A", 1, 2), Body("A", "A", "A", "A", 2, 2)]),
        (1, [Body("A", "A", "A", "A", 5)]),
        (1, [Body("A", "A", "A", "B", 6)]),
        (1, [Body("A", "A", "B", "C", 7)]),
        (1, [Body("B", "A", "C", "B", 8)]),
        (1, [Body("C", "B", "B", "C", 9)]),
        (6, [Body("B", "C", "C", "B", 10, 2), Body("C", "B", "B", "C", 11, 2, route=True)]),
        (1, [Body("B", "C", "C", None, 22)]),
        (1, [Body("C", "B", None, None, 23, route=True)]),
        (1, [Body(None, "C", None, None, 24, route=True)]),
    ]
    total = {}
    for times, bodies in blocks:
        cycle = {}
        for b in bodies:
            for s, k in b.counts().items():
                b.base[s] = total.get(s, 0) + cycle.get(s, 0)
                cycle[s] = cycle.get(s, 0) + k
        for b in bodies:
            b.stride = dict(cycle) if times > 1 else {}
        for s, k in cycle.items():
            total[s] = total.get(s, 0) + k * times
    return blocks, total


def stretches(eng, blocks):
    for times, bodies in blocks:
        if times == 1:
            for b in bodies:
                yield b
        else:
            with eng.Fori(0, times) as i:
                for b in bodies:
                    b.i = i
                    yield b
                    b.i = 0


def need(eng, sem, value):
    if not isinstance(value, int) or value > 0:
        eng.wait_ge(sem, value)


def build(nc, a):
    blocks, total = plan()
    ctx = ExitStack()
    with ctx:
        def sb(name, shape, dt):
            return ctx.enter_context(nc.sbuf_tensor(name, shape, dt))

        def sem(name):
            return ctx.enter_context(nc.semaphore(name))

        parts_dram = nc.dram_tensor("parts_scratch", [2, 2, 2, D, T], F16).ap()
        recip_dram = nc.dram_tensor("recip_scratch", [H, T], F32).ap()
        rows_dram = nc.dram_tensor("rows_scratch", [E * CAP, D], F32).ap()
        expert_dram = nc.dram_tensor("expert_scratch", [E * CAP, D], F32).ap()

        psS = ctx.enter_context(nc.psum_tensor("psS", [P, RING_S, T], F32))
        psK = ctx.enter_context(nc.psum_tensor("psK", [P, RING_K, T], F32))
        psO = ctx.enter_context(nc.psum_tensor("psO", [P, T], F32))
        psM = ctx.enter_context(nc.psum_tensor("psM", [P, T], F32))

        X = sb("X", [P, NB, TT * D], F32)
        stack = sb("stack", [P, 2, 2, H * T], F16)
        probs = sb("probs", [P, P_RING, 2, T], F32)
        V = sb("V", [P, 2, TT, H * 2 * HD], F32)
        parts = sb("parts", [P, 2, FT, 2, T], F16)
        xn = sb("xn", [P, TT, D], F32)
        xT = sb("xT", [P, FT, T], F32)
        U = sb("U", [P, 2, T], F32)
        packed = sb("packed", [P, FT, T], F32)
        sums = sb("sums", [P, 64], F32)
        recip = sb("recip", [P, 64], F32)
        recipB = sb("recipB", [P, FT, T], F32)
        attn = sb("attn", [P, FT, T], F32)
        wo1 = sb("wo1", [P, FT, D], F32)
        wx = sb("wx", [P, 4, FT, D], F32)
        wc = sb("wc", [P, 2, D], F32)
        wp = sb("wp", [P, FT, D], F32)
        wg = sb("wg", [P, FT, E], F32)
        shared = sb("shared", [P, 3072 + 1536], F32)
        rope_cs = shared[:, 0:1024].rearrange("p (s t) -> p s t", s=2)
        rope_x = shared[:, 1024:2048].rearrange("p (s t) -> p s t", s=2)
        rope_c = shared[:, 2048:2560]
        rope_s = shared[:, 2560:3072]
        wqkv = shared[:, 3072:4608].rearrange("p (k n) -> p k n", k=FT)
        attn_b = shared[:, 0:1024].rearrange("p (f t) -> p f t", f=FT)
        ctx_sb = shared[:, 1024:1536].rearrange("p (t c) -> p t c", t=TT)
        ctxT = shared[:, 1536:2048]
        zT = shared[:, 2048:3072].rearrange("p (f t) -> p f t", f=FT)
        bias_v = sb("bias_v", [P, 3, D], F32)
        bias_o = sb("bias_o", [P, 2, D], F32)
        bias_qk = sb("bias_qk", [P, 6, FT], F32)
        consts = sb("consts", [P, 4 * P + TT * E], F32)
        ident = consts[:, 0:P]
        expert_no = consts[:, 4 * P:4 * P + TT * E]
        halves = sb("halves", [P, 4, P], BF16)
        ident_bf, mask_q, mask_k, tri = (halves[:, j, :] for j in range(4))
        ones_bf = sb("ones_bf", [P, P], BF16)
        ident_h = sb("ident_h", [P, P], F16)
        negmax = sb("negmax", [P, 2, S_UNITS // NG], F32)
        mparts = sb("mparts", [P, TT, 2, GH], F16)
        mrows = sb("mrows", [2 * GH, T], F16)
        stats = sb("stats", [P, TT, 6], F32)
        lnt = sb("lnt", [P, 7, TT], F32)
        rstd = sb("rstd", [P, TT], F32)
        minus_half = sb("minus_half", [P, TT], F32)
        rt = sb("rt", [P, 6, TT * E], F32)
        rs = sb("rs", [P, 10, TT], F32)
        onehot = sb("onehot", [P, TT * E], BF16)
        filled = sb("filled", [P, E], F32)
        scatter_to = sb("scatter_to", [P, TT], U32)
        gather_from = sb("gather_from", [P, NB, TT], U32)
        gates = sb("gates", [P, NB, TT], F32)

        free0, free1 = (stack[:, q, :, :].rearrange("p a n -> p (a n)").bitcast(F32) for q in range(2))
        w1_sb = [free0[:, 2048 * c:2048 * (c + 1)].rearrange("p (k f) -> p k f", k=FT) for c in range(2)]
        w2_sb = [free0[:, 4096 + 2048 * c:4096 + 2048 * (c + 1)].rearrange("p (k m) -> p k m", k=FF) for c in range(2)]
        hT = [free1[:, 2048 * c:2048 * (c + 1)].rearrange("p (f s) -> p f s", f=FF) for c in range(2)]
        rows_sb = [free1[:, 4096 + 512 * c:4096 + 512 * (c + 1)].rearrange("p (s m) -> p s m", s=2) for c in range(2)]
        rowsT = [free1[:, 5120 + 512 * c:5120 + 512 * (c + 1)].rearrange("p (m s) -> p m s", m=FT) for c in range(2)]
        eo_sb = [free1[:, 6144 + 512 * c:6144 + 512 * (c + 1)].rearrange("p (s m) -> p s m", s=2) for c in range(2)]
        psH = [psS[:, 0, :], psS[:, 1, :], psS[:, 2, :], psK[:, 0, :]]
        psY = [psK[:, 1, :], psK[:, 2, :]]
        psR = [psO[:, :], psM[:, :]]
        got = probs[:, :, :, :].rearrange("p r h t -> p r (h t)")

        s = {name: sem(name) for name in total}
        x0_in, x_in, w_in, w1_in0, cst_in = (sem(n) for n in ("x0_in", "x_in", "w_in", "w1_in0", "cst_in"))
        zeroed, rows_zero, stack_set0, stack_set1, cst_set, v_ones, misc_set = (
            sem(n) for n in ("zeroed", "rows_zero", "stack_set0", "stack_set1", "cst_set", "v_ones", "misc_set"))
        w1_in, w2_in, rows_in, eo_stored = ([sem(f"{n}_{c}") for c in range(2)]
                                            for n in ("w1_in", "w2_in", "rows_in", "eo_stored"))
        rowsT_done, rowsT_out, hid_done, hid_out, y_done, y_out = (
            sem(n) for n in ("rowsT_done", "rowsT_out", "hid_done", "hid_out", "y_done", "y_out"))
        got_in = [sem(f"got_in_{c}") for c in range(P_RING)]
        got_used, out_stored = sem("got_used"), sem("out_stored")

        def s_unit(b, t, j):
            u = 2 * (t + LEAD) + j
            later = u >= S_UNITS
            return later, u % S_UNITS, 2 * t + j if b.kind else 2 * t + j - 2 * (SLOTS - LEAD)

        def has_s(b, later):
            return b.nxt if later else b.kind

        def stack_of(parity, q_or_k):
            return stack[:, parity, q_or_k, :].rearrange("p (h t) -> p h t", h=H)

        def v_of(parity):
            return V[:, parity, :, :].rearrange("p k (h c) -> p k h c", h=H)

        def evacuated(b, t):
            if t == 2 and b.prev:
                return NG - 1
            return t // 8 - 1 if b.kind and t > 2 and t % 8 == 2 else None

        block = ctx.enter_context(nc.Block())

        @block.sync
        def _(sp):
            sp.dma_start(X[:, 0, :].rearrange("p (t d) -> p t d", t=TT),
                         a["x"][0].rearrange("(t p) d -> p t d", p=P)).then_inc(x0_in, 16)
            sp.dma_start(consts[:, :], a["consts"]).then_inc(cst_in, 16)
            sp.dma_start(wqkv, a["W_qkv_T"].rearrange("(k p) n -> p k n", p=P)).then_inc(w1_in0, 16)
            sp.dma_start(rope_cs, a["rope"].rearrange("s p t -> p s t")).then_inc(w1_in0, 16)
            for j, name in enumerate(("A_bq", "A_bk", "L0_xattn_bq", "L0_xattn_bk", "L0_xattn_bcq", "L0_xattn_bck")):
                src = a["L0_attn_b_qkv"][D * j:D * (j + 1)] if j < 2 else a[name]
                with nc.allow_non_contiguous_dma("a bias per feature, once"):
                    sp.dma_start(bias_qk[:, j, :], src.rearrange("(f p) -> p f", p=P)).then_inc(w1_in0, 16)
            for j, src in enumerate((a["L0_attn_b_qkv"][2 * D:3 * D], a["L0_xattn_bv"], a["L0_xattn_bcv"])):
                sp.dma_start(bias_v[:, j, :], src.rearrange("(o n) -> o n", o=1).to_broadcast([P, D])).then_inc(w1_in0, 16)
            for j, src in enumerate((a["L0_attn_b_out"], a["L0_xattn_bp"])):
                sp.dma_start(bias_o[:, j, :], src.rearrange("(o n) -> o n", o=1).to_broadcast([P, D])).then_inc(w1_in0, 16)
            for n in range(1, NB):
                sp.dma_start(X[:, n, :].rearrange("p (t d) -> p t d", t=TT),
                             a["x"][n].rearrange("(t p) d -> p t d", p=P)).then_inc(x_in, 16)
            sp.dma_start(wo1[:, :, :], a["W_out_T"].rearrange("(k p) n -> p k n", p=P)).then_inc(w_in, 16)
            for j, name in enumerate(("L0_xattn_Wq", "L0_xattn_Wk", "L0_xattn_Wv", "L0_xattn_Wcq")):
                sp.dma_start(wx[:, j, :, :], a[name].rearrange("(k p) n -> p k n", p=P)).then_inc(w_in, 16)
            sp.dma_start(wc[:, 0, :], a["L0_xattn_Wck"]).then_inc(w_in, 16)
            sp.dma_start(wc[:, 1, :], a["L0_xattn_Wcv"]).then_inc(w_in, 16)
            sp.dma_start(wp[:, :, :], a["L0_xattn_Wp"].rearrange("(k p) n -> p k n", p=P)).then_inc(w_in, 16)
            sp.dma_start(wg[:, :, :], a["L0_ffn_Wg"].rearrange("(k p) n -> p k n", p=P)).then_inc(w_in, 16)
            sp.wait_ge(zeroed, 1)
            for j in range(2):
                sp.dma_start(rows_dram.rearrange("(j p r) d -> j p (r d)", j=2, p=P)[j],
                             probs[:, :, :, :].rearrange("p r h t -> p (r h t)")).then_inc(rows_zero, 16)
            for b in stretches(sp, blocks):
                np_ = 1 - b.parity
                jobs = b.jobs()
                for t in range(SLOTS):
                    if t == 0 and b.nx2 == "C":
                        need(sp, s["ctxT_out"], b.at("ctxT_out"))
                        if b.n == 7:
                            sp.wait_ge(s["lo_out"], b.at("lo_out"))
                        sp.dma_start(ctx_sb, a["ctx"][bass.ds(b.batch(2), 1)].rearrange("o (t p) c -> p (o t) c", p=P)
                                     ).then_inc(s["ctx_in"], 16)
                    g = evacuated(b, t)
                    if g is not None:
                        mine = t > 2
                        k = (1 if b.prev else 0) + g + 1 if mine else 1
                        sp.wait_ge(s["av_out"], b.at("av_out", k))
                        if mine and g == 0:
                            need(sp, s["attn_out"], b.at("attn_out", int(b.prev is not None)))
                        for i in range(GH):
                            h = GH * g + i
                            sp.dma_start(packed[HD * (h % 8):HD * (h % 8 + 1), h // 8, :],
                                         U[32 * i:32 * i + HD, g % 2, :]).then_inc(s[f"packed_{g % 2}"], 16)
                            sp.dma_start(sums[8 * h:8 * h + 8, :],
                                         U[32 * i + HD:32 * i + HD + 1, g % 2, :]).then_inc(s[f"packed_{g % 2}"], 16)
                    if t == 5 and b.prev:
                        sp.wait_ge(s["recip_done"], b.at("recip_done", 1))
                        sp.dma_start(recip_dram.rearrange("h (c t) -> (h c) t", c=8), recip[:, :]).then_inc(s["recip_stored"], 16)
                        sp.wait_ge(s["recip_stored"], b.at("recip_stored", 16))
                        for ft in range(FT):
                            sp.dma_start(recipB[:, ft, :],
                                         recip_dram.rearrange("(f h o) t -> f h o t", f=FT, o=1)[ft].to_broadcast([8, HD, T])
                                         ).then_inc(s["recip_in"], 16)
                    if b.nxt and t == 2:
                        sp.wait_ge((stack_set0, stack_set1)[np_], 2)
                        sp.wait_ge(s["parts_stored"], b.at("parts_stored"))
                        for qk, slots in ((0, (0, 0, 1, 1)), (1, (0, 1, 0, 1))):
                            for j, part in enumerate(slots):
                                sp.dma_start(stack_of(np_, qk)[HD * j:HD * (j + 1), :, :],
                                             parts_dram[np_, qk, part].rearrange("(h d) t -> d h t", d=HD)
                                             ).then_inc(s["stack_in"], 16)
                    for slot, name, j in jobs:
                        if name != "proj":
                            continue
                        ft, qk = j // 2, j % 2
                        if b.nx2 == "A" and t == slot:
                            sp.wait_ge(s["rope_in"], b.at("rope_in", j + 1))
                            for o in range(2):
                                sp.dma_start(rope_s[o::2, :], rope_x[1 - o::2, j % 2, :]).then_inc(s["swap_in"], 16)
                        if t == slot + (3 if b.nx2 == "A" else 1):
                            sp.wait_ge(s["lo_out"], b.at("lo_out", j + 1))
                            sp.dma_start(parts_dram[b.parity, qk, :, ft * P:(ft + 1) * P, :].rearrange("s p t -> p s t"),
                                         parts[:, qk, ft, :, :]).then_inc(s["parts_stored"], 16)
                    if b.n == 23 and t == 16:
                        for c in range(2):
                            sp.dma_start(w1_sb[c], a["L0_ffn_w1"][c].rearrange("(k p) f -> p k f", p=P)).then_inc(w1_in[c], 16)
                            sp.dma_start(w2_sb[c], a["L0_ffn_w2"][c].rearrange("(k p) m -> p k m", p=P)).then_inc(w2_in[c], 16)
            sp.wait_ge(s["scattered"], total["scattered"])

            def load_rows(e, c):
                sp.dma_start(rows_sb[c], rows_dram[bass.ds(e * CAP, CAP), :].rearrange("(s p) m -> p s m", p=P)
                             ).then_inc(rows_in[c], 16)

            def store_out(e, c):
                need(sp, y_out, e + 1)
                sp.dma_start(expert_dram[bass.ds(e * CAP, CAP), :].rearrange("(s p) m -> p s m", p=P), eo_sb[c]
                             ).then_inc(eo_stored[c], 16)

            for c in range(2):
                load_rows(c, c)
            with sp.Fori(0, E // 2 - 1) as i:
                for c in range(2):
                    need(sp, hid_done, (i * 2 + c + 1) * 4)
                    sp.dma_start(w1_sb[c], a["L0_ffn_w1"][bass.ds(i * 2 + 2 + c, 1)].rearrange("o (k p) f -> p (o k) f", p=P)
                                 ).then_inc(w1_in[c], 16)
                    need(sp, rowsT_done, i * 2 + c + 1)
                    load_rows(i * 2 + 2 + c, c)
                    need(sp, y_done, i * 2 + c + 1)
                    sp.dma_start(w2_sb[c], a["L0_ffn_w2"][bass.ds(i * 2 + 2 + c, 1)].rearrange("o (k p) m -> p (o k) m", p=P)
                                 ).then_inc(w2_in[c], 16)
                    store_out(i * 2 + c, c)
            for c in range(2):
                store_out(E - 2 + c, c)
            for n in range(NB):
                sp.wait_ge(got_used, n * TT + TT)
                sp.dma_start(a["out"][n].rearrange("(t p) d -> p t d", p=P),
                             X[:, n, :].rearrange("p (t d) -> p t d", t=TT)).then_inc(out_stored, 16)
            sp.wait_ge(out_stored, 16 * NB)

        @block.tensor
        def _(pe):
            pe.wait_ge(cst_set, 7)
            pe.wait_ge(w1_in0, 16 * 13)
            for b in stretches(pe, blocks):
                np_ = 1 - b.parity
                jobs = b.jobs()
                for t in range(SLOTS):
                    av = b.av(t)
                    if av:
                        prev, unit, q0, q1, first = av
                        par = np_ if prev else b.parity
                        g, kt = unit // 8, unit % 8 // 2
                        if first:
                            need(pe, s["exp_done"], b.at("exp_done", 0 if prev else 2 * unit + 4))
                            if not prev and unit == 0:
                                pe.wait_ge(s["v_out"], b.at("v_out"))
                            if kt == 0:
                                need(pe, s["av_out"], b.at("av_out", int(b.prev is not None) + g))
                        for i in range(GH):
                            mm = nc.tensor.matmul(psO[32 * i:32 * i + 32, q0:q1], v_of(par)[:, kt, GH * g + i, :],
                                                  probs[:, (unit + i // 2) % P_RING, i % 2, q0:q1],
                                                  start=kt == 0 and q0 == 0, stop=kt == TT - 1, skip_group_check=True)
                        mm.then_inc(s["av_done"], 1)

                    def maxima(j):
                        later, u, k = s_unit(b, t, j)
                        kind = has_s(b, later)
                        if not kind:
                            return
                        par = np_ if later else b.parity
                        h, qt = u // TT, u % TT
                        if later and u == 0:
                            pe.wait_ge(s["stack_in"], b.at("stack_in", 128))
                        if u == 0 or u >= RING_S:
                            need(pe, s["max_done"], b.at("max_done", k - (RING_S - 1 if u else 0)))
                        n = (qt + 1) * P if kind == "B" else T
                        out = psS[:, u % RING_S, 0:n]
                        mm = nc.tensor.matmul(out, stack_of(par, 0)[0:STACK, h, qt * P:(qt + 1) * P],
                                              stack_of(par, 1)[0:STACK, h, 0:n], start=True, stop=kind != "B",
                                              skip_group_check=kind == "B")
                        if kind == "B":
                            mm = nc.tensor.matmul(psS[:, u % RING_S, n - P:n], ident_bf, mask_q, start=False, stop=True,
                                                  skip_group_check=True)
                        mm.then_inc(s["scores_q"], 1)

                    def exponents(i):
                        if not b.kind:
                            return
                        g, kt, w = t // 8, t % 8 // 2, 2 * t + i
                        if t % 8 == 0 and i == 0:
                            pe.wait_ge(s[f"negmax_in_{g % 2}"], b.at(f"negmax_in_{g % 2}", (0, 32, 32, 64)[g]))
                        if w == 0 or w >= RING_K:
                            need(pe, s["exp_done"], b.at("exp_done", w - RING_K + 1 if w else 0))
                        q0 = q_from(b.kind, kt)
                        h = GH * g + 2 * (t % 2) + i
                        mm = nc.tensor.matmul(psK[:, w % RING_K, q0:T],
                                              stack_of(b.parity, 1)[0:MROWS, h, kt * P:(kt + 1) * P],
                                              stack_of(b.parity, 0)[0:MROWS, h, q0:T],
                                              start=True, stop=b.kind != "B", skip_group_check=b.kind == "B")
                        if b.kind == "B":
                            mm = nc.tensor.matmul(psK[:, w % RING_K, q0:q0 + P], ident_bf, mask_k, start=False,
                                                  stop=True, skip_group_check=True)
                        mm.then_inc(s["scores_k"], 1)

                    maxima(0)
                    exponents(0)
                    maxima(1)
                    exponents(1)
                    for idx, (slot, name, j) in enumerate(jobs):
                        if slot != t:
                            continue
                        freed = b.freed(idx - 1)
                        need(pe, s[freed[0]], b.at(*freed))
                        if name == "xT" or name == "zT":
                            route = name == "zT"
                            ln_no = int(b.nx2 in ("A", "B")) + 1 if route else 1
                            pe.wait_ge(s["ln_out"], b.at("ln_out", ln_no))
                            for tt in range(TT):
                                mm = nc.tensor.transpose(psM[:, tt * P:(tt + 1) * P], xn[:, tt, j * P:(j + 1) * P], ident)
                        elif name == "ctxT":
                            pe.wait_ge(s["ctx_in"], b.at("ctx_in", 16))
                            for tt in range(TT):
                                mm = nc.tensor.transpose(psM[:, tt * P:(tt + 1) * P], ctx_sb[:, tt, :], ident)
                        elif name == "proj":
                            ft, qk = j // 2, j % 2
                            if j == 0:
                                if b.nx2 != "A":
                                    pe.wait_ge(w_in, 16 * 9)
                                if b.nx2 != "C":
                                    pe.wait_ge(s["xT_out"], b.at("xT_out", 2))
                            if b.nx2 == "C" and qk == 1:
                                pe.wait_ge(s["ctxT_out"], b.at("ctxT_out", 1))
                                mm = nc.tensor.matmul(psM[:, :], wc[:, 0, ft * P:(ft + 1) * P], ctxT, start=True, stop=True)
                            else:
                                for k in range(FT):
                                    if b.nx2 == "A":
                                        w = wqkv[:, k, qk * D + ft * P:qk * D + (ft + 1) * P]
                                    else:
                                        w = wx[:, 3 if b.nx2 == "C" else qk, k, ft * P:(ft + 1) * P]
                                    mm = nc.tensor.matmul(psM[:, :], w, xT[:, k, :], start=k == 0, stop=k == FT - 1)
                        elif name == "v":
                            for i in range(2):
                                tt = 2 * j + i
                                out = psM[:, i * D:(i + 1) * D]
                                if b.nxt == "C":
                                    mm = nc.tensor.matmul(out, ctxT[:, tt * P:(tt + 1) * P], wc[:, 1, :], start=True, stop=True)
                                    continue
                                for k in range(FT):
                                    w = wqkv[:, k, 2 * D:3 * D] if b.nxt == "A" else wx[:, 2, k, :]
                                    mm = nc.tensor.matmul(out, xT[:, k, tt * P:(tt + 1) * P], w, start=k == 0, stop=k == FT - 1)
                        elif name == "negmax":
                            k = j if b.kind and j else (4 if b.kind else 1)
                            pe.wait_ge(s["negmax_split"], b.at("negmax_split", k))
                            mrow_ps = psM[:, 0:T // 2].bitcast(F16)
                            for qt in range(TT):
                                mm = nc.tensor.transpose(mrow_ps[0:2 * GH, qt * P:(qt + 1) * P],
                                                         mparts[:, qt, :, :].rearrange("p s h -> p (s h)"), ident_h[:, :])
                        elif name == "out":
                            pe.wait_ge(s["attn_out"], b.at("attn_out", 1))
                            if b.fin == "A":
                                pe.wait_ge(w_in, 16 * 9)
                            w = wo1 if b.fin == "A" else wp
                            for i in range(2):
                                tt = 2 * j + i
                                for k in range(FT):
                                    mm = nc.tensor.matmul(psM[:, i * D:(i + 1) * D], attn[:, k, tt * P:(tt + 1) * P],
                                                          w[:, k, :], start=k == 0, stop=k == FT - 1)
                        elif name == "logits":
                            pe.wait_ge(s["zT_out"], b.at("zT_out", 2))
                            for tt in range(TT):
                                for k in range(FT):
                                    mm = nc.tensor.matmul(psM[:, tt * E:(tt + 1) * E], zT[:, k, tt * P:(tt + 1) * P],
                                                          wg[:, k, :], start=k == 0, stop=k == FT - 1)
                        elif name == "count":
                            pe.wait_ge(s["onehot_out"], b.at("onehot_out", 1))
                            for tt in range(TT + 1):
                                for o in range(min(tt + 1, TT)):
                                    w = tri if o == tt else ones_bf[:, :]
                                    mm = nc.tensor.matmul(psM[:, tt * E:(tt + 1) * E], w, onehot[:, o * E:(o + 1) * E],
                                                          start=o == 0, stop=o == min(tt, TT - 1))
                        mm.then_inc(s["jobs_done"], 1)
            pe.wait_ge(s["route_dve"], total["route_dve"])
            pe.wait_ge(s["av_out"], total["av_out"])

            def transpose_rows(c, loaded, free):
                pe.wait_ge(rows_in[c], loaded)
                need(pe, rowsT_out, free)
                for m in range(FT):
                    for st in range(2):
                        mm = nc.tensor.transpose(psR[c][:, m * CAP + st * P:m * CAP + (st + 1) * P],
                                                 rows_sb[c][:, st, m * P:(m + 1) * P], ident)
                mm.then_inc(rowsT_done, 1)

            def hidden(e, c, loaded):
                pe.wait_ge(w1_in[c], loaded)
                pe.wait_ge(rowsT_out, e + 1)
                for f2 in range(FF // 2):
                    need(pe, hid_out, e * 4 + f2 - 3)
                    for i in range(2):
                        f = 2 * f2 + i
                        for k in range(FT):
                            mm = nc.tensor.matmul(psH[f2][:, i * CAP:(i + 1) * CAP], w1_sb[c][:, k, f * P:(f + 1) * P],
                                                  rowsT[c][:, k, :], start=k == 0, stop=k == FT - 1)
                    mm.then_inc(hid_done, 1)

            def output(e, c, loaded, free):
                pe.wait_ge(w2_in[c], loaded)
                pe.wait_ge(hid_out, e * 4 + 4)
                need(pe, y_out, free)
                for st in range(2):
                    for f in range(FF):
                        mm = nc.tensor.matmul(psY[c][:, st * D:(st + 1) * D], hT[c][:, f, st * P:(st + 1) * P],
                                              w2_sb[c][:, f, :], start=f == 0, stop=f == FF - 1)
                mm.then_inc(y_done, 1)

            transpose_rows(0, 16, 0)
            transpose_rows(1, 16, 0)
            hidden(0, 0, 16)
            hidden(1, 1, 16)
            transpose_rows(0, 32, 1)
            output(0, 0, 16, 0)
            hidden(2, 0, 32)
            transpose_rows(1, 32, 2)
            output(1, 1, 16, 0)
            with pe.Fori(0, E // 2 - 2) as i:
                hidden(i * 2 + 3, 1, i * 16 + 32)
                transpose_rows(0, i * 16 + 48, i * 2 + 3)
                output(i * 2 + 2, 0, i * 16 + 32, i * 2 + 1)
                hidden(i * 2 + 4, 0, i * 16 + 48)
                transpose_rows(1, i * 16 + 48, i * 2 + 4)
                output(i * 2 + 3, 1, i * 16 + 32, i * 2 + 2)
            hidden(E - 1, 1, 16 * (E // 2))
            output(E - 2, 0, 16 * (E // 2), E - 3)
            output(E - 1, 1, 16 * (E // 2), E - 2)

        @block.scalar
        def _(act):
            act.wait_ge(rows_zero, 32)
            act.wait_ge(w1_in0, 16 * 13)
            for b in stretches(act, blocks):
                np_ = 1 - b.parity
                jobs = b.jobs()
                for t in range(SLOTS):
                    g = evacuated(b, t)
                    if g is not None:
                        act.wait_ge(s["av_done"], b.at("av_done", b.av_count(t)))
                        if t == 2:
                            used = b.at("packed_1")
                        elif g % 2:
                            used = b.at("packed_1", 128 if b.prev else 0)
                        else:
                            used = b.at("packed_0", 64 * g)
                        need(act, s[f"packed_{g % 2}"], used)
                        nc.scalar.copy(U[:, g % 2, :], psO[:, :]).then_inc(s["av_out"], 1)
                    if b.kind:
                        q0 = q_from(b.kind, t % 8 // 2)
                        if t % 2 == 0:
                            need(act, s["av_done"], b.at("av_done", b.av_count(t)))
                        for i in range(2):
                            act.wait_ge(s["scores_k"], b.at("scores_k", 2 * t + i + 1))
                            nc.scalar.activation(probs[:, t % P_RING, i, q0:T], psK[:, (2 * t + i) % RING_K, q0:T], ACT.Exp,
                                                 scale=SM_SCALE).then_inc(s["exp_done"], 1)
                    for idx, (slot, name, j) in enumerate(jobs):
                        if slot == t and name in ("xT", "zT", "ctxT", "proj", "negmax"):
                            act.wait_ge(s["jobs_done"], b.at("jobs_done", idx + 1))
                            if name == "xT":
                                need(act, s["v_out"], b.at("v_out"))
                                nc.scalar.copy(xT[:, j, :], psM[:, :]).then_inc(s["xT_out"], 1)
                            elif name == "zT":
                                nc.scalar.copy(zT[:, j, :], psM[:, :]).then_inc(s["zT_out"], 1)
                            elif name == "ctxT":
                                nc.scalar.copy(ctxT, psM[:, :]).then_inc(s["ctxT_out"], 1)
                            elif name == "proj":
                                ft, qk = j // 2, j % 2
                                bias = bias_qk[:, 2 * "ABC".index(b.nx2) + qk, ft:ft + 1]
                                if b.nx2 == "A":
                                    need(act, s["rope_out"], b.at("rope_out", j - 1))
                                    nc.scalar.activation(rope_x[:, j % 2, :], psM[:, :], ACT.Identity, bias=bias
                                                         ).then_inc(s["rope_in"], 1)
                                else:
                                    if j == 0:
                                        need(act, s["parts_stored"], b.at("parts_stored"))
                                    nc.scalar.activation(parts[:, qk, ft, 0, :], psM[:, :], ACT.Identity, bias=bias
                                                         ).then_inc(s["hi_out"], 1)
                            else:
                                k = j if b.kind and j else (4 if b.kind else 1)
                                g = j
                                o = (g + 1) % 2
                                if b.kind:
                                    before = {1: (0, 0), 2: (1, 32), 3: (0, 32), 0: (1, 64)}[g]
                                    need(act, s[f"negmax_in_{before[0]}"], b.at(f"negmax_in_{before[0]}", before[1]))
                                nc.scalar.copy(mrows[:, :], psM[0:2 * GH, 0:T // 2].bitcast(F16)
                                               ).then_inc(s["negmax_rows"], 1)
                                act.wait_ge(s["negmax_rows"], b.at("negmax_rows", k))
                                par = b.parity if j else np_
                                for part in range(2):
                                    act.dma_start(stack_of(par, 0)[STACK + part:STACK + part + 1, GH * g:GH * (g + 1), :],
                                                  mrows[GH * part:GH * (part + 1), :]).then_inc(s[f"negmax_in_{g % 2}"], 16)
                        if name == "proj" and b.nx2 == "A" and t == slot + 2:
                            act.wait_ge(s["rope_out"], b.at("rope_out", j + 1))
                            if j == 0:
                                need(act, s["parts_stored"], b.at("parts_stored"))
                            nc.scalar.copy(parts[:, j % 2, j // 2, 0, :], rope_s).then_inc(s["hi_out"], 1)
                        if name == "logits" and slot == t:
                            act.wait_ge(s["route_dve"], b.at("route_dve", 2))
                            nc.scalar.activation(rt[:, 1, :], rt[:, 0, :], ACT.Exp).then_inc(s["route_exp"], 1)
            def out_rows(e, c):
                act.wait_ge(rowsT_done, e + 1)
                need(act, hid_done, e * 4 - 4)
                nc.scalar.copy(rowsT[c].rearrange("p m s -> p (m s)"), psR[c]).then_inc(rowsT_out, 1)

            def out_y(e, c, stored):
                act.wait_ge(y_done, e + 1)
                need(act, eo_stored[c], stored)
                nc.scalar.copy(eo_sb[c].rearrange("p s m -> p (s m)"), psY[c]).then_inc(y_out, 1)

            out_rows(0, 0)
            out_rows(1, 1)
            out_rows(2, 0)
            out_y(0, 0, 0)
            out_rows(3, 1)
            out_y(1, 1, 0)
            with act.Fori(0, E // 2 - 2) as i:
                out_rows(i * 2 + 4, 0)
                out_y(i * 2 + 2, 0, i * 16 + 16)
                out_rows(i * 2 + 5, 1)
                out_y(i * 2 + 3, 1, i * 16 + 16)
            out_y(E - 2, 0, 16 * (E // 2 - 1))
            out_y(E - 1, 1, 16 * (E // 2 - 1))

        @block.vector
        def _(dve):
            nc.vector.memset(probs[:, :, :, :], 0.0).then_inc(zeroed, 1)
            nc.vector.memset(minus_half[:, :], -0.5).then_inc(misc_set, 1)
            nc.vector.memset(filled[:, :], 0.0).then_inc(misc_set, 1)
            dve.wait_ge(cst_in, 16)
            nc.vector.tensor_copy(ident_bf, ident).then_inc(cst_set, 1)
            nc.vector.tensor_copy(ident_h[:, :], ident).then_inc(cst_set, 1)
            for j, dst in ((1, mask_q), (2, mask_k), (3, tri)):
                nc.vector.tensor_copy(dst, consts[:, j * P:(j + 1) * P]).then_inc(cst_set, 1)
            nc.vector.memset(ones_bf[:, :], 1.0).then_inc(cst_set, 1)
            nc.vector.memset(V[:, :, :, :].rearrange("p a k (h c) -> p (a k) h c", h=H)[:, :, :, HD:2 * HD], 1.0
                             ).then_inc(cst_set, 1)
            dve.wait_ge(cst_set, 7)
            nc.vector.memset(stack[64:96, 0, :, :], 0.0).then_inc(stack_set0, 1)
            nc.vector.memset(stack[96:98, 0, 1, :], MSCALE).then_inc(stack_set0, 1)
            dve.wait_ge(w1_in0, 16 * 13)

            def layernorm(b, batch, t, first, k):
                if t in (first, first + 1):
                    for tt in range(2 * (t - first), 2 * (t - first) + 2):
                        o = nc.vector.bn_stats(stats[:, tt, :], X[:, bass.ds(batch, 1), tt * D:(tt + 1) * D].rearrange("p o d -> p (o d)"))
                if t == first + 1:
                    o.then_inc(s["bn_done"], 1)
                    need(dve, s["bn_done"], b.at("bn_done", k))
                    mean_e, ss_e, mean_o, ss_o = (stats[:, :, c] for c in (1, 2, 4, 5))
                    nc.vector.tensor_tensor(lnt[:, 0, :], mean_e, mean_o, ALU.add)
                    nc.vector.tensor_tensor(lnt[:, 1, :], mean_e, mean_o, ALU.subtract)
                    nc.vector.tensor_tensor(lnt[:, 2, :], ss_e, ss_o, ALU.add).then_inc(s["ln_step"], 1)
                    dve.wait_ge(s["ln_step"], b.at("ln_step", 3 * k - 2))
                    nc.vector.tensor_tensor(lnt[:, 3, :], lnt[:, 1, :], lnt[:, 1, :], ALU.mult).then_inc(s["ln_step"], 1)
                    nc.vector.tensor_scalar(lnt[:, 5, :], lnt[:, 0, :], 0.5, None, ALU.mult)
                    dve.wait_ge(s["ln_step"], b.at("ln_step", 3 * k - 1))
                    nc.vector.scalar_tensor_tensor(out=lnt[:, 4, :], in0=lnt[:, 3, :], scalar=D / 4.0, in1=lnt[:, 2, :],
                                                   op0=ALU.mult, op1=ALU.add).then_inc(s["ln_step"], 1)
                    dve.wait_ge(s["ln_step"], b.at("ln_step", 3 * k))
                    nc.vector.tensor_scalar(lnt[:, 6, :], lnt[:, 4, :], 1.0 / D, LN_EPS, ALU.mult, ALU.add
                                            ).then_inc(s["ln_var"], 1)
                if t in (first + 2, first + 3):
                    dve.wait_ge(s["ln_rstd"], b.at("ln_rstd", k))
                    need(dve, s["scattered"], b.at("scattered"))
                    need(dve, s["xT_out"], b.at("xT_out", 2 * (k - 1)))
                    for tt in range(2 * (t - first) - 4, 2 * (t - first) - 2):
                        o = nc.vector.tensor_scalar(xn[:, tt, :], X[:, bass.ds(batch, 1), tt * D:(tt + 1) * D].rearrange("p o d -> p (o d)"),
                                                    lnt[:, 5, tt:tt + 1], rstd[:, tt:tt + 1], ALU.subtract, ALU.mult)
                if t == first + 3:
                    o.then_inc(s["ln_out"], 1)

            for b in stretches(dve, blocks):
                np_ = 1 - b.parity
                jobs = b.jobs()
                ln = int(b.nx2 in ("A", "B"))
                for t in range(SLOTS):
                    if b.nx2 == "B" and t == 3:
                        need(dve, s["x_out"], b.at("x_out"))
                    if b.route and t == 12:
                        need(dve, s["x_out"], b.at("x_out", 2 if b.fin else 0))
                    for j in range(2):
                        later, u, k = s_unit(b, t, j)
                        kind = has_s(b, later)
                        if not kind:
                            continue
                        g = u // (S_UNITS // NG)
                        n = (u % TT + 1) * P if kind == "B" else T
                        if u % (S_UNITS // NG) == 0:
                            need(dve, s["negmax_split"], b.at("negmax_split", t // 8 if b.kind else 0))
                        dve.wait_ge(s["scores_q"], b.at("scores_q", k + 1))
                        nc.vector.tensor_reduce(negmax[:, g % 2, u % 16:u % 16 + 1], psS[:, u % RING_S, 0:n], AX_X, ALU.max,
                                                negate=True).then_inc(s["max_done"], 1)
                    if (b.kind and t in (4, 12, 20)) or (b.nxt and t == 28):
                        g = (t // 8 + 1) % NG
                        k = t // 8 + 1 if b.kind else 1
                        done = 2 * (t - 4) + 8 if b.kind else 16
                        view = negmax[:, g % 2, :].rearrange("p (h q) -> p q h", h=GH)
                        dve.wait_ge(s["max_done"], b.at("max_done", done))
                        need(dve, s["negmax_rows"], b.at("negmax_rows", k - 1))
                        nc.vector.tensor_scalar(mparts[:, :, 0, :], view, 1.0 / MSCALE, None, ALU.mult
                                                ).then_inc(s["negmax_hi"], 1)
                        dve.wait_ge(s["negmax_hi"], b.at("negmax_hi", k))
                        nc.vector.scalar_tensor_tensor(out=mparts[:, :, 1, :], in0=view, scalar=1.0 / MSCALE,
                                                       in1=mparts[:, :, 0, :], op0=ALU.mult, op1=ALU.subtract
                                                       ).then_inc(s["negmax_split"], 1)
                    if t == 5 and b.prev:
                        dve.wait_ge(s["packed_0"], b.at("packed_0"))
                        dve.wait_ge(s["packed_1"], b.at("packed_1", 128))
                        need(dve, s["recip_stored"], b.at("recip_stored"))
                        nc.vector.reciprocal(recip[:, :], sums[:, :]).then_inc(s["recip_done"], 1)
                    if ln and t in range(3, 7):
                        if b.nx2 == "A" and t == 3:
                            dve.wait_ge(*((x0_in, 16) if b.n == -2 else (x_in, 16 * (NB - 1))))
                        layernorm(b, b.batch(2), t, 3, 1)
                    if b.n == -2 and t == 7:
                        nc.vector.memset(stack[64:96, 1, :, :], 0.0).then_inc(stack_set1, 1)
                        nc.vector.memset(stack[96:98, 1, 1, :], MSCALE).then_inc(stack_set1, 1)
                    for idx, (slot, name, j) in enumerate(jobs):
                        if slot != t:
                            continue
                        done = b.at("jobs_done", idx + 1)
                        if name == "proj" and b.nx2 != "A":
                            ft, qk = j // 2, j % 2
                            dve.wait_ge(s["hi_out"], b.at("hi_out", j + 1))
                            nc.vector.scalar_tensor_tensor(
                                out=parts[:, qk, ft, 1, :], in0=psM[:, :],
                                scalar=bias_qk[:, 2 * "ABC".index(b.nx2) + qk, ft:ft + 1], in1=parts[:, qk, ft, 0, :],
                                op0=ALU.add, op1=ALU.subtract).then_inc(s["lo_out"], 1)
                        elif name == "v":
                            dve.wait_ge(s["jobs_done"], done)
                            for i in range(2):
                                tt = 2 * j + i
                                nc.vector.tensor_tensor(
                                    v_of(np_)[:, tt, :, 0:HD],
                                    psM[:, i * D:(i + 1) * D].rearrange("p (h c) -> p h c", h=H),
                                    bias_v[:, "ABC".index(b.nxt), :].rearrange("p (h c) -> p h c", h=H), ALU.add
                                ).then_inc(s["v_out"], 1)
                        elif name == "out":
                            dve.wait_ge(s["jobs_done"], done)
                            need(dve, s["x_bias"], b.at("x_bias", 0))
                            xs = X[:, bass.ds(b.batch(-1), 1), 2 * j * D:2 * (j + 1) * D].rearrange("p o d -> p (o d)")
                            nc.vector.tensor_tensor(xs, psM[:, :], xs, ALU.add).then_inc(s["x_out"], 1)
                    for slot, name, j in jobs:
                        if name == "proj" and b.nx2 == "A" and t == slot + 2:
                            dve.wait_ge(s["rope_sin"], b.at("rope_sin", j + 1))
                            nc.vector.tensor_tensor(rope_s, rope_s, rope_c, ALU.add).then_inc(s["rope_out"], 1)
                    if b.route:
                        layernorm(b, b.batch(-1) if b.kind is None else b.batch(-2), t, 12, ln + 1)
                        step = [2 * 0]

                        def chain(ins, k):
                            ins.then_inc(s["route_dve"], 1)
                            dve.wait_ge(s["route_dve"], b.at("route_dve", k))

                        def wide(j):
                            return rt[:, j, :].rearrange("p (t e) -> p t e", e=E)

                        def over(j):
                            return rs[:, j, :, None].to_broadcast([P, TT, E])

                        gb = b.batch(-1) if b.kind is None else b.batch(-2)
                        idx = [i for i, job in enumerate(jobs) if job[1] == "logits"][0]
                        if t == 22:
                            dve.wait_ge(s["jobs_done"], b.at("jobs_done", idx + 1))
                            logits = psM[:, 0:TT * E].rearrange("p (t e) -> p t e", e=E)
                            chain(nc.vector.tensor_reduce(rs[:, 0, :], logits, AX_X, ALU.max), 1)
                            chain(nc.vector.tensor_tensor(wide(0), logits, over(0), ALU.subtract), 2)
                        if t == 23:
                            dve.wait_ge(s["route_exp"], b.at("route_exp", 1))
                            chain(nc.vector.tensor_reduce(rs[:, 1, :], wide(1), AX_X, ALU.add), 3)
                            chain(nc.vector.reciprocal(rs[:, 2, :], rs[:, 1, :]), 4)
                            chain(nc.vector.tensor_tensor(wide(2), wide(1), over(2), ALU.mult), 5)
                            chain(nc.vector.tensor_reduce(rs[:, 3, :], wide(2), AX_X, ALU.max), 6)
                            chain(nc.vector.tensor_tensor(wide(3), wide(2), over(3), ALU.is_ge), 7)
                            chain(nc.vector.scalar_tensor_tensor(out=rt[:, 4, :], in0=rt[:, 3, :], scalar=-1000.0,
                                                                 in1=expert_no, op0=ALU.mult, op1=ALU.add), 8)
                            chain(nc.vector.tensor_reduce(rs[:, 4, :], wide(4), AX_X, ALU.min), 9)
                            chain(nc.vector.tensor_tensor(wide(5), wide(4), over(4), ALU.is_equal), 10)
                            nc.vector.tensor_copy(onehot[:, :], rt[:, 5, :]).then_inc(s["onehot_out"], 1)
                        if t == 25:
                            dve.wait_ge(s["jobs_done"], b.at("jobs_done", idx + 2))
                            before = psM[:, 0:TT * E].rearrange("p (t e) -> p t e", e=E)
                            chain(nc.vector.tensor_tensor(wide(0), before, filled[:, None, :].to_broadcast([P, TT, E]), ALU.add), 11)
                            chain(nc.vector.tensor_tensor(filled[:, :], psM[:, TT * E:(TT + 1) * E], filled[:, :], ALU.add), 12)
                            chain(nc.vector.tensor_tensor(wide(1), wide(0), wide(5), ALU.mult), 13)
                            chain(nc.vector.tensor_reduce(rs[:, 5, :], wide(1), AX_X, ALU.add), 14)
                            chain(nc.vector.tensor_scalar(rs[:, 6, :], rs[:, 5, :], float(CAP), None, ALU.is_lt), 15)
                            chain(nc.vector.tensor_tensor(gates[:, bass.ds(gb, 1), :].rearrange("p o t -> p (o t)"),
                                                          rs[:, 3, :], rs[:, 6, :], ALU.mult), 16)
                            chain(nc.vector.tensor_scalar(rs[:, 7, :], rs[:, 5, :], float(CAP - 1), 1000.0 * CAP,
                                                          ALU.min, ALU.add), 17)
                            chain(nc.vector.scalar_tensor_tensor(out=rs[:, 8, :], in0=rs[:, 4, :], scalar=float(CAP),
                                                                 in1=rs[:, 7, :], op0=ALU.mult, op1=ALU.add), 18)
                            chain(nc.vector.tensor_copy(gather_from[:, bass.ds(gb, 1), :].rearrange("p o t -> p (o t)"),
                                                        rs[:, 8, :]), 19)
                            chain(nc.vector.tensor_scalar(rs[:, 9, :], rs[:, 6, :], -65536.0, 65536.0, ALU.mult, ALU.add), 20)
                            nc.vector.tensor_tensor(scatter_to[:, :], rs[:, 8, :], rs[:, 9, :], ALU.add
                                                    ).then_inc(s["index_out"], 1)

            def relu(e, c):
                for f2 in range(FF // 2):
                    dve.wait_ge(hid_done, e * 4 + f2 + 1)
                    if f2 == 0:
                        need(dve, y_done, e - 1)
                    nc.vector.tensor_scalar(hT[c][:, 2 * f2:2 * f2 + 2, :].rearrange("p f s -> p (f s)"), psH[f2],
                                            0.0, None, ALU.max).then_inc(hid_out, 1)

            relu(0, 0)
            relu(1, 1)
            with dve.Fori(0, E // 2 - 1) as i:
                for c in range(2):
                    relu(i * 2 + 2 + c, c)
            for n in range(NB):
                dve.wait_ge(got_in[n % P_RING], 16 * TT * (n // P_RING + 1))
                for tt in range(TT):
                    xs = X[:, n, tt * D:(tt + 1) * D]
                    nc.vector.scalar_tensor_tensor(out=xs, in0=got[:, n % P_RING, tt * D:(tt + 1) * D],
                                                   scalar=gates[:, n, tt:tt + 1], in1=xs, op0=ALU.mult, op1=ALU.add
                                                   ).then_inc(got_used, 1)

        @block.gpsimd
        def _(pool):
            pool.wait_ge(misc_set, 2)
            pool.wait_ge(w1_in0, 16 * 13)

            def rstd_of(b, k):
                need(pool, s["ln_var"], b.at("ln_var", k))
                nc.gpsimd.tensor_tensor(rstd[:, :], lnt[:, 6, :], minus_half[:, :], ALU.pow).then_inc(s["ln_rstd"], 1)

            for b in stretches(pool, blocks):
                jobs = b.jobs()
                ln = int(b.nx2 in ("A", "B"))
                for t in range(SLOTS):
                    if ln and t == 4:
                        rstd_of(b, 1)
                    if ln and t == 7:
                        need(pool, s["ln_out"], b.at("ln_out", 1))
                        xs = X[:, bass.ds(b.batch(2), 1), :].rearrange("p o (t d) -> p (o t) d", t=TT)
                        bo = bias_o[:, 0 if b.nx2 == "A" else 1, None, :].to_broadcast([P, TT, D])
                        nc.gpsimd.tensor_tensor(xs, xs, bo, ALU.add).then_inc(s["x_bias"], 1)
                    if t == 6 and b.prev:
                        pool.wait_ge(s["recip_in"], b.at("recip_in", 16 * FT))
                        need(pool, s["x_out"], b.at("x_out"))
                        pool.wait_ge(s["packed_0"], b.at("packed_0"))
                        pool.wait_ge(s["packed_1"], b.at("packed_1", 128))
                        if b.prev == "C":
                            nc.gpsimd.tensor_tensor(packed[:, :, :], packed[:, :, :], recipB[:, :, :], ALU.mult
                                                    ).then_inc(s["attn_mul"], 1)
                            pool.wait_ge(s["attn_mul"], b.at("attn_mul", 1))
                            nc.gpsimd.tensor_tensor(attn[:, :, :], attn_b, packed[:, :, :], ALU.add
                                                    ).then_inc(s["attn_out"], 1)
                        else:
                            dst = attn[:, :, :] if b.prev == "A" else attn_b
                            nc.gpsimd.tensor_tensor(dst, packed[:, :, :], recipB[:, :, :], ALU.mult
                                                    ).then_inc(s["attn_out"], 1)
                    for slot, name, j in jobs:
                        if name == "proj" and b.nx2 == "A":
                            if t == slot + 1:
                                pool.wait_ge(s["rope_in"], b.at("rope_in", j + 1))
                                need(pool, s["rope_out"], b.at("rope_out", j))
                                nc.gpsimd.tensor_tensor(rope_c, rope_x[:, j % 2, :], rope_cs[:, 0, :], ALU.mult
                                                        ).then_inc(s["rope_cos"], 1)
                                pool.wait_ge(s["rope_cos"], b.at("rope_cos", j + 1))
                                pool.wait_ge(s["swap_in"], b.at("swap_in", 32 * (j + 1)))
                                nc.gpsimd.tensor_tensor(rope_s, rope_s, rope_cs[:, 1, :], ALU.mult
                                                        ).then_inc(s["rope_sin"], 1)
                            if t == slot + 2:
                                pool.wait_ge(s["hi_out"], b.at("hi_out", j + 1))
                                nc.gpsimd.tensor_tensor(parts[:, j % 2, j // 2, 1, :], rope_s, parts[:, j % 2, j // 2, 0, :],
                                                        ALU.subtract).then_inc(s["lo_out"], 1)
                    if b.route and t == 13:
                        rstd_of(b, ln + 1)
                    if b.route and t == 28:
                        pool.wait_ge(rows_zero, 32)
                        pool.wait_ge(s["index_out"], b.at("index_out", 1))
                        for tt in range(TT):
                            nc.gpsimd.indirect_dma_start(
                                out=rows_dram[:, :], out_offset=bass.IndirectOffsetOnAxis(ap=scatter_to[:, tt:tt + 1], axis=0),
                                in_=xn[:, tt, :], in_offset=None, bounds_check=E * CAP - 1, oob_is_err=False
                            ).then_inc(s["scattered"], 16)
            for c in range(2):
                pool.wait_ge(eo_stored[c], 16 * (E // 2))
            for n in range(NB):
                if n >= P_RING:
                    pool.wait_ge(got_used, TT * (n - P_RING + 1))
                for tt in range(TT):
                    nc.gpsimd.indirect_dma_start(
                        out=got[:, n % P_RING, tt * D:(tt + 1) * D], out_offset=None, in_=expert_dram[:, :],
                        in_offset=bass.IndirectOffsetOnAxis(ap=gather_from[:, n, tt:tt + 1], axis=0)
                    ).then_inc(got_in[n % P_RING], 16)


def _constants():
    i = np.arange(P)
    ident = np.eye(P, dtype=np.float32)
    mask_q = np.where(i[None, :] > i[:, None], np.float32(NEG), np.float32(0))
    mask_k = np.ascontiguousarray(mask_q.T)
    before = (i[:, None] < i[None, :]).astype(np.float32)
    number = np.tile(np.arange(E, dtype=np.float32), (P, TT))
    consts = np.concatenate([ident, mask_q, mask_k, before, number], axis=1)
    half = HD // 2
    theta = (np.float32(1.0) / np.float32(10000.0) ** (np.arange(half, dtype=np.float32) / np.float32(half)))
    freqs = np.arange(T, dtype=np.float32)[:, None] * theta[None, :].astype(np.float32)
    col = (i % HD) // 2
    rope = np.stack([np.cos(freqs)[:, col].T, np.sin(freqs)[:, col].T * np.where(i % 2, 1, -1)[:, None]]).astype(np.float32)
    return consts, np.ascontiguousarray(rope)


def kernel(**inputs):
    import numpy as _np
    import concourse.bacc as _bacc
    from concourse import mybir as _mybir
    from concourse.bass_utils import run_bass_kernel_spmd as _run

    nc = _bacc.Bacc("TRN2", target_bir_lowering=False, num_devices=1)
    consts, rope = _constants()
    arrays = {"consts": consts, "rope": rope}
    for name, v in inputs.items():
        if name == "L0_attn_W_qkv":
            arrays["W_qkv_T"] = _np.ascontiguousarray(_np.asarray(v).T)
        elif name == "L0_attn_W_out":
            arrays["W_out_T"] = _np.ascontiguousarray(_np.asarray(v).T)
        else:
            arrays["ctx" if name == "ctx_512" else name] = _np.ascontiguousarray(v)
    aps, feed = {}, {}
    for name, v in arrays.items():
        feed[f"in_{name}_dram"] = v
        aps[name] = nc.dram_tensor(f"in_{name}_dram", v.shape, _mybir.dt.from_np(v.dtype), kind="ExternalInput").ap()
    aps["out"] = nc.dram_tensor("out_0_dram", (NB, T, D), _mybir.dt.from_np(_np.dtype("float32")), kind="ExternalOutput").ap()
    build(nc, aps)
    r = _run(nc, [feed], core_ids=[0])
    return r.results[0]["out_0_dram"]
```

```python
from contextlib import ExitStack

import numpy as np

import concourse.bass as bass
from concourse import mybir

F32 = mybir.dt.float32
F16 = mybir.dt.float16
BF16 = mybir.dt.bfloat16
U32 = mybir.dt.uint32
ALU = mybir.AluOpType
ACT = mybir.ActivationFunctionType
AX_X = mybir.AxisListType.X

P = 128
NB, T, D, DC = 8, 512, 256, 128
H, HD = 16, 16
TT = T // P
FT = D // P
GH = 4
NG = H // GH
SLOTS = NG * TT * 2
S_UNITS = H * TT
RING_S = RING_K = 3
LEAD = 12
E, CAP, F = 16, NB * T // 16, 1024
FF = F // P
STACK = 96
MROWS = STACK + 2
WSCALE = 16.0
MSCALE = 1024.0
SM_SCALE = HD ** -0.5
P_RING = 4
NO_ROW = 65536
NEG = -1e30
LN_EPS = 1e-5


def q_from(kind, kt):
    return kt * P if kind == "B" else 0


class Body:

    def __init__(self, kind, prev, nxt, nx2, n, dn=0, route=False):
        self.kind, self.prev, self.nxt, self.nx2, self.route = kind, prev, nxt, nx2, route
        self.parity = n % 2
        self.fin = prev if prev in ("A", "C") else None
        self.attn_slot = 16 if kind else 7
        self.ln_slot, self.norm_slot = (7, 9) if nx2 == "B" else (2, 6)
        self.n, self.dn = n, dn
        self.base, self.stride, self.i = {}, {}, 0

    def at(self, sem, k=0):
        return self.base[sem] + self.i * self.stride.get(sem, 0) + k if self.stride.get(sem, 0) \
            else self.base[sem] + k

    def batch(self, ahead=0):
        n = self.n + ahead
        if n < NB:
            return n + self.dn * self.i if self.dn else n
        b = (n - NB) // 2
        return b + (self.dn // 2) * self.i if self.dn else b

    def counts(self):
        c, run, prep, had = {}, self.kind is not None, self.nxt, self.prev is not None
        c["scores_q"] = c["max_done"] = (2 * (SLOTS - LEAD) if run else 0) + (2 * LEAD if prep else 0)
        groups = (3 if run else 0) + (1 if prep else 0)
        c["negmax_hi"] = c["negmax_split"] = c["negmax_rows"] = groups
        c["negmax_in_0"] = 32 * ((1 if run else 0) + (1 if prep else 0))
        c["negmax_in_1"] = 64 if run else 0
        c["scores_k"] = c["exp_done"] = 2 * SLOTS if run else 0
        c["av_done"] = self.av_count(SLOTS - 1)
        c["av_out"] = (3 if run else 0) + (1 if had else 0)
        c["packed_0"] = 128 * 2 if run else 0
        c["packed_1"] = (128 if run else 0) + (128 if had else 0)
        c["recip_done"] = c["attn_mul"] = int(had)
        c["attn_hi"] = c["attn_out"] = int(self.fin is not None)
        c["recip_stored"] = 16 * int(had)
        c["recip_in"] = 16 * FT * int(had)
        c["attn_sum"] = int(self.prev == "C")
        c["jobs_done"] = len(self.jobs())
        ln = int(self.nx2 in ("A", "B"))
        rt = int(self.route)
        c["bn_done"] = c["ln_var"] = c["ln_rstd"] = c["ln_out"] = ln + rt
        c["ln_step"] = 3 * (ln + rt)
        c["x_bias"] = ln
        c["xT_out"] = c["xT_lo"] = 2 * ln
        c["ctx_in"] = 16 * int(self.nx2 == "C")
        c["ctxT_out"] = c["ctxT_lo"] = int(self.nx2 == "C")
        rope = 4 * int(self.nx2 == "A")
        for s in ("rope_in", "rope_cos", "rope_sin", "rope_out"):
            c[s] = rope
        c["swap_in_0"] = c["swap_in_1"] = 16 * rope
        c["hi_out"] = c["lo_out"] = 4 if self.nx2 else 0
        c["parts_stored"] = 64 if self.nx2 else 0
        c["stack_in"] = 128 if prep else 0
        c["v_out"] = 4 if prep else 0
        c["x_out"] = 2 if self.fin else 0
        c["zT_out"] = 2 * rt
        c["route_dve"] = ROUTE_STEPS * rt
        c["route_exp"] = c["onehot_out"] = c["index_out"] = c["gate_set"] = rt
        c["scattered"] = c["back_scattered"] = 16 * TT * rt
        c["back_set"] = rt
        c["x_stored"] = 16 * rt
        return c

    def av(self, t):
        kind = self.kind if t >= 3 else self.prev
        if not kind:
            return None
        half = (t + 1) % 2
        unit = (t - 3 - half) % SLOTS
        first = q_from(kind, unit % 8 // 2)
        q0, q1 = max(first, half * T // 2), (half + 1) * T // 2
        return (t < 3, unit, q0, q1, q0 == first) if q0 < q1 else None

    def av_count(self, t):
        return sum(self.av(i) is not None for i in range(t + 1))

    def jobs(self):
        out = []
        if self.nxt:
            out += [(2, "v", 0), (4, "v", 1), (29, "negmax", 0)]
        if self.kind:
            out += [(5, "negmax", 1), (13, "negmax", 2), (21, "negmax", 3)]
        if self.nx2 == "A":
            out += [(6, "xT", 0), (7, "xT", 1)]
            out += [({-2: 9, -1: 17}[self.n] + 2 * j if self.n < 0 else (8, 12, 20, 24)[j], "proj", j) for j in range(4)]
        if self.nx2 == "B":
            out += [(11, "xT", 0), (12, "xT", 1), (14, "proj", 0), (16, "proj", 1), (18, "proj", 2), (20, "proj", 3)]
        if self.nx2 == "C":
            out += [(7, "ctxT", 0), (9, "proj", 0), (11, "proj", 1), (14, "proj", 2), (17, "proj", 3)]
        if self.fin:
            out += [(23 + (self.nx2 == "B"), "out", 0), (27, "out", 1)] if self.kind else [(8, "out", 0), (9, "out", 1)]
        if self.route:
            out += [(19, "zT", 0), (20, "zT", 1), (22, "logits", 0), (25, "count", 0)]
        return sorted(out, key=lambda j: j[0])

    def freed(self, idx):
        if idx < 0:
            return ("rope_in" if self.n < 0 else "negmax_rows" if self.kind else "route_dve"), 0
        _, name, j = self.jobs()[idx]
        if name == "proj":
            return ("rope_in" if self.nx2 == "A" else "lo_out"), j + 1
        if name == "negmax":
            return "negmax_rows", (j if j else 4) if self.kind else 1
        return {"xT": ("xT_lo", j + 1), "ctxT": ("ctxT_lo", 1), "zT": ("zT_out", j + 1), "v": ("v_out", 2 * j + 2),
                "out": ("x_out", j + 1), "logits": ("route_dve", 2),
                "count": ("route_dve", 12)}[name]


ROUTE_STEPS = 18


def plan():
    blocks = [
        (1, [Body(None, None, None, "A", -2)]),
        (1, [Body(None, None, "A", "A", -1)]),
        (1, [Body("A", None, "A", "A", 0)]),
        (2, [Body("A", "A", "A", "A", 1, 2), Body("A", "A", "A", "A", 2, 2)]),
        (1, [Body("A", "A", "A", "A", 5)]),
        (1, [Body("A", "A", "A", "B", 6)]),
        (1, [Body("A", "A", "B", "C", 7)]),
        (1, [Body("B", "A", "C", "B", 8)]),
        (1, [Body("C", "B", "B", "C", 9)]),
        (6, [Body("B", "C", "C", "B", 10, 2), Body("C", "B", "B", "C", 11, 2, route=True)]),
        (1, [Body("B", "C", "C", None, 22)]),
        (1, [Body("C", "B", None, None, 23, route=True)]),
        (1, [Body(None, "C", None, None, 24, route=True)]),
    ]
    total = {}
    for times, bodies in blocks:
        cycle = {}
        for b in bodies:
            for s, k in b.counts().items():
                b.base[s] = total.get(s, 0) + cycle.get(s, 0)
                cycle[s] = cycle.get(s, 0) + k
        for b in bodies:
            b.stride = dict(cycle) if times > 1 else {}
        for s, k in cycle.items():
            total[s] = total.get(s, 0) + k * times
    return blocks, total


def stretches(eng, blocks):
    for times, bodies in blocks:
        if times == 1:
            for b in bodies:
                yield b
        else:
            with eng.Fori(0, times) as i:
                for b in bodies:
                    b.i = i
                    yield b
                    b.i = 0


def need(eng, sem, value):
    if not isinstance(value, int) or value > 0:
        eng.wait_ge(sem, value)


def build(nc, a):
    blocks, total = plan()
    ctx = ExitStack()
    with ctx:
        def sb(name, shape, dt):
            return ctx.enter_context(nc.sbuf_tensor(name, shape, dt))

        def sem(name):
            return ctx.enter_context(nc.semaphore(name))

        parts_dram = nc.dram_tensor("parts_scratch", [2, 2, 2, D, T], F16).ap()
        recip_dram = nc.dram_tensor("recip_scratch", [H, T], F32).ap()
        rows_dram = nc.dram_tensor("rows_scratch", [E * CAP, D], F32).ap()
        back_dram = nc.dram_tensor("back_scratch", [E * CAP, D + 2], F32).ap()

        psS = ctx.enter_context(nc.psum_tensor("psS", [P, RING_S, T], F32))
        psK = ctx.enter_context(nc.psum_tensor("psK", [P, RING_K, T], F32))
        psO = ctx.enter_context(nc.psum_tensor("psO", [P, T], F32))
        psM = ctx.enter_context(nc.psum_tensor("psM", [P, T], F32))

        X = sb("X", [P, NB, TT * D], F32)
        stack = sb("stack", [P, 2, 2, H * T], F16)
        probs = sb("probs", [P, P_RING, 2, T], F32)
        V = sb("V", [P, 2, TT, H * 2 * HD], F32)
        parts = sb("parts", [P, 2, FT, 2, T], F16)
        xn = sb("xn", [P, TT, D], F32)
        xT = sb("xT", [P, 2, FT, T], F16)
        U = sb("U", [P, 2, T], F32)
        packed = sb("packed", [P, FT, T], F32)
        sums = sb("sums", [P, 64], F32)
        recip = sb("recip", [P, 64], F32)
        recipB = sb("recipB", [P, FT, T], F32)
        attn = sb("attn", [P, 2, FT, T], F16)
        wo1 = sb("wo1", [P, 2, FT, D], F16)
        wx = sb("wx", [P, 4, 2, FT, D], F16)
        wc = sb("wc", [P, 2, 2, D], F16)
        wp = sb("wp", [P, 2, FT, D], F16)
        wg = sb("wg", [P, FT, E], F32)
        shared = sb("shared", [P, 3072 + 1536], F32)
        rope_cs = shared[:, 0:1024].rearrange("p (s t) -> p s t", s=2)
        rope_x = shared[:, 1024:2048].rearrange("p (s t) -> p s t", s=2)
        rope_s = shared[:, 2048:3072].rearrange("p (s t) -> p s t", s=2)
        rope_c = xn[:, :, :].rearrange("p (s k) d -> p s (k d)", s=2)
        wqkv = shared[:, 3072:4608].bitcast(F16).rearrange("p (a k n) -> p a k n", a=2, k=FT)
        attn_b = shared[:, 0:1024].rearrange("p (f t) -> p f t", f=FT)
        ctx_sb = shared[:, 1024:1536].rearrange("p (t c) -> p t c", t=TT)
        ctxT = shared[:, 1536:2048].bitcast(F16).rearrange("p (a t) -> p a t", a=2)
        zT = shared[:, 2048:3072].rearrange("p (f t) -> p f t", f=FT)
        back = shared[:, 3072:3072 + TT * (D + 2)].rearrange("p (t d) -> p t d", t=TT)
        bias_v = sb("bias_v", [P, 3, D], F32)
        bias_o = sb("bias_o", [P, 2, D], F32)
        bias_qk = sb("bias_qk", [P, 6, FT], F32)
        consts = sb("consts", [P, 4 * P + TT * E + TT], F32)
        ident = consts[:, 0:P]
        expert_no = consts[:, 4 * P:4 * P + TT * E]
        token_no = consts[:, 4 * P + TT * E:]
        halves = sb("halves", [P, 4, P], BF16)
        ident_bf, mask_q, mask_k, tri = (halves[:, j, :] for j in range(4))
        ones_bf = sb("ones_bf", [P, P], BF16)
        ident_h = sb("ident_h", [P, P], F16)
        negmax = sb("negmax", [P, 2, S_UNITS // NG], F32)
        mparts = sb("mparts", [P, TT, 2, GH], F16)
        mrows = sb("mrows", [2 * GH, T], F16)
        stats = sb("stats", [P, TT, 6], F32)
        lnt = sb("lnt", [P, 7, TT], F32)
        rstd = sb("rstd", [P, TT], F32)
        minus_half = sb("minus_half", [P, TT], F32)
        gate_scale = sb("gate_scale", [P, TT], F32)
        rt = sb("rt", [P, 6, TT * E], F32)
        rs = sb("rs", [P, 10, TT], F32)
        onehot = sb("onehot", [P, TT * E], BF16)
        filled = sb("filled", [P, E], F32)
        scatter_to = sb("scatter_to", [P, TT], U32)
        put_to = sb("put_to", [P, 2, 2], U32)

        raw = probs[:, :, :, :].rearrange("p r h t -> p (r h t)")
        raw_qkv = raw[:, 0:1536].rearrange("p (k n) -> p k n", k=FT)
        raw_o = raw[:, 1536:2048].rearrange("p (k n) -> p k n", k=FT)
        raw_x = raw[:, 2048:4096].rearrange("p (j k n) -> p j k n", j=4, k=FT)
        raw_c = packed[:, 0, :].rearrange("p (j n) -> p j n", j=2)
        raw_p = packed[:, 1, :].rearrange("p (k n) -> p k n", k=FT)
        to_split = [(wqkv[:, a, :, :], raw_qkv) for a in range(2)], [
            pair for a in range(2) for pair in ((wo1[:, a, :, :], raw_o), (wx[:, :, a, :, :], raw_x),
                                                (wc[:, :, a, :], raw_c), (wp[:, a, :, :], raw_p))]

        free0, free1 = (stack[:, q, :, :].rearrange("p a n -> p (a n)").bitcast(F32) for q in range(2))
        w1_sb = [free0[:, 2048 * c:2048 * (c + 1)].rearrange("p (k f) -> p k f", k=FT) for c in range(2)]
        w2_sb = [free0[:, 4096 + 2048 * c:4096 + 2048 * (c + 1)].rearrange("p (k m) -> p k m", k=FF) for c in range(2)]
        hT = [free1[:, 2048 * c:2048 * (c + 1)].bitcast(F16).rearrange("p (a f s) -> p a f s", a=2, f=FF) for c in range(2)]
        rows_sb = [free1[:, 4096 + 512 * c:4096 + 512 * (c + 1)].rearrange("p (s m) -> p s m", s=2) for c in range(2)]
        rowsT = [free1[:, 5120 + 512 * c:5120 + 512 * (c + 1)].bitcast(F16).rearrange("p (a m s) -> p a m s", a=2, m=FT)
                 for c in range(2)]
        halves_of = [V[:, :, :, :].rearrange("p a k n -> p (a k n)").bitcast(F16),
                     X[:, 0:4, :].rearrange("p b n -> p (b n)").bitcast(F16)]
        w1_parts = [halves_of[c][:, 0:4096].rearrange("p (a k f) -> p a k f", a=2, k=FT) for c in range(2)]
        w2_parts = [halves_of[c][:, 4096:8192].rearrange("p (a k m) -> p a k m", a=2, k=FF) for c in range(2)]
        eo_sb = [free1[:, 6144 + 512 * c:6144 + 512 * (c + 1)].rearrange("p (s m) -> p s m", s=2) for c in range(2)]
        psH = [psS[:, 0, :], psS[:, 1, :], psS[:, 2, :], psK[:, 0, :]]
        psY = [psK[:, 1, :], psK[:, 2, :]]
        psR = [psO[:, :], psM[:, :]]
        back_sb = [probs[:, c, :, :].rearrange("p h t -> p (h t)")[:, 0:2 * (D + 2)].rearrange("p (s d) -> p s d", s=2)
                   for c in range(2)]

        s = {name: sem(name) for name in total}
        x0_in, x1_in, x_in, w_in, wqkv_in, bias_in, cst_in, w_hi, w_lo = (
            sem(n) for n in ("x0_in", "x1_in", "x_in", "w_in", "wqkv_in", "bias_in", "cst_in", "w_hi", "w_lo"))
        rows_zero, stack_set0, stack_set1, cst_set, v_ones, misc_set = (
            sem(n) for n in ("rows_zero", "stack_set0", "stack_set1", "cst_set", "v_ones", "misc_set"))
        ew1_in, ew2_in, rows_in = ([sem(f"{n}_{c}") for c in range(2)]
                                            for n in ("ew1_in", "ew2_in", "rows_in"))
        rowsT_done, rows_hi, rows_lo, hid_done, hid_hi, hid_lo, y_done, y_out, w1_hi, w1_lo, w2_hi, w2_lo = (
            sem(n) for n in ("rowsT_done", "rows_hi", "rows_lo", "hid_done", "hid_hi", "hid_lo", "y_done", "y_out",
                             "w1_hi", "w1_lo", "w2_hi", "w2_lo"))
        back_in, put_done = ([sem(f"{n}_{c}") for c in range(2)] for n in ("back_in", "put_done"))

        def s_unit(b, t, j):
            u = 2 * (t + LEAD) + j
            later = u >= S_UNITS
            return later, u % S_UNITS, 2 * t + j if b.kind else 2 * t + j - 2 * (SLOTS - LEAD)

        def has_s(b, later):
            return b.nxt if later else b.kind

        products = ((0, 0), (0, 1), (1, 0))

        def product(out, left, right, ks):
            steps = [(k, x, y) for k in ks for x, y in products]
            for k, x, y in steps:
                mm = nc.tensor.matmul(out, left(x, k), right(y, k), start=(k, x, y) == steps[0], stop=(k, x, y) == steps[-1])
            return mm

        def stack_of(parity, q_or_k):
            return stack[:, parity, q_or_k, :].rearrange("p (h t) -> p h t", h=H)

        def v_of(parity):
            return V[:, parity, :, :].rearrange("p k (h c) -> p k h c", h=H)

        def evacuated(b, t):
            if t == 2 and b.prev:
                return NG - 1
            return t // 8 - 1 if b.kind and t > 2 and t % 8 == 2 else None

        def expert_hi(act, e, c, loaded, which):
            src, dst, came, used, out = ((w1_sb[c], w1_parts[c], ew1_in[c], (hid_done, e * 4 - 4), w1_hi),
                                         (w2_sb[c], w2_parts[c], ew2_in[c], (y_done, e - 1), w2_hi))[which]
            act.wait_ge(came, loaded)
            need(act, *used)
            for k in range(2):
                n = src.shape[1] // 2
                o = nc.scalar.mul(dst[:, 0, n * k:n * (k + 1), :], src[:, n * k:n * (k + 1), :], WSCALE)
            o.then_inc(out, 1)

        block = ctx.enter_context(nc.Block())

        @block.sync
        def _(sp):
            sp.dma_start(X[:, 0, :].rearrange("p (t d) -> p t d", t=TT),
                         a["x"][0].rearrange("(t p) d -> p t d", p=P)).then_inc(x0_in, 16)
            sp.dma_start(raw_qkv, a["W_qkv_T"].rearrange("(k p) n -> p k n", p=P)).then_inc(wqkv_in, 16)
            for j, src in enumerate((a["L0_attn_b_out"], a["L0_xattn_bp"])):
                sp.dma_start(bias_o[:, j, :], src.rearrange("(o n) -> o n", o=1).to_broadcast([P, D])).then_inc(bias_in, 16)
            for j, src in enumerate((a["L0_attn_b_qkv"][2 * D:3 * D], a["L0_xattn_bv"], a["L0_xattn_bcv"])):
                sp.dma_start(bias_v[:, j, :], src.rearrange("(o n) -> o n", o=1).to_broadcast([P, D])).then_inc(bias_in, 16)
            sp.dma_start(X[:, 1, :].rearrange("p (t d) -> p t d", t=TT),
                         a["x"][1].rearrange("(t p) d -> p t d", p=P)).then_inc(x1_in, 16)

            def load_rest():
                for n in range(2, NB):
                    sp.dma_start(X[:, n, :].rearrange("p (t d) -> p t d", t=TT),
                                 a["x"][n].rearrange("(t p) d -> p t d", p=P)).then_inc(x_in, 16)

            def load_weights():
                sp.dma_start(raw_o, a["W_out_T"].rearrange("(k p) n -> p k n", p=P)).then_inc(w_in, 16)
                for j, name in enumerate(("L0_xattn_Wq", "L0_xattn_Wk", "L0_xattn_Wv", "L0_xattn_Wcq")):
                    sp.dma_start(raw_x[:, j, :, :], a[name].rearrange("(k p) n -> p k n", p=P)).then_inc(w_in, 16)
                sp.dma_start(raw_c[:, 0, :], a["L0_xattn_Wck"]).then_inc(w_in, 16)
                sp.dma_start(raw_c[:, 1, :], a["L0_xattn_Wcv"]).then_inc(w_in, 16)
                sp.dma_start(raw_p, a["L0_xattn_Wp"].rearrange("(k p) n -> p k n", p=P)).then_inc(w_in, 16)
                sp.dma_start(wg[:, :, :], a["L0_ffn_Wg"].rearrange("(k p) n -> p k n", p=P)).then_inc(w_in, 16)

            for b in stretches(sp, blocks):
                np_ = 1 - b.parity
                jobs = b.jobs()
                for t in range(SLOTS):
                    if b.n == -1 and t == 0:
                        load_weights()
                    if b.n == 0 and t == 0:
                        sp.wait_ge(w_lo, 5)
                    if b.n == -1 and t == 3:
                        load_rest()
                    if b.n == 7 and t % 8 == 6:
                        sp.dma_start(rows_dram.rearrange("(j p r) d -> j p (r d)", j=NG, p=32)[t // 8],
                                     stack[64:96, 0, :, :].rearrange("p a n -> p (a n)").bitcast(F32)).then_inc(rows_zero, 16)
                        sp.dma_start(back_dram.rearrange("(j p r) d -> j p (r d)", j=NG, p=32)[t // 8, :, 0:8192],
                                     stack[64:96, 0, :, :].rearrange("p a n -> p (a n)").bitcast(F32)).then_inc(rows_zero, 16)
                        sp.dma_start(back_dram.rearrange("(j p r) d -> j p (r d)", j=NG, p=32)[t // 8, :, 8192:],
                                     stack[64:96, 0, 0, 0:128].bitcast(F32)).then_inc(rows_zero, 16)
                    if b.route and t == 14:
                        need(sp, s["x_out"], b.at("x_out", 2 if b.fin else 0))
                        gb = b.batch(-1) if b.kind is None else b.batch(-2)
                        sp.dma_start(a["out"][bass.ds(gb, 1)].rearrange("o (t p) d -> p (o t) d", p=P),
                                     X[:, bass.ds(gb, 1), :].rearrange("p o (t d) -> p (o t) d", t=TT)).then_inc(s["x_stored"], 16)
                    if t == 0 and b.nx2 == "C":
                        need(sp, s["ctxT_out"], b.at("ctxT_out"))
                        if b.n == 7:
                            sp.wait_ge(s["lo_out"], b.at("lo_out"))
                        sp.dma_start(ctx_sb, a["ctx"][bass.ds(b.batch(2), 1)].rearrange("o (t p) c -> p (o t) c", p=P)
                                     ).then_inc(s["ctx_in"], 16)
                    g = evacuated(b, t)
                    if g is not None:
                        mine = t > 2
                        k = (1 if b.prev else 0) + g + 1 if mine else 1
                        sp.wait_ge(s["av_out"], b.at("av_out", k))
                        if mine and g == 0:
                            need(sp, s["attn_mul"], b.at("attn_mul", int(b.prev is not None)))
                        for i in range(GH):
                            h = GH * g + i
                            sp.dma_start(packed[HD * (h % 8):HD * (h % 8 + 1), h // 8, :],
                                         U[32 * i:32 * i + HD, g % 2, :]).then_inc(s[f"packed_{g % 2}"], 16)
                            sp.dma_start(sums[8 * h:8 * h + 8, :],
                                         U[32 * i + HD:32 * i + HD + 1, g % 2, :]).then_inc(s[f"packed_{g % 2}"], 16)
                    for slot, name, g in jobs:
                        if name == "negmax" and t == slot:
                            sp.wait_ge(s["negmax_rows"], b.at("negmax_rows", g if b.kind and g else (4 if b.kind else 1)))
                            for part in range(2):
                                sp.dma_start(stack_of(b.parity if g else np_, 0)[STACK + part:STACK + part + 1, GH * g:GH * (g + 1), :],
                                             mrows[GH * part:GH * (part + 1), :]).then_inc(s[f"negmax_in_{g % 2}"], 16)
                    if t == 5 and b.prev:
                        sp.wait_ge(s["recip_done"], b.at("recip_done", 1))
                        sp.dma_start(recip_dram.rearrange("h (c t) -> (h c) t", c=8), recip[:, :]).then_inc(s["recip_stored"], 16)
                        sp.wait_ge(s["recip_stored"], b.at("recip_stored", 16))
                        for ft in range(FT):
                            sp.dma_start(recipB[:, ft, :],
                                         recip_dram.rearrange("(f h o) t -> f h o t", f=FT, o=1)[ft].to_broadcast([8, HD, T])
                                         ).then_inc(s["recip_in"], 16)
                    if b.nxt and t == (2 if b.n < 0 else 14):
                        sp.wait_ge(s["parts_stored"], b.at("parts_stored"))
                        for qk, slots in ((0, (0, 0, 1, 1)), (1, (0, 1, 0, 1))):
                            for j, part in enumerate(slots):
                                sp.dma_start(stack_of(np_, qk)[HD * j:HD * (j + 1), :, :],
                                             parts_dram[np_, qk, part].rearrange("(h d) t -> d h t", d=HD)
                                             ).then_inc(s["stack_in"], 16)
                    for slot, name, j in jobs:
                        if name != "proj":
                            continue
                        ft, qk = j // 2, j % 2
                        if b.nx2 == "A" and t == slot:
                            if b.n < 0:
                                need(sp, s["lo_out"], b.at("lo_out", j - 1))
                            sp.wait_ge(s["rope_in"], b.at("rope_in", j + 1))
                            for o in range(2):
                                sp.dma_start(rope_s[o::2, j % 2, :], rope_x[1 - o::2, j % 2, :]).then_inc(s[f"swap_in_{j % 2}"], 16)
                        if t == slot + (6 if b.nx2 == "A" else 1):
                            sp.wait_ge(s["lo_out"], b.at("lo_out", j + 1))
                            sp.dma_start(parts_dram[b.parity, qk, :, ft * P:(ft + 1) * P, :].rearrange("s p t -> p s t"),
                                         parts[:, qk, ft, :, :]).then_inc(s["parts_stored"], 16)
                    if b.n == 23 and t == 16:
                        for c in range(2):
                            sp.dma_start(w1_sb[c], a["L0_ffn_w1"][c].rearrange("(k p) f -> p k f", p=P)).then_inc(ew1_in[c], 16)
                            sp.dma_start(w2_sb[c], a["L0_ffn_w2"][c].rearrange("(k p) m -> p k m", p=P)).then_inc(ew2_in[c], 16)
            sp.wait_ge(s["scattered"], total["scattered"])

            def load_rows(e, c):
                sp.dma_start(rows_sb[c], rows_dram[bass.ds(e * CAP, CAP), :].rearrange("(s p) m -> p s m", p=P)
                             ).then_inc(rows_in[c], 16)

            for c in range(2):
                load_rows(c, c)
            with sp.Fori(0, E // 2 - 1) as i:
                for c in range(2):
                    need(sp, rowsT_done, i * 2 + c + 1)
                    load_rows(i * 2 + 2 + c, c)
                    need(sp, w1_lo, i * 2 + c + 1)
                    sp.dma_start(w1_sb[c], a["L0_ffn_w1"][bass.ds(i * 2 + 2 + c, 1)].rearrange("o (k p) f -> p (o k) f", p=P)
                                 ).then_inc(ew1_in[c], 16)
                    need(sp, w2_lo, i * 2 + c + 1)
                    sp.dma_start(w2_sb[c], a["L0_ffn_w2"][bass.ds(i * 2 + 2 + c, 1)].rearrange("o (k p) m -> p (o k) m", p=P)
                                 ).then_inc(ew2_in[c], 16)
            sp.wait_ge(s["x_stored"], total["x_stored"])
            for c in range(2):
                sp.wait_ge(put_done[c], 16 * E)

        @block.tensor
        def _(pe):
            pe.wait_ge(cst_in, 16)
            pe.wait_ge(wqkv_in, 16 * 8)
            for b in stretches(pe, blocks):
                np_ = 1 - b.parity
                if b.n == -1:
                    pe.wait_ge(cst_set, 6)
                if b.n == 0:
                    pe.wait_ge(v_ones, 1)
                    pe.wait_ge(w_lo, 5)
                jobs = b.jobs()
                for t in range(SLOTS):
                    av = b.av(t)
                    if av:
                        prev, unit, q0, q1, first = av
                        par = np_ if prev else b.parity
                        g, kt = unit // 8, unit % 8 // 2
                        if first:
                            need(pe, s["exp_done"], b.at("exp_done", 0 if prev else 2 * unit + 4))
                            if not prev and unit == 0:
                                pe.wait_ge(s["v_out"], b.at("v_out"))
                            if kt == 0:
                                need(pe, s["av_out"], b.at("av_out", int(b.prev is not None) + g))
                        for i in range(GH):
                            mm = nc.tensor.matmul(psO[32 * i:32 * i + 32, q0:q1], v_of(par)[:, kt, GH * g + i, :],
                                                  probs[:, (unit + i // 2) % P_RING, i % 2, q0:q1],
                                                  start=kt == 0 and q0 == 0, stop=kt == TT - 1, skip_group_check=True)
                        mm.then_inc(s["av_done"], 1)

                    def maxima(j):
                        later, u, k = s_unit(b, t, j)
                        kind = has_s(b, later)
                        if not kind:
                            return
                        par = np_ if later else b.parity
                        h, qt = u // TT, u % TT
                        if later and u == 0:
                            if b.n in (-1, 0):
                                pe.wait_ge((stack_set0, stack_set1)[np_], 2)
                            pe.wait_ge(s["stack_in"], b.at("stack_in", 128))
                        if u == 0 or u >= RING_S:
                            need(pe, s["max_done"], b.at("max_done", k - (RING_S - 1 if u else 0)))
                        n = (qt + 1) * P if kind == "B" else T
                        out = psS[:, u % RING_S, 0:n]
                        mm = nc.tensor.matmul(out, stack_of(par, 0)[0:STACK, h, qt * P:(qt + 1) * P],
                                              stack_of(par, 1)[0:STACK, h, 0:n], start=True, stop=kind != "B",
                                              skip_group_check=kind == "B")
                        if kind == "B":
                            mm = nc.tensor.matmul(psS[:, u % RING_S, n - P:n], ident_bf, mask_q, start=False, stop=True,
                                                  skip_group_check=True)
                        mm.then_inc(s["scores_q"], 1)

                    def exponents(i):
                        if not b.kind:
                            return
                        g, kt, w = t // 8, t % 8 // 2, 2 * t + i
                        if t % 8 == 0 and i == 0:
                            pe.wait_ge(s[f"negmax_in_{g % 2}"], b.at(f"negmax_in_{g % 2}", (0, 32, 32, 64)[g]))
                        if w == 0 or w >= RING_K:
                            need(pe, s["exp_done"], b.at("exp_done", w - RING_K + 1 if w else 0))
                        q0 = q_from(b.kind, kt)
                        h = GH * g + 2 * (t % 2) + i
                        mm = nc.tensor.matmul(psK[:, w % RING_K, q0:T],
                                              stack_of(b.parity, 1)[0:MROWS, h, kt * P:(kt + 1) * P],
                                              stack_of(b.parity, 0)[0:MROWS, h, q0:T],
                                              start=True, stop=b.kind != "B", skip_group_check=b.kind == "B")
                        if b.kind == "B":
                            mm = nc.tensor.matmul(psK[:, w % RING_K, q0:q0 + P], ident_bf, mask_k, start=False,
                                                  stop=True, skip_group_check=True)
                        mm.then_inc(s["scores_k"], 1)

                    maxima(0)
                    exponents(0)
                    maxima(1)
                    exponents(1)
                    for idx, (slot, name, j) in enumerate(jobs):
                        if slot != t:
                            continue
                        freed = b.freed(idx - 1)
                        need(pe, s[freed[0]], b.at(*freed))
                        if name == "xT" or name == "zT":
                            route = name == "zT"
                            ln_no = int(b.nx2 in ("A", "B")) + 1 if route else 1
                            pe.wait_ge(s["ln_out"], b.at("ln_out", ln_no))
                            for tt in range(TT):
                                mm = nc.tensor.transpose(psM[:, tt * P:(tt + 1) * P], xn[:, tt, j * P:(j + 1) * P], ident)
                        elif name == "ctxT":
                            pe.wait_ge(s["ctx_in"], b.at("ctx_in", 16))
                            for tt in range(TT):
                                mm = nc.tensor.transpose(psM[:, tt * P:(tt + 1) * P], ctx_sb[:, tt, :], ident)
                        elif name == "proj":
                            ft, qk = j // 2, j % 2
                            if j == 0 and b.nx2 != "C":
                                pe.wait_ge(s["xT_lo"], b.at("xT_lo", 2))
                                if b.n < 0:
                                    pe.wait_ge(w_lo, 1)
                            if b.nx2 == "C" and qk == 1:
                                pe.wait_ge(s["ctxT_lo"], b.at("ctxT_lo", 1))
                                mm = product(psM[:, :], lambda x, k: wc[:, 0, x, ft * P:(ft + 1) * P],
                                             lambda y, k: ctxT[:, y, :], range(1))
                            else:
                                def w(x, k):
                                    if b.nx2 == "A":
                                        return wqkv[:, x, k, qk * D + ft * P:qk * D + (ft + 1) * P]
                                    return wx[:, 3 if b.nx2 == "C" else qk, x, k, ft * P:(ft + 1) * P]
                                mm = product(psM[:, :], w, lambda y, k: xT[:, y, k, :], range(FT))
                        elif name == "v":
                            for i in range(2):
                                tt = 2 * j + i
                                out = psM[:, i * D:(i + 1) * D]
                                if b.nxt == "C":
                                    mm = product(out, lambda x, k: ctxT[:, x, tt * P:(tt + 1) * P], lambda y, k: wc[:, 1, y, :],
                                                 range(1))
                                    continue
                                mm = product(out, lambda x, k: xT[:, x, k, tt * P:(tt + 1) * P],
                                             lambda y, k: wqkv[:, y, k, 2 * D:3 * D] if b.nxt == "A" else wx[:, 2, y, k, :],
                                             range(FT))
                        elif name == "negmax":
                            k = j if b.kind and j else (4 if b.kind else 1)
                            pe.wait_ge(s["negmax_split"], b.at("negmax_split", k))
                            mrow_ps = psM[:, 0:T // 2].bitcast(F16)
                            for qt in range(TT):
                                mm = nc.tensor.transpose(mrow_ps[0:2 * GH, qt * P:(qt + 1) * P],
                                                         mparts[:, qt, :, :].rearrange("p s h -> p (s h)"), ident_h[:, :])
                        elif name == "out":
                            pe.wait_ge(s["attn_out"], b.at("attn_out", 1))
                            w = wo1 if b.fin == "A" else wp
                            for i in range(2):
                                tt = 2 * j + i
                                mm = product(psM[:, i * D:(i + 1) * D], lambda x, k: attn[:, x, k, tt * P:(tt + 1) * P],
                                             lambda y, k: w[:, y, k, :], range(FT))
                        elif name == "logits":
                            pe.wait_ge(s["zT_out"], b.at("zT_out", 2))
                            pe.wait_ge(w_in, 16 * 9)
                            for tt in range(TT):
                                for k in range(FT):
                                    mm = nc.tensor.matmul(psM[:, tt * E:(tt + 1) * E], zT[:, k, tt * P:(tt + 1) * P],
                                                          wg[:, k, :], start=k == 0, stop=k == FT - 1)
                        elif name == "count":
                            pe.wait_ge(s["onehot_out"], b.at("onehot_out", 1))
                            for tt in range(TT + 1):
                                for o in range(min(tt + 1, TT)):
                                    w = tri if o == tt else ones_bf[:, :]
                                    mm = nc.tensor.matmul(psM[:, tt * E:(tt + 1) * E], w, onehot[:, o * E:(o + 1) * E],
                                                          start=o == 0, stop=o == min(tt, TT - 1))
                        mm.then_inc(s["jobs_done"], 1)
            pe.wait_ge(s["route_dve"], total["route_dve"])
            pe.wait_ge(s["av_out"], total["av_out"])

            def transpose_rows(c, loaded, free):
                pe.wait_ge(rows_in[c], loaded)
                need(pe, rows_lo, free)
                for m in range(FT):
                    for st in range(2):
                        mm = nc.tensor.transpose(psR[c][:, m * CAP + st * P:m * CAP + (st + 1) * P],
                                                 rows_sb[c][:, st, m * P:(m + 1) * P], ident)
                mm.then_inc(rowsT_done, 1)

            def hidden(e, c):
                pe.wait_ge(w1_lo, e + 1)
                pe.wait_ge(rows_lo, e + 1)
                for f2 in range(FF // 2):
                    need(pe, hid_lo, e * 4 + f2 - 3)
                    for i in range(2):
                        f = 2 * f2 + i
                        mm = product(psH[f2][:, i * CAP:(i + 1) * CAP], lambda x, k: w1_parts[c][:, x, k, f * P:(f + 1) * P],
                                     lambda y, k: rowsT[c][:, y, k, :], range(FT))
                    mm.then_inc(hid_done, 1)

            def output(e, c, free):
                pe.wait_ge(w2_lo, e + 1)
                pe.wait_ge(hid_lo, e * 4 + 4)
                need(pe, y_out, free)
                for st in range(2):
                    mm = product(psY[c][:, st * D:(st + 1) * D], lambda x, f: hT[c][:, x, f, st * P:(st + 1) * P],
                                 lambda y, f: w2_parts[c][:, y, f, :], range(FF))
                mm.then_inc(y_done, 1)

            transpose_rows(0, 16, 0)
            transpose_rows(1, 16, 0)
            hidden(0, 0)
            hidden(1, 1)
            transpose_rows(0, 32, 1)
            output(0, 0, 0)
            hidden(2, 0)
            transpose_rows(1, 32, 2)
            output(1, 1, 0)
            with pe.Fori(0, E // 2 - 2) as i:
                hidden(i * 2 + 3, 1)
                transpose_rows(0, i * 16 + 48, i * 2 + 3)
                output(i * 2 + 2, 0, i * 2 + 1)
                hidden(i * 2 + 4, 0)
                transpose_rows(1, i * 16 + 48, i * 2 + 4)
                output(i * 2 + 3, 1, i * 2 + 2)
            hidden(E - 1, 1)
            output(E - 2, 0, E - 3)
            output(E - 1, 1, E - 2)

        @block.scalar
        def _(act):
            act.dma_start(consts[:, :], a["consts"]).then_inc(cst_in, 16)
            act.dma_start(rope_cs, a["rope"].rearrange("s p t -> p s t")).then_inc(wqkv_in, 16)
            for j, name in enumerate(("A_bq", "A_bk", "L0_xattn_bq", "L0_xattn_bk", "L0_xattn_bcq", "L0_xattn_bck")):
                src = a["L0_attn_b_qkv"][D * j:D * (j + 1)] if j < 2 else a[name]
                with nc.allow_non_contiguous_dma("a bias per feature, once"):
                    act.dma_start(bias_qk[:, j, :], src.rearrange("(f p) -> p f", p=P)).then_inc(wqkv_in, 16)
            act.wait_ge(wqkv_in, 16 * 8)
            nc.scalar.mul(to_split[0][0][0], to_split[0][0][1], WSCALE).then_inc(w_hi, 1)
            for b in stretches(act, blocks):
                np_ = 1 - b.parity
                if b.n == 0:
                    act.wait_ge(w_lo, 5)
                jobs = b.jobs()
                for t in range(SLOTS):
                    if b.n == -1 and t == 9:
                        act.wait_ge(w_in, 16 * 9)
                        for dst, src in to_split[1][0:4]:
                            nc.scalar.mul(dst, src, WSCALE).then_inc(w_hi, 1)
                    if b.fin and t == b.attn_slot:
                        act.wait_ge(*((s["attn_mul"], b.at("attn_mul", 1)) if b.fin == "A" else
                                      (s["attn_sum"], b.at("attn_sum", 1))))
                        need(act, s["x_out"], b.at("x_out"))
                        nc.scalar.copy(attn[:, 0, :, :], recipB[:, :, :]).then_inc(s["attn_hi"], 1)
                    if b.n == 24 and t == 3:
                        act.wait_ge(s["av_done"], total["av_done"])
                        act.wait_ge(s["x_stored"], b.at("x_stored"))
                        act.wait_ge(s["back_set"], b.at("back_set"))
                        for c in range(2):
                            for which in range(2):
                                expert_hi(act, c, c, 16, which)
                    g = evacuated(b, t)
                    if g is not None:
                        act.wait_ge(s["av_done"], b.at("av_done", b.av_count(t)))
                        if t == 2:
                            used = b.at("packed_1")
                        elif g % 2:
                            used = b.at("packed_1", 128 if b.prev else 0)
                        else:
                            used = b.at("packed_0", 64 * g)
                        need(act, s[f"packed_{g % 2}"], used)
                        nc.scalar.copy(U[:, g % 2, :], psO[:, :]).then_inc(s["av_out"], 1)
                    if b.kind:
                        q0 = q_from(b.kind, t % 8 // 2)
                        if t % 2 == 0:
                            need(act, s["av_done"], b.at("av_done", b.av_count(t)))
                        for i in range(2):
                            act.wait_ge(s["scores_k"], b.at("scores_k", 2 * t + i + 1))
                            nc.scalar.activation(probs[:, t % P_RING, i, q0:T], psK[:, (2 * t + i) % RING_K, q0:T], ACT.Exp,
                                                 scale=SM_SCALE / (1 if b.kind == "A" else WSCALE ** 2)
                                                 ).then_inc(s["exp_done"], 1)
                    for idx, (slot, name, j) in enumerate(jobs):
                        if slot == t and name in ("xT", "zT", "ctxT", "proj", "negmax"):
                            act.wait_ge(s["jobs_done"], b.at("jobs_done", idx + 1))
                            if name == "xT":
                                need(act, s["v_out"], b.at("v_out"))
                                nc.scalar.copy(xT[:, 0, j, :], psM[:, :]).then_inc(s["xT_out"], 1)
                            elif name == "zT":
                                nc.scalar.copy(zT[:, j, :], psM[:, :]).then_inc(s["zT_out"], 1)
                            elif name == "ctxT":
                                nc.scalar.copy(ctxT[:, 0, :], psM[:, :]).then_inc(s["ctxT_out"], 1)
                            elif name == "proj":
                                ft, qk = j // 2, j % 2
                                bias = bias_qk[:, 2 * "ABC".index(b.nx2) + qk, ft:ft + 1]
                                if b.nx2 == "A":
                                    need(act, s["rope_out"], b.at("rope_out", j - 1))
                                    nc.scalar.activation(rope_x[:, j % 2, :], psM[:, :], ACT.Identity, bias=bias,
                                                         scale=1.0 / WSCALE).then_inc(s["rope_in"], 1)
                                else:
                                    if j == 0:
                                        need(act, s["parts_stored"], b.at("parts_stored"))
                                    nc.scalar.activation(parts[:, qk, ft, 0, :], psM[:, :], ACT.Identity, bias=bias
                                                         ).then_inc(s["hi_out"], 1)
                            else:
                                if b.kind:
                                    before = {1: (0, 0), 2: (1, 32), 3: (0, 32), 0: (1, 64)}[j]
                                    need(act, s[f"negmax_in_{before[0]}"], b.at(f"negmax_in_{before[0]}", before[1]))
                                nc.scalar.copy(mrows[:, :], psM[0:2 * GH, 0:T // 2].bitcast(F16)
                                               ).then_inc(s["negmax_rows"], 1)
                        if name == "proj" and b.nx2 == "A" and t == slot + 5:
                            act.wait_ge(s["rope_out"], b.at("rope_out", j + 1))
                            if j == 0:
                                need(act, s["parts_stored"], b.at("parts_stored"))
                            nc.scalar.copy(parts[:, j % 2, j // 2, 0, :], rope_s[:, j % 2, :]).then_inc(s["hi_out"], 1)
                        if name == "logits" and slot == t:
                            act.wait_ge(s["route_dve"], b.at("route_dve", 2))
                            nc.scalar.activation(rt[:, 1, :], rt[:, 0, :], ACT.Exp).then_inc(s["route_exp"], 1)
            def rows_high(e, c):
                act.wait_ge(rowsT_done, e + 1)
                need(act, hid_done, e * 4 - 4)
                nc.scalar.copy(rowsT[c][:, 0, :, :], psR[c].rearrange("p (m s) -> p m s", m=FT)).then_inc(rows_hi, 1)

            def relu_high(e, c, f2):
                act.wait_ge(hid_done, e * 4 + f2 + 1)
                if f2 == 0:
                    need(act, y_done, e - 1)
                nc.scalar.activation(hT[c][:, 0, 2 * f2:2 * f2 + 2, :], psH[f2].rearrange("p (f s) -> p f s", f=2), ACT.Relu
                                     ).then_inc(hid_hi, 1)

            def step(e, c, loaded, ahead=True):
                relu_high(e, c, 0)
                if ahead:
                    expert_hi(act, e + 1, 1 - c, loaded, 0)
                for f2 in range(1, 4):
                    relu_high(e, c, f2)
                if ahead:
                    rows_high(e + 1, 1 - c)
                    expert_hi(act, e + 1, 1 - c, loaded, 1)

            rows_high(0, 0)
            rows_high(1, 1)
            for f2 in range(4):
                relu_high(0, 0, f2)
            step(1, 1, 32)
            with act.Fori(0, E // 2 - 2) as i:
                step(i * 2 + 2, 0, i * 16 + 32)
                step(i * 2 + 3, 1, i * 16 + 48)
            step(E - 2, 0, 16 * (E // 2))
            step(E - 1, 1, 0, ahead=False)

        @block.vector
        def _(dve):
            nc.vector.memset(minus_half[:, :], -0.5).then_inc(misc_set, 1)
            nc.vector.memset(gate_scale[:, :], WSCALE ** -2)
            nc.vector.memset(filled[:, :], 0.0).then_inc(misc_set, 1)

            def expert_lo(e, c, which):
                src, dst, hi, out = ((w1_sb[c], w1_parts[c], w1_hi, w1_lo), (w2_sb[c], w2_parts[c], w2_hi, w2_lo))[which]
                dve.wait_ge(hi, e + 1)
                nc.vector.scalar_tensor_tensor(out=dst[:, 1, :, :], in0=src, scalar=WSCALE, in1=dst[:, 0, :, :],
                                               op0=ALU.mult, op1=ALU.subtract).then_inc(out, 1)

            def split_low(high, low, k):
                dve.wait_ge(w_hi, k)
                nc.vector.scalar_tensor_tensor(out=low[0], in0=low[1], scalar=WSCALE, in1=high[0],
                                               op0=ALU.mult, op1=ALU.subtract).then_inc(w_lo, 1)

            def layernorm(b, batch, t, first, k):
                if t in (first, first + 1):
                    for tt in range(2 * (t - first), 2 * (t - first) + 2):
                        o = nc.vector.bn_stats(stats[:, tt, :], X[:, bass.ds(batch, 1), tt * D:(tt + 1) * D].rearrange("p o d -> p (o d)"))
                if t == first + 1:
                    o.then_inc(s["bn_done"], 1)
                    need(dve, s["bn_done"], b.at("bn_done", k))
                    mean_e, ss_e, mean_o, ss_o = (stats[:, :, c] for c in (1, 2, 4, 5))
                    nc.vector.tensor_tensor(lnt[:, 0, :], mean_e, mean_o, ALU.add)
                    nc.vector.tensor_tensor(lnt[:, 1, :], mean_e, mean_o, ALU.subtract)
                    nc.vector.tensor_tensor(lnt[:, 2, :], ss_e, ss_o, ALU.add).then_inc(s["ln_step"], 1)
                    dve.wait_ge(s["ln_step"], b.at("ln_step", 3 * k - 2))
                    nc.vector.tensor_tensor(lnt[:, 3, :], lnt[:, 1, :], lnt[:, 1, :], ALU.mult).then_inc(s["ln_step"], 1)
                    nc.vector.tensor_scalar(lnt[:, 5, :], lnt[:, 0, :], 0.5, None, ALU.mult)
                    dve.wait_ge(s["ln_step"], b.at("ln_step", 3 * k - 1))
                    nc.vector.scalar_tensor_tensor(out=lnt[:, 4, :], in0=lnt[:, 3, :], scalar=D / 4.0, in1=lnt[:, 2, :],
                                                   op0=ALU.mult, op1=ALU.add).then_inc(s["ln_step"], 1)
                    dve.wait_ge(s["ln_step"], b.at("ln_step", 3 * k))
                    nc.vector.tensor_scalar(lnt[:, 6, :], lnt[:, 4, :], 1.0 / D, LN_EPS, ALU.mult, ALU.add
                                            ).then_inc(s["ln_var"], 1)
                if t in (first + 2, first + 3):
                    dve.wait_ge(s["ln_rstd"], b.at("ln_rstd", k))
                    need(dve, s["scattered"], b.at("scattered"))
                    need(dve, s["xT_out"], b.at("xT_out", 2 * (k - 1)))
                    for tt in range(2 * (t - first) - 4, 2 * (t - first) - 2):
                        o = nc.vector.tensor_scalar(xn[:, tt, :], X[:, bass.ds(batch, 1), tt * D:(tt + 1) * D].rearrange("p o d -> p (o d)"),
                                                    lnt[:, 5, tt:tt + 1], rstd[:, tt:tt + 1], ALU.subtract, ALU.mult)
                if t == first + 3:
                    o.then_inc(s["ln_out"], 1)

            for b in stretches(dve, blocks):
                np_ = 1 - b.parity
                jobs = b.jobs()
                ln = int(b.nx2 in ("A", "B"))
                for t in range(SLOTS):
                    if b.nx2 == "B" and t == b.ln_slot:
                        need(dve, s["x_out"], b.at("x_out"))
                    if b.route and t == 12:
                        need(dve, s["x_out"], b.at("x_out", 2 if b.fin else 0))
                    for j in range(2):
                        later, u, k = s_unit(b, t, j)
                        kind = has_s(b, later)
                        if not kind:
                            continue
                        g = u // (S_UNITS // NG)
                        n = (u % TT + 1) * P if kind == "B" else T
                        if u % (S_UNITS // NG) == 0:
                            need(dve, s["negmax_split"], b.at("negmax_split", t // 8 if b.kind else 0))
                        dve.wait_ge(s["scores_q"], b.at("scores_q", k + 1))
                        nc.vector.tensor_reduce(negmax[:, g % 2, u % 16:u % 16 + 1], psS[:, u % RING_S, 0:n], AX_X, ALU.max,
                                                negate=True).then_inc(s["max_done"], 1)
                    if (b.kind and t in (4, 12, 20)) or (b.nxt and t == 28):
                        g = (t // 8 + 1) % NG
                        k = t // 8 + 1 if b.kind else 1
                        done = 2 * (t - 4) + 8 if b.kind else 16
                        view = negmax[:, g % 2, :].rearrange("p (h q) -> p q h", h=GH)
                        dve.wait_ge(s["max_done"], b.at("max_done", done))
                        need(dve, s["negmax_rows"], b.at("negmax_rows", k - 1))
                        nc.vector.tensor_scalar(mparts[:, :, 0, :], view, 1.0 / MSCALE, None, ALU.mult
                                                ).then_inc(s["negmax_hi"], 1)
                        dve.wait_ge(s["negmax_hi"], b.at("negmax_hi", k))
                        nc.vector.scalar_tensor_tensor(out=mparts[:, :, 1, :], in0=view, scalar=1.0 / MSCALE,
                                                       in1=mparts[:, :, 0, :], op0=ALU.mult, op1=ALU.subtract
                                                       ).then_inc(s["negmax_split"], 1)
                    if t == 5 and b.prev:
                        dve.wait_ge(s["packed_0"], b.at("packed_0"))
                        dve.wait_ge(s["packed_1"], b.at("packed_1", 128))
                        need(dve, s["recip_stored"], b.at("recip_stored"))
                        nc.vector.reciprocal(recip[:, :], sums[:, :]).then_inc(s["recip_done"], 1)
                    if b.n == 24 and t == 5:
                        for c in range(2):
                            for which in range(2):
                                expert_lo(c, c, which)
                    if ln and t in range(b.ln_slot, b.ln_slot + 4):
                        if b.nx2 == "A" and t == b.ln_slot:
                            if b.n < 0:
                                dve.wait_ge(*((x0_in, 16) if b.n == -2 else (x1_in, 16)))
                            elif b.n == 0:
                                dve.wait_ge(x_in, 16 * (NB - 2))
                        layernorm(b, b.batch(2), t, b.ln_slot, 1)
                    if b.n == -2 and t == 7:
                        split_low(*to_split[0], 1)
                        dve.wait_ge(cst_in, 16)
                        nc.vector.tensor_copy(ident_bf, ident).then_inc(cst_set, 1)
                        nc.vector.tensor_copy(ident_h[:, :], ident).then_inc(cst_set, 1)
                        for j, dst in ((1, mask_q), (2, mask_k), (3, tri)):
                            nc.vector.tensor_copy(dst, consts[:, j * P:(j + 1) * P]).then_inc(cst_set, 1)
                        nc.vector.memset(ones_bf[:, :], 1.0).then_inc(cst_set, 1)
                    if b.n == -1 and t == 9:
                        nc.vector.tensor_scalar(bias_qk[:, 2:6, :], bias_qk[:, 2:6, :], WSCALE, None, ALU.mult)
                        for o in range(4):
                            split_low(to_split[1][o], to_split[1][4 + o], o + 2)
                    if b.n == -1 and t == 0:
                        dve.wait_ge(wqkv_in, 16 * 8)
                        dve.wait_ge(bias_in, 16 * 5)
                    if b.n == -2 and t == 25:
                        nc.vector.memset(V[:, :, :, :].rearrange("p a k (h c) -> p (a k) h c", h=H)[:, :, :, HD:2 * HD], 1.0
                                         ).then_inc(v_ones, 1)
                    for idx, (slot, name, j) in enumerate(jobs):
                        if slot != t:
                            continue
                        done = b.at("jobs_done", idx + 1)
                        if name == "proj" and b.nx2 != "A":
                            ft, qk = j // 2, j % 2
                            dve.wait_ge(s["hi_out"], b.at("hi_out", j + 1))
                            nc.vector.scalar_tensor_tensor(
                                out=parts[:, qk, ft, 1, :], in0=psM[:, :],
                                scalar=bias_qk[:, 2 * "ABC".index(b.nx2) + qk, ft:ft + 1], in1=parts[:, qk, ft, 0, :],
                                op0=ALU.add, op1=ALU.subtract).then_inc(s["lo_out"], 1)
                        elif name == "xT":
                            dve.wait_ge(s["xT_out"], b.at("xT_out", j + 1))
                            nc.vector.tensor_tensor(xT[:, 1, j, :], psM[:, :], xT[:, 0, j, :], ALU.subtract).then_inc(s["xT_lo"], 1)
                        elif name == "ctxT":
                            dve.wait_ge(s["ctxT_out"], b.at("ctxT_out", 1))
                            nc.vector.tensor_tensor(ctxT[:, 1, :], psM[:, :], ctxT[:, 0, :], ALU.subtract).then_inc(s["ctxT_lo"], 1)
                        elif name == "v":
                            dve.wait_ge(s["jobs_done"], done)
                            for i in range(2):
                                tt = 2 * j + i
                                nc.vector.scalar_tensor_tensor(
                                    out=v_of(np_)[:, tt, :, 0:HD],
                                    in0=psM[:, i * D:(i + 1) * D].rearrange("p (h c) -> p h c", h=H), scalar=1.0 / WSCALE,
                                    in1=bias_v[:, "ABC".index(b.nxt), :].rearrange("p (h c) -> p h c", h=H),
                                    op0=ALU.mult, op1=ALU.add).then_inc(s["v_out"], 1)
                        elif name == "out":
                            dve.wait_ge(s["jobs_done"], done)
                            need(dve, s["x_bias"], b.at("x_bias", 0))
                            xs = X[:, bass.ds(b.batch(-1), 1), 2 * j * D:2 * (j + 1) * D].rearrange("p o d -> p (o d)")
                            nc.vector.scalar_tensor_tensor(out=xs, in0=psM[:, :], scalar=1.0 / WSCALE, in1=xs,
                                                           op0=ALU.mult, op1=ALU.add).then_inc(s["x_out"], 1)
                    for slot, name, j in jobs:
                        if name == "proj" and b.nx2 == "A" and t == slot + 4:
                            dve.wait_ge(s["rope_sin"], b.at("rope_sin", j + 1))
                            nc.vector.tensor_tensor(rope_s[:, j % 2, :], rope_s[:, j % 2, :], rope_c[:, j % 2, :], ALU.add).then_inc(s["rope_out"], 1)
                    if b.route:
                        layernorm(b, b.batch(-1) if b.kind is None else b.batch(-2), t, 12, ln + 1)

                        def chain(ins, k):
                            ins.then_inc(s["route_dve"], 1)
                            dve.wait_ge(s["route_dve"], b.at("route_dve", k))

                        def wide(j):
                            return rt[:, j, :].rearrange("p (t e) -> p t e", e=E)

                        def over(j):
                            return rs[:, j, :, None].to_broadcast([P, TT, E])

                        gb = b.batch(-1) if b.kind is None else b.batch(-2)
                        idx = [i for i, job in enumerate(jobs) if job[1] == "logits"][0]
                        if t == 22:
                            dve.wait_ge(s["jobs_done"], b.at("jobs_done", idx + 1))
                            logits = psM[:, 0:TT * E].rearrange("p (t e) -> p t e", e=E)
                            chain(nc.vector.tensor_reduce(rs[:, 0, :], logits, AX_X, ALU.max), 1)
                            chain(nc.vector.tensor_tensor(wide(0), logits, over(0), ALU.subtract), 2)
                        if t == 23:
                            dve.wait_ge(s["route_exp"], b.at("route_exp", 1))
                            chain(nc.vector.tensor_reduce(rs[:, 1, :], wide(1), AX_X, ALU.add), 3)
                            chain(nc.vector.reciprocal(rs[:, 2, :], rs[:, 1, :]), 4)
                            chain(nc.vector.tensor_tensor(wide(2), wide(1), over(2), ALU.mult), 5)
                            chain(nc.vector.tensor_reduce(rs[:, 3, :], wide(2), AX_X, ALU.max), 6)
                            chain(nc.vector.tensor_tensor(wide(3), wide(2), over(3), ALU.is_ge), 7)
                            chain(nc.vector.scalar_tensor_tensor(out=rt[:, 4, :], in0=rt[:, 3, :], scalar=-1000.0,
                                                                 in1=expert_no, op0=ALU.mult, op1=ALU.add), 8)
                            chain(nc.vector.tensor_reduce(rs[:, 4, :], wide(4), AX_X, ALU.min), 9)
                            chain(nc.vector.tensor_tensor(wide(5), wide(4), over(4), ALU.is_equal), 10)
                            nc.vector.tensor_copy(onehot[:, :], rt[:, 5, :]).then_inc(s["onehot_out"], 1)
                        if t == 25:
                            dve.wait_ge(s["jobs_done"], b.at("jobs_done", idx + 2))
                            before = psM[:, 0:TT * E].rearrange("p (t e) -> p t e", e=E)
                            chain(nc.vector.tensor_tensor(wide(0), before, filled[:, None, :].to_broadcast([P, TT, E]), ALU.add), 11)
                            chain(nc.vector.tensor_tensor(filled[:, :], psM[:, TT * E:(TT + 1) * E], filled[:, :], ALU.add), 12)
                            chain(nc.vector.tensor_tensor(wide(1), wide(0), wide(5), ALU.mult), 13)
                            chain(nc.vector.tensor_reduce(rs[:, 5, :], wide(1), AX_X, ALU.add), 14)
                            chain(nc.vector.tensor_scalar(rs[:, 6, :], rs[:, 5, :], float(CAP), None, ALU.is_lt), 15)
                            chain(nc.vector.tensor_scalar(rs[:, 7, :], rs[:, 5, :], 1000.0 * CAP, None, ALU.add), 16)
                            chain(nc.vector.scalar_tensor_tensor(out=rs[:, 8, :], in0=rs[:, 4, :], scalar=float(CAP),
                                                                 in1=rs[:, 7, :], op0=ALU.mult, op1=ALU.add), 17)
                            chain(nc.vector.tensor_scalar(rs[:, 9, :], rs[:, 6, :], -float(NO_ROW), float(NO_ROW),
                                                          ALU.mult, ALU.add), 18)
                            need(dve, s["back_set"], b.at("back_set", 1))
                            nc.vector.tensor_copy(back[:, :, D + 1], token_no)
                            nc.vector.tensor_tensor(scatter_to[:, :], rs[:, 8, :], rs[:, 9, :], ALU.add
                                                    ).then_inc(s["index_out"], 1)
                            nc.vector.tensor_scalar(token_no, token_no, -float(T), None, ALU.add)

            def rows_low(e, c):
                dve.wait_ge(rows_hi, e + 1)
                nc.vector.tensor_tensor(rowsT[c][:, 1, :, :], psR[c].rearrange("p (m s) -> p m s", m=FT), rowsT[c][:, 0, :, :],
                                        ALU.subtract).then_inc(rows_lo, 1)

            def relu_low(e, c, split=False):
                for f2 in range(FF // 2):
                    if split and f2 == 1:
                        expert_lo(e + 1, 1 - c, 0)
                    dve.wait_ge(hid_hi, e * 4 + f2 + 1)
                    nc.vector.scalar_tensor_tensor(out=hT[c][:, 1, 2 * f2:2 * f2 + 2, :], in0=psH[f2].rearrange("p (f s) -> p f s", f=2),
                                                   scalar=0.0, in1=hT[c][:, 0, 2 * f2:2 * f2 + 2, :],
                                                   op0=ALU.max, op1=ALU.subtract).then_inc(hid_lo, 1)

            def result(e, c, loaded, put):
                dve.wait_ge(back_in[c], loaded)
                dve.wait_ge(y_done, e + 1)
                need(dve, put_done[c], put)
                nc.vector.tensor_scalar(put_to[:, c, :], back_sb[c][:, :, D + 1], -1.0, float(NO_ROW), ALU.mult, ALU.add)
                for st in range(2):
                    o = nc.vector.scalar_tensor_tensor(out=eo_sb[c][:, st, :], in0=psY[c][:, st * D:(st + 1) * D],
                                                       scalar=back_sb[c][:, st, D:D + 1], in1=back_sb[c][:, st, 0:D],
                                                       op0=ALU.mult, op1=ALU.add)
                o.then_inc(y_out, 1)

            def step(e, c, loaded, put):
                relu_low(e, c, split=True)
                rows_low(e + 1, 1 - c)
                result(e - 1, 1 - c, loaded, put)
                expert_lo(e + 1, 1 - c, 1)

            rows_low(0, 0)
            rows_low(1, 1)
            relu_low(0, 0)
            step(1, 1, 16, 0)
            step(2, 0, 16, 0)
            with dve.Fori(0, E // 2 - 2) as i:
                step(i * 2 + 3, 1, i * 16 + 32, i * 32 + 32)
                step(i * 2 + 4, 0, i * 16 + 32, i * 32 + 32)
            relu_low(E - 1, 1)
            for c in range(2):
                result(E - 2 + c, c, 16 * (E // 2), 16 * (E - 2))

        @block.gpsimd
        def _(pool):
            pool.wait_ge(misc_set, 2)
            pool.wait_ge(wqkv_in, 16 * 8)

            def set_stack(par, done):
                rows = stack[64:96, par, :, :].rearrange("p a n -> p (a n)").bitcast(F32)
                nc.gpsimd.memset(rows, 0.0).then_inc(done, 1)
                pool.wait_ge(done, 1)
                pair = float(np.array([MSCALE, MSCALE], np.float16).view(np.float32)[0])
                nc.gpsimd.memset(stack[96:98, par, 1, :].bitcast(F32), pair).then_inc(done, 1)
                pool.wait_ge(done, 2)

            def rstd_of(b, k):
                need(pool, s["ln_var"], b.at("ln_var", k))
                nc.gpsimd.tensor_tensor(rstd[:, :], lnt[:, 6, :], minus_half[:, :], ALU.pow).then_inc(s["ln_rstd"], 1)

            for b in stretches(pool, blocks):
                jobs = b.jobs()
                ln = int(b.nx2 in ("A", "B"))
                for t in range(SLOTS):
                    if ln and t == b.ln_slot + 1:
                        rstd_of(b, 1)
                    if ln and t == b.ln_slot + 4:
                        if b.n == -2:
                            pool.wait_ge(bias_in, 16 * 5)
                        need(pool, s["ln_out"], b.at("ln_out", 1))
                        xs = X[:, bass.ds(b.batch(2), 1), :].rearrange("p o (t d) -> p (o t) d", t=TT)
                        bo = bias_o[:, 0 if b.nx2 == "A" else 1, None, :].to_broadcast([P, TT, D])
                        nc.gpsimd.tensor_tensor(xs, xs, bo, ALU.add).then_inc(s["x_bias"], 1)
                    if b.n == -2 and t == 8:
                        pool.wait_ge(s["x_bias"], b.at("x_bias", 1))
                    if b.n == 0 and t == 0:
                        pool.wait_ge(s["lo_out"], b.at("lo_out"))
                    if (b.n, t) in ((-2, 8), (0, 0)):
                        set_stack(*((0, stack_set0) if b.n else (1, stack_set1)))
                    if t == b.norm_slot and b.prev:
                        pool.wait_ge(s["recip_in"], b.at("recip_in", 16 * FT))
                        pool.wait_ge(s["packed_0"], b.at("packed_0"))
                        pool.wait_ge(s["packed_1"], b.at("packed_1", 128))
                        nc.gpsimd.tensor_tensor(attn_b if b.prev == "B" else recipB[:, :, :], packed[:, :, :],
                                                recipB[:, :, :], ALU.mult).then_inc(s["attn_mul"], 1)
                        if b.prev == "C":
                            pool.wait_ge(s["attn_mul"], b.at("attn_mul", 1))
                            nc.gpsimd.tensor_tensor(recipB[:, :, :], attn_b, recipB[:, :, :], ALU.add
                                                    ).then_inc(s["attn_sum"], 1)
                    if b.fin and t == b.attn_slot + int(b.kind is not None):
                        pool.wait_ge(s["attn_hi"], b.at("attn_hi", 1))
                        nc.gpsimd.tensor_tensor(attn[:, 1, :, :], recipB[:, :, :], attn[:, 0, :, :], ALU.subtract
                                                ).then_inc(s["attn_out"], 1)
                    for slot, name, j in jobs:
                        if name == "proj" and b.nx2 == "A":
                            if t == slot + 1:
                                pool.wait_ge(s["rope_in"], b.at("rope_in", j + 1))
                                if j > 1 or b.n < 0:
                                    need(pool, s["rope_out"], b.at("rope_out", j - 1))
                                nc.gpsimd.tensor_tensor(rope_c[:, j % 2, :], rope_x[:, j % 2, :], rope_cs[:, 0, :], ALU.mult
                                                        ).then_inc(s["rope_cos"], 1)
                                pool.wait_ge(s["rope_cos"], b.at("rope_cos", j + 1))
                                pool.wait_ge(s[f"swap_in_{j % 2}"], b.at(f"swap_in_{j % 2}", 32 * (j // 2 + 1)))
                                nc.gpsimd.tensor_tensor(rope_s[:, j % 2, :], rope_s[:, j % 2, :], rope_cs[:, 1, :], ALU.mult
                                                        ).then_inc(s["rope_sin"], 1)
                            if t == slot + 5:
                                pool.wait_ge(s["hi_out"], b.at("hi_out", j + 1))
                                nc.gpsimd.tensor_tensor(parts[:, j % 2, j // 2, 1, :], rope_s[:, j % 2, :], parts[:, j % 2, j // 2, 0, :],
                                                        ALU.subtract).then_inc(s["lo_out"], 1)
                    if b.route and t == 13:
                        rstd_of(b, ln + 1)
                    if b.route and t == 15:
                        need(pool, s["back_scattered"], b.at("back_scattered"))
                        need(pool, s["x_out"], b.at("x_out", 2 if b.fin else 0))
                        gb = b.batch(-1) if b.kind is None else b.batch(-2)
                        nc.gpsimd.tensor_copy(back[:, :, 0:D], X[:, bass.ds(gb, 1), :].rearrange("p o (t d) -> p (o t) d", t=TT)
                                              ).then_inc(s["back_set"], 1)
                    if b.route and t == 28:
                        pool.wait_ge(s["index_out"], b.at("index_out", 1))
                        nc.gpsimd.tensor_tensor(back[:, :, D], rs[:, 3, :], gate_scale[:, :], ALU.mult).then_inc(s["gate_set"], 1)
                        pool.wait_ge(rows_zero, 16 * NG * 3)
                        pool.wait_ge(s["gate_set"], b.at("gate_set", 1))
                        for tt in range(TT):
                            nc.gpsimd.indirect_dma_start(
                                out=rows_dram[:, :], out_offset=bass.IndirectOffsetOnAxis(ap=scatter_to[:, tt:tt + 1], axis=0),
                                in_=xn[:, tt, :], in_offset=None, bounds_check=E * CAP - 1, oob_is_err=False
                            ).then_inc(s["scattered"], 16)
                        for tt in range(TT):
                            nc.gpsimd.indirect_dma_start(
                                out=back_dram[:, :], out_offset=bass.IndirectOffsetOnAxis(ap=scatter_to[:, tt:tt + 1], axis=0),
                                in_=back[:, tt, :], in_offset=None, bounds_check=E * CAP - 1, oob_is_err=False
                            ).then_inc(s["back_scattered"], 16)
            out_rows_dram = a["out"].rearrange("n t d -> (n t) d")

            def load_back(e):
                nc.gpsimd.dma_start(back_sb[e % 2], back_dram[e * CAP:(e + 1) * CAP, :].rearrange("(s p) m -> p s m", p=P)
                                    ).then_inc(back_in[e % 2], 16)

            pool.wait_ge(s["back_scattered"], total["back_scattered"])
            pool.wait_ge(s["av_out"], total["av_out"])
            for e in range(2):
                load_back(e)
            pool.wait_ge(s["x_stored"], total["x_stored"])
            for e in range(E):
                c = e % 2
                pool.wait_ge(y_out, e + 1)
                if e + 2 < E:
                    load_back(e + 2)
                for st in range(2):
                    nc.gpsimd.indirect_dma_start(
                        out=out_rows_dram, out_offset=bass.IndirectOffsetOnAxis(ap=put_to[:, c, st:st + 1], axis=0),
                        in_=eo_sb[c][:, st, :], in_offset=None, bounds_check=NB * T - 1, oob_is_err=False
                    ).then_inc(put_done[c], 16)


def _constants():
    i = np.arange(P)
    ident = np.eye(P, dtype=np.float32)
    mask_q = np.where(i[None, :] > i[:, None], np.float32(NEG), np.float32(0))
    mask_k = np.ascontiguousarray(mask_q.T)
    before = (i[:, None] < i[None, :]).astype(np.float32)
    number = np.tile(np.arange(E, dtype=np.float32), (P, TT))
    token = (NO_ROW - (i[:, None] + P * np.arange(TT)[None, :])).astype(np.float32)
    consts = np.concatenate([ident, mask_q, mask_k, before, number, token], axis=1)
    half = HD // 2
    theta = (np.float32(1.0) / np.float32(10000.0) ** (np.arange(half, dtype=np.float32) / np.float32(half)))
    freqs = np.arange(T, dtype=np.float32)[:, None] * theta[None, :].astype(np.float32)
    col = (i % HD) // 2
    rope = np.stack([np.cos(freqs)[:, col].T, np.sin(freqs)[:, col].T * np.where(i % 2, 1, -1)[:, None]]).astype(np.float32)
    return consts, np.ascontiguousarray(rope)


def kernel(**inputs):
    import numpy as _np
    import concourse.bacc as _bacc
    from concourse import mybir as _mybir
    from concourse.bass_utils import run_bass_kernel_spmd as _run

    nc = _bacc.Bacc("TRN2", target_bir_lowering=False, num_devices=1)
    consts, rope = _constants()
    arrays = {"consts": consts, "rope": rope}
    for name, v in inputs.items():
        if name == "L0_attn_W_qkv":
            arrays["W_qkv_T"] = _np.ascontiguousarray(_np.asarray(v).T)
        elif name == "L0_attn_W_out":
            arrays["W_out_T"] = _np.ascontiguousarray(_np.asarray(v).T)
        else:
            arrays["ctx" if name == "ctx_512" else name] = _np.ascontiguousarray(v)
    aps, feed = {}, {}
    for name, v in arrays.items():
        feed[f"in_{name}_dram"] = v
        aps[name] = nc.dram_tensor(f"in_{name}_dram", v.shape, _mybir.dt.from_np(v.dtype), kind="ExternalInput").ap()
    aps["out"] = nc.dram_tensor("out_0_dram", (NB, T, D), _mybir.dt.from_np(_np.dtype("float32")), kind="ExternalOutput").ap()
    build(nc, aps)
    r = _run(nc, [feed], core_ids=[0])
    return r.results[0]["out_0_dram"]
```
